# Optimizing a Trainium2 kernel written in Bass

```python
import numpy as np
import jax
import jax.numpy as jnp

def _softmax(x, axis=-1):
    return jax.nn.softmax(x, axis=axis)

def _gelu(x):
    return jax.nn.gelu(x, approximate=True)

def _silu(x):
    return jax.nn.silu(x)

def _sigmoid(x):
    return jax.nn.sigmoid(x)

def _layernorm(x, axis=-1, eps=1e-05):
    m = jnp.mean(x, axis=axis, keepdims=True)
    v = jnp.var(x, axis=axis, keepdims=True)
    return (x - m) / jnp.sqrt(v + eps)

def _scatter_add(tgt, idx, src, axis=0):
    return tgt.at[idx].add(src)

def _segment_sum(src, seg, n):
    return jax.ops.segment_sum(src, seg, n)
kernel_name = 'mk_xattn_ffn_d2_seqx_r4_0787e5'

def setup_inputs(seed: int=0):
    np.random.seed(seed)
    _w = jnp.asarray

    def _rec_inputs():
        import jax
        import jax.numpy as jnp
        _rk = jax.random.key(seed)
        x = -0.0002928 + 1 * jax.random.normal(jax.random.fold_in(_rk, 1), (2, 1024, 256), jnp.float32)
        _lenS = 1024 - jax.random.randint(jax.random.fold_in(_rk, 7), (2,), 0, max(1, 1024 // 4) + 1, jnp.int32)
        _lenS2 = 77 - jax.random.randint(jax.random.fold_in(_rk, 8), (2,), 0, max(1, 77 // 4) + 1, jnp.int32)
        _ctx_1024P = jax.random.normal(jax.random.fold_in(_rk, 11), (2, 16, 256), jnp.float32)
        _ctx_1024c = jax.random.dirichlet(jax.random.fold_in(_rk, 511), 0.3 * jnp.ones((16,), jnp.float32), (2, 77))
        _ctx_1024t = jnp.einsum('bsk,bkd->bsd', _ctx_1024c, _ctx_1024P)
        _ctx_1024t = _ctx_1024t * jax.lax.rsqrt(jnp.mean(jnp.square(_ctx_1024t)) + 1e-12) * 0.953939
        ctx_1024 = -1.39393e-06 + 0.999914 * (_ctx_1024t + 0.3 * jax.random.normal(jax.random.fold_in(_rk, 611), (2, 77, 256), jnp.float32))
        return (x, ctx_1024)
    x, ctx_1024 = _rec_inputs()

    def _L0_xattn_setup():
        import jax, jax.numpy as jnp
        import numpy as np
        EPS = 1e-06

        def rmsnorm(x, scale):
            ms = jnp.mean(jnp.square(x), axis=-1, keepdims=True)
            return x * jax.lax.rsqrt(ms + EPS) * scale
        key = jax.random.key(seed)
        ks = jax.random.split(key, 8)
        B, Q, K, D, H, DH = (2, 512, 512, 256, 16, 64)
        s = 1.0 / np.sqrt(D)
        return {'inputs_q': jax.random.normal(ks[0], (B, Q, D), jnp.float32), 'inputs_kv': jax.random.normal(ks[1], (B, K, D), jnp.float32), 'Wq': jax.random.normal(ks[2], (D, H, DH), jnp.float32) * s, 'Wk': jax.random.normal(ks[3], (D, H, DH), jnp.float32) * s, 'Wv': jax.random.normal(ks[4], (D, H, DH), jnp.float32) * s, 'scale_q': jnp.ones((DH,), jnp.float32), 'scale_k': jnp.ones((DH,), jnp.float32), 'Wo': jax.random.normal(ks[5], (H, DH, D), jnp.float32) * (1.0 / np.sqrt(H * DH)), 'bo': jnp.zeros((D,), jnp.float32)}
    _L0_xattn_all = _L0_xattn_setup()
    _L0_xattn_in = {k: v for k, v in _L0_xattn_all.items() if k in ('Wq', 'Wk', 'Wv', 'scale_q', 'scale_k', 'Wo', 'bo')}
    del _L0_xattn_all

    def _L0_ffn_setup():
        import jax, jax.numpy as jnp
        import numpy as np
        D, H, E, K = (256, 256, 8, 2)

        def _moe(x, router_w, w_in, b_in, w_out, b_out):
            B, S, Dm = x.shape
            T = B * S
            x2 = x.reshape(T, Dm)
            logits = x2 @ router_w
            probs = jax.nn.softmax(logits, axis=-1)
            top_p, top_e = jax.lax.top_k(probs, K)
            flat_e = top_e.reshape(-1)
            flat_p = top_p.reshape(-1)
            tok = jnp.repeat(jnp.arange(T), K)
            order = jnp.argsort(flat_e)
            se, sp, st = (flat_e[order], flat_p[order], tok[order])
            xd = x2[st]
            N = xd.shape[0]
            h = jnp.zeros((N, H), x.dtype)
            for e in range(E):
                m = (se == e)[:, None]
                h = h + jnp.where(m, jax.nn.gelu(xd @ w_in[e] + b_in[e]), 0.0)
            y = jnp.zeros((N, Dm), x.dtype)
            for e in range(E):
                m = (se == e)[:, None]
                y = y + jnp.where(m, h @ w_out[e] + b_out[e], 0.0)
            y = y * sp[:, None]
            out = jnp.zeros((T, Dm), x.dtype).at[st].add(y)
            return out.reshape(B, S, Dm)
        key = jax.random.key(seed)
        ks = jax.random.split(key, 5)
        s = lambda k, shape, scale: jax.random.normal(k, shape, dtype=jnp.float32) * scale
        return {'input_batch': s(ks[0], (2, 128, D), 1.0), 'router_w': s(ks[1], (D, E), D ** (-0.5)), 'w_in': s(ks[2], (E, D, H), D ** (-0.5)), 'b_in': jnp.zeros((E, H), jnp.float32), 'w_out': s(ks[3], (E, H, D), H ** (-0.5)), 'b_out': jnp.zeros((E, D), jnp.float32)}
    _L0_ffn_all = _L0_ffn_setup()
    _L0_ffn_in = {k: v for k, v in _L0_ffn_all.items() if k in ('router_w', 'w_in', 'b_in', 'w_out', 'b_out')}
    del _L0_ffn_all

    def _L1_xattn_setup():
        import jax, jax.numpy as jnp
        import numpy as np
        D1, D2, D3 = (256, 256, 256)
        key = jax.random.key(seed)
        k1, k2, kw, kb = jax.random.split(key, 4)
        x1 = jax.random.normal(k1, (8, 512, D1), dtype=jnp.float32)
        x2 = jax.random.normal(k2, (8, 512, D2), dtype=jnp.float32)
        bound = 1.0 / np.sqrt(D1 + D2)
        W = jax.random.uniform(kw, (D3, D1 + D2), minval=-bound, maxval=bound, dtype=jnp.float32)
        b = jax.random.uniform(kb, (D3,), minval=-bound, maxval=bound, dtype=jnp.float32)
        return {'x1': x1, 'x2': x2, 'W': W, 'b': b}
    _L1_xattn_all = _L1_xattn_setup()
    _L1_xattn_in = {k: v for k, v in _L1_xattn_all.items() if k in ('W', 'b')}
    del _L1_xattn_all

    def _L1_ffn_setup():
        import jax, jax.numpy as jnp
        import numpy as np
        B, S, D, H, E, K = (4, 512, 256, 1024, 8, 2)
        key = jax.random.key(seed)
        ks = jax.random.split(key, 7)
        s_d = 1.0 / np.sqrt(D)
        s_h = 1.0 / np.sqrt(H)
        return {'x': jax.random.normal(ks[0], (B, S, D), dtype=jnp.float32), 'router_w': jax.random.uniform(ks[1], (E, D), jnp.float32, -s_d, s_d), 'router_b': jax.random.uniform(ks[2], (E,), jnp.float32, -s_d, s_d), 'w1': jax.random.uniform(ks[3], (E, H, D), jnp.float32, -s_d, s_d), 'b1': jax.random.uniform(ks[4], (E, H), jnp.float32, -s_d, s_d), 'w2': jax.random.uniform(ks[5], (E, D, H), jnp.float32, -s_h, s_h), 'b2': jax.random.uniform(ks[6], (E, D), jnp.float32, -s_h, s_h)}
    _L1_ffn_all = _L1_ffn_setup()
    _L1_ffn_in = {k: v for k, v in _L1_ffn_all.items() if k in ('router_w', 'router_b', 'w1', 'b1', 'w2', 'b2')}
    del _L1_ffn_all
    return {'x': x, 'ctx_1024': ctx_1024, 'L0_xattn_Wq': _L0_xattn_in['Wq'], 'L0_xattn_Wk': _L0_xattn_in['Wk'], 'L0_xattn_Wv': _L0_xattn_in['Wv'], 'L0_xattn_scale_q': _L0_xattn_in['scale_q'], 'L0_xattn_scale_k': _L0_xattn_in['scale_k'], 'L0_xattn_Wo': _L0_xattn_in['Wo'], 'L0_xattn_bo': _L0_xattn_in['bo'], 'L0_ffn_router_w': _L0_ffn_in['router_w'], 'L0_ffn_w_in': _L0_ffn_in['w_in'], 'L0_ffn_b_in': _L0_ffn_in['b_in'], 'L0_ffn_w_out': _L0_ffn_in['w_out'], 'L0_ffn_b_out': _L0_ffn_in['b_out'], 'L1_xattn_W': _L1_xattn_in['W'], 'L1_xattn_b': _L1_xattn_in['b'], 'L1_ffn_router_w': _L1_ffn_in['router_w'], 'L1_ffn_router_b': _L1_ffn_in['router_b'], 'L1_ffn_w1': _L1_ffn_in['w1'], 'L1_ffn_b1': _L1_ffn_in['b1'], 'L1_ffn_w2': _L1_ffn_in['w2'], 'L1_ffn_b2': _L1_ffn_in['b2']}

def reference(x, ctx_1024, L0_xattn_Wq, L0_xattn_Wk, L0_xattn_Wv, L0_xattn_scale_q, L0_xattn_scale_k, L0_xattn_Wo, L0_xattn_bo, L0_ffn_router_w, L0_ffn_w_in, L0_ffn_b_in, L0_ffn_w_out, L0_ffn_b_out, L1_xattn_W, L1_xattn_b, L1_ffn_router_w, L1_ffn_router_b, L1_ffn_w1, L1_ffn_b1, L1_ffn_w2, L1_ffn_b2):
    import jax
    import jax.numpy as jnp

    def _L0_xattn_ref(inputs_q, inputs_kv, Wq, Wk, Wv, scale_q, scale_k, Wo, bo):
        import jax, jax.numpy as jnp
        import numpy as np
        EPS = 1e-06

        def rmsnorm(x, scale):
            ms = jnp.mean(jnp.square(x), axis=-1, keepdims=True)
            return x * jax.lax.rsqrt(ms + EPS) * scale
        softmax_axis = -1
        q = jnp.einsum('bqd,dhe->bqhe', inputs_q, Wq)
        k = jnp.einsum('bkd,dhe->bkhe', inputs_kv, Wk)
        v = jnp.einsum('bkd,dhe->bkhe', inputs_kv, Wv)
        q = rmsnorm(q, scale_q)
        k = rmsnorm(k, scale_k)
        q = q / jnp.sqrt(jnp.asarray(q.shape[-1], q.dtype))
        attn = jnp.einsum('bqhe,bkhe->bhqk', q, k)
        attn = jax.nn.softmax(attn, axis=softmax_axis)
        x = jnp.einsum('bhqk,bkhe->bqhe', attn, v)
        out = jnp.einsum('bqhe,hed->bqd', x, Wo) + bo
        return out

    def _L0_ffn_ref(input_batch, router_w, w_in, b_in, w_out, b_out):
        import jax, jax.numpy as jnp
        import numpy as np
        D, H, E, K = (256, 256, 8, 2)

        def _moe(x, router_w, w_in, b_in, w_out, b_out):
            B, S, Dm = x.shape
            T = B * S
            x2 = x.reshape(T, Dm)
            logits = x2 @ router_w
            probs = jax.nn.softmax(logits, axis=-1)
            top_p, top_e = jax.lax.top_k(probs, K)
            flat_e = top_e.reshape(-1)
            flat_p = top_p.reshape(-1)
            tok = jnp.repeat(jnp.arange(T), K)
            order = jnp.argsort(flat_e)
            se, sp, st = (flat_e[order], flat_p[order], tok[order])
            xd = x2[st]
            N = xd.shape[0]
            h = jnp.zeros((N, H), x.dtype)
            for e in range(E):
                m = (se == e)[:, None]
                h = h + jnp.where(m, jax.nn.gelu(xd @ w_in[e] + b_in[e]), 0.0)
            y = jnp.zeros((N, Dm), x.dtype)
            for e in range(E):
                m = (se == e)[:, None]
                y = y + jnp.where(m, h @ w_out[e] + b_out[e], 0.0)
            y = y * sp[:, None]
            out = jnp.zeros((T, Dm), x.dtype).at[st].add(y)
            return out.reshape(B, S, Dm)
        return _moe(input_batch, router_w, w_in, b_in, w_out, b_out)

    def _L1_xattn_ref(x1, x2, W, b):
        import jax, jax.numpy as jnp
        import numpy as np
        D1, D2, D3 = (256, 256, 256)
        d1 = x1.shape[-1]
        W1 = W[:, :d1]
        W2 = W[:, d1:]
        part1 = jnp.einsum('bld,ed->ble', x1, W1)
        part2 = jnp.einsum('bld,ed->be', x2, W2) / x2.shape[1]
        return part1 + part2[:, None, :] + b

    def _L1_ffn_ref(x, router_w, router_b, w1, b1, w2, b2):
        import jax, jax.numpy as jnp
        import numpy as np
        B, S, D, H, E, K = (4, 512, 256, 1024, 8, 2)
        Bx, Sx, Dx = x.shape
        x_flat = x.reshape(-1, Dx)
        logits = x_flat @ router_w.T + router_b
        probs = jax.nn.softmax(logits, axis=-1)
        topk_prob, topk_idx = jax.lax.top_k(probs, K)
        y = jnp.zeros_like(x_flat)
        for e in range(E):
            gate = jnp.sum(jnp.where(topk_idx == e, topk_prob, 0.0), axis=-1)
            h = jax.nn.gelu(x_flat @ w1[e].T + b1[e])
            out = h @ w2[e].T + b2[e]
            y = y + gate[:, None] * out
        return y.reshape(Bx, Sx, Dx)
    x = x + _L0_xattn_ref(_layernorm(x, axis=-1), ctx_1024, L0_xattn_Wq, L0_xattn_Wk, L0_xattn_Wv, L0_xattn_scale_q, L0_xattn_scale_k, L0_xattn_Wo, L0_xattn_bo)
    x = x + _L0_ffn_ref(_layernorm(x, axis=-1), L0_ffn_router_w, L0_ffn_w_in, L0_ffn_b_in, L0_ffn_w_out, L0_ffn_b_out)
    x = x + _L1_xattn_ref(_layernorm(x, axis=-1), ctx_1024, L1_xattn_W, L1_xattn_b)
    x = x + _L1_ffn_ref(_layernorm(x, axis=-1), L1_ffn_router_w, L1_ffn_router_b, L1_ffn_w1, L1_ffn_b1, L1_ffn_w2, L1_ffn_b2)
    return x

_drawn_inputs = setup_inputs


def setup_inputs(seed=0):
    import zlib

    import numpy as np

    out = dict(_drawn_inputs(seed))
    spreads = {'L0_xattn_scale_q': (1.0, 0.2),
     'L0_xattn_scale_k': (1.0, 0.2),
     'L0_xattn_bo': (0.0, 0.1),
     'L0_ffn_b_in': (0.0, 0.304),
     'L0_ffn_b_out': (0.0, 0.1)}
    factors = {'L1_xattn_b': 2.947, 'L1_ffn_router_b': 6.667, 'L1_ffn_b1': 8.0, 'L1_ffn_b2': 8.0}
    for name, (base, spread) in spreads.items():
        noise = np.random.default_rng([zlib.crc32(name.encode()), seed]).standard_normal(out[name].shape)
        drawn = base * np.exp(spread * noise) if base else spread * noise
        out[name] = jnp.asarray(drawn.astype(out[name].dtype))
    for name, factor in factors.items():
        out[name] = (out[name] * factor).astype(out[name].dtype)
    return out
```

```python
import math
from contextlib import ExitStack

import concourse.bass as bass
from concourse import mybir

F32, F16, I32, U32 = mybir.dt.float32, mybir.dt.float16, mybir.dt.int32, mybir.dt.uint32
ALU = mybir.AluOpType
ACT = mybir.ActivationFunctionType
AX = mybir.AxisListType

P = 128
RSQRT_SEED = 0x5F3759DF


def product(shape):
    r = 1
    for n in shape:
        r *= n
    return r


def carve(region, at, shape, dt):
    size = 2 if dt == F16 else 4
    end = at + product(shape) * size
    v = region[:, at // 4:(end + 3) // 4]
    if dt != F32:
        v = v.bitcast(dt)
    if len(shape) > 1:
        names = [f"d{n}" for n in range(len(shape))]
        v = v.rearrange(f"p ({' '.join(names)}) -> p {' '.join(names)}", **dict(zip(names[1:], shape[1:])))
    return v, end


class LayerNorm:

    def __init__(self, n, sem, region, at, ps, D):
        self.n, self.ps = n, ps
        self.full32, at = carve(region, at, [2, D], F32)
        self.rows, at = carve(region, at, [2, 2 * D], F16)
        self.xT, at = carve(region, at, [2, 2 * D // P, P], F16)
        self.end = at
        self.var = sem(f"ln{n}_variance")
        self.full = sem(f"ln{n}_normed")
        self.hi = sem(f"ln{n}_hi")
        self.lo = sem(f"ln{n}_lo")
        self.tr = sem(f"ln{n}_transposed")
        self.cols = sem(f"ln{n}_columns")


class Moe:
    pass


def build(nc, x, ctx_t, wq, wk, wv, scale_q, scale_k, wo, bo, rw0, w_in0, b_in0, w_out0, b_out0,
          cw1_t, cw2_t, cb, rw1_t, rb1, w1_t, b1, w2_t, b2, out):
    T, D = x.shape
    DC = D // P
    NT = T // P
    NB = 2
    L = ctx_t.shape[1] // NB
    DH = scale_q.shape[0]
    HE = wq.shape[1]
    NH = HE // DH
    NP = NH // 2
    PW = 2 * L
    NS = NH * L
    KC = math.ceil(NS / P)
    E = rw0.shape[1]
    H0, H1 = w_in0.shape[2], w1_t.shape[2]
    SW = 2 * P
    NSLOT = (2 * T + E * (SW - 1)) // SW
    NQ = 2 * NSLOT
    WS = 64.0
    PS = 1024.0
    LN_EPS, RMS_EPS = 1e-5, 1e-6
    CH = 1024
    NEG = -3.0e38
    RING = 4

    with ExitStack() as ctx:
        def sb(name, shape, dt):
            return ctx.enter_context(nc.sbuf_tensor(name, shape, dt))

        sems = {}

        def sem(name):
            if name not in sems:
                sems[name] = ctx.enter_context(nc.semaphore(name))
            return sems[name]

        W1R = sb("w1_region", [P, 16384], F32)
        W2R = sb("w2_region", [P, 16384], F32)
        WBR = sb("wb_region", [P, 8192], F32)
        X = sb("x_res", [P, NT, D], F32)
        SLR = sb("slot_region", [P, 4096], F32)
        STG = sb("staging", [P, 2, CH], F32)

        w1s, _ = carve(W1R, 0, [E * 2 * DC * H1], F16)
        w2s, _ = carve(W2R, 0, [E * 2 * (H1 // P) * D], F16)
        wb_in, at = carve(WBR, 0, [E * 2 * DC * H0], F16)
        wb_out, at = carve(WBR, at, [E * 2 * (H0 // P) * D], F16)

        PSUM = ctx.enter_context(nc.psum_tensor("banks", [P, 8, 512], F32))
        bank = [PSUM[:, i, :] for i in range(8)]

        def half(k, n):
            return bank[k][:, 256 * n:256 * n + 256].bitcast(F16).rearrange("p (a b) -> p a b", b=P)

        zt, at = carve(W1R, 0, [NP, NB, 2 * P + PW], F32)
        pb2, at = carve(W1R, at, [KC * P], F32)
        vwf, at = carve(W1R, at, [2, D], F32)
        onehot0, _ = carve(W1R, 32768, [2 * NT, P], F16)
        ln0 = LayerNorm(0, sem, W1R, at, half(0, 0), D)
        ln1 = LayerNorm(1, sem, W1R, ln0.end, half(0, 1), D)
        ctx_s, at = carve(W1R, ln1.end, [DC, NB * L], F32)
        cw2, at = carve(W1R, at, [DC, D], F32)
        cmb, at = carve(W1R, at, [DC, NB, P], F32)
        cmean, at = carve(W1R, at, [DC, NB], F32)
        route0, _ = carve(W1R, ln1.end, [1600], F32)
        assert at <= 65536
        wk_s, at = carve(WBR, 0, [DC, HE], F32)
        wv_s, at = carve(WBR, at, [DC, HE], F32)
        wo_s, at = carve(WBR, at, [NP, D], F32)
        assert at <= 32768
        wq_h, at = carve(W2R, 0, [DC, HE], F16)
        wq_l, at = carve(W2R, at, [DC, HE], F16)
        kbh, at = carve(W2R, at, [NP, NB, 2, L], F16)
        kbl, at = carve(W2R, at, [NP, NB, 2, L], F16)
        vw, at = carve(W2R, at, [NB, KC, 2, D], F16)
        qsq, at = carve(W2R, at, [NP, P], F32)
        pb01, at = carve(W2R, at, [2, KC * P], F32)
        qh, at = carve(W2R, at, [NP, P], F16)
        ql, at = carve(W2R, at, [NP, P], F16)
        pth_at = at
        pth, at = carve(W2R, at, [KC, P], F16)
        ptl, at = carve(W2R, at, [KC, P], F16)
        bo_row, at = carve(W2R, at, [D], F32)
        ident_f, at = carve(W2R, at, [P], F32)
        heads2, at = carve(W2R, at, [P], F32)
        assert at <= 65536
        pb = [pb01[:, 0, :], pb01[:, 1, :], pb2]
        kf = pb[0][:, 0:NP * NB * L].rearrange("p (j c) -> p j c", j=NP)
        k_tmp, _ = carve(W2R, pth_at, [2, NP * NB * L // 2], F32)
        ksq = pb[1][:, 0:NP * NB * L].rearrange("p (j c) -> p j c", j=NP)

        ident_h = sb("ident_h", [P, P], F16)
        before = sb("before", [P, P], F32)
        ones = sb("ones", [P, P], F32)
        first8 = sb("first8", [P, E], F32)
        iota_r = sb("iota_r", [P, P], F16)
        iota_t = sb("iota_t", [P, NT], F32)
        ctx_bias = sb("ctx_bias", [P, NB, D], F32)
        wc = sb("wc", [P, 2, DC, D], F16)
        rws = sb("rws", [P, 2, 2, DC, E], F16)
        rbb = sb("rbb", [P, E], F32)
        b_in0_s = sb("b_in0_s", [P, E * (H0 // P)], F32)
        b1_s = sb("b1_s", [P, E * (H1 // P)], F32)
        sks = sb("sks", [P, 4], F32)
        neghalf = sb("neghalf", [P, 1], F32)
        st6 = sb("st6", [P, 4, 6], F32)
        mv = sb("mv", [P, 4, 2, 2], F32)
        rv = sb("rv", [P, 4, 2, 2], F32)
        mxs = sb("mxs", [P, NH], F32)
        rq = sb("rq", [P, 2, NH], F32)
        rs = sb("rs", [P, NH], F32)
        lg = sb("lg", [P, NT, E], F32)
        gates = sb("gates", [P, 2, NT], F32)
        slots = sb("slots", [P, NT, 2], U32)
        index = sb("index", [P, NQ], U32)
        expert = sb("expert", [P, 2, NSLOT], I32)

        rows_dram = nc.dram_tensor("normed_rows", [T, 2 * D], F16).ap()
        y_dram = nc.dram_tensor("sorted_y", [NQ * P, D], F32).ap()

        chunks = []
        for dc in range(DC):
            chunks.append((wq[dc * P:(dc + 1) * P, :], wq_h[:, dc, :], wq_l[:, dc, :]))
        chunks.append((cw1_t.rearrange("(c p) n -> p c n", p=P), wc[:, 0, :, :], wc[:, 1, :, :]))
        chunks.append((None, rws[:, 0, :, :, :].rearrange("p a b c -> p (a b c)"),
                       rws[:, 1, :, :, :].rearrange("p a b c -> p (a b c)")))
        PRE = len(chunks)
        per = DC * H0
        for store, src in ((wb_in, w_in0), (wb_out, w_out0)):
            v = store.rearrange("p (e s n) -> p e s n", s=2, n=per)
            g = CH // per
            for e in range(0, E, g):
                chunks.append((src[e:e + g].rearrange("e (c p) n -> p e c n", p=P), v[:, e:e + g, 0, :], v[:, e:e + g, 1, :]))
        B_CH = len(chunks)
        per = DC * H1
        big = []
        for store, src in ((w1s, w1_t), (w2s, w2_t)):
            v = store.rearrange("p (e s n) -> p e s n", s=2, n=per)
            w = src.rearrange("e (c p) n -> p e c n", p=P)
            cs = w.shape[2] * CH // per
            for e in range(E):
                for part in range(per // CH):
                    c = slice(part * CH, (part + 1) * CH)
                    big.append((e, (w[:, e, part * cs:(part + 1) * cs, :], v[:, e, 0, c], v[:, e, 1, c])))
        chunks += [c for e, c in big if e < E - 1] + [c for e, c in big if e == E - 1]
        NCH = len(chunks)
        A_CH = 16
        LATE = 2 * (per // CH)

        def staged(k):
            hi = chunks[k][1]
            v = STG[:, k % 2, 0:product(hi.shape[1:])]
            if len(hi.shape) == 3:
                v = v.rearrange("p (a b) -> p a b", a=hi.shape[1])
            return v

        moes = []
        for layer, (H, wa, wb, b_s) in enumerate(((H0, wb_in, wb_out, b_in0_s), (H1, w1s, w2s, b1_s))):
            m = Moe()
            m.H, m.HC, m.wa, m.wb, m.b = H, H // P, wa, wb, b_s
            m.HH = m.HC // 2
            m.rows, at = carve(SLR, 0, [RING, 2, 2 * D], F16)
            m.xT, at = carve(SLR, at, [2, 2 * DC, SW], F16)
            m.y, at = carve(SLR, at, [2, 2, D], F32)
            if layer == 0:
                m.g, at = carve(W1R, 65536 - 8192, [2, m.HH, SW], F32)
                m.hh, at = carve(W1R, at, [2, m.HC, SW], F16)
                m.hl, at = carve(W1R, at, [2, m.HC, SW], F16)
                m.b2, _ = carve(W2R, 65536 - 8192, [E * D], F32)
            else:
                m.hh, at = carve(WBR, 0, [2, m.HC, SW], F16)
                m.hl, at = carve(WBR, at, [2, m.HC, SW], F16)
                m.g, at = carve(WBR, at, [2, m.HH, SW], F32)
                m.b2, at = carve(WBR, at, [E * D], F32)
                assert at <= 32768
            moes.append(m)
        NG_BUF = 3
        yg, at = carve(WBR, 0, [NG_BUF, 2, D], F32)
        ln2 = LayerNorm(2, sem, WBR, at, half(0, 0), D)
        ln3 = LayerNorm(3, sem, WBR, ln2.end, half(1, 0), D)
        route1, at = carve(SLR, 0, [1600], F32)
        onehot1, at = carve(SLR, at, [2 * NT, P], F16)
        assert ln3.end <= 24576 and at <= 16384
        yg1, _ = carve(WBR, 0, [8, 2, D], F32)
        routes = [route0, route1]
        onehots = [onehot0, onehot1]

        GP = 4
        groups = [(a, min(a + GP, KC)) for a in range(0, KC, GP)]
        NG = len(groups)
        score_banks = PSUM[:, 3:6, 0:6 * L].rearrange("p b (h k) -> p b h k", k=L)
        SSQ = bank[5][:, 320:320 + NH]
        LOG = bank[5][:, 400:400 + E]
        q_ps = PSUM[:, 1:3, :].rearrange("p b (j t) -> p (b j) t", t=P)
        o_ps = bank[0][:, 0:D]
        c_ps = bank[6][:, 0:D]
        FULL = NP // 3
        LAST = slice(FULL * 6, NH)


        def hidden(m, a):
            return PSUM[:, 1 + 2 * a:3 + 2 * a, :].rearrange("p b (c t) -> p (b c) t", t=SW)[:, 0:m.HH, :]

        block = ctx.enter_context(nc.Block())

        @block.sync
        def _(sp):
            def load(dst, src, name):
                sp.dma_start(dst, src).then_inc(sem(name), 16)

            def stage(k):
                if k >= 2:
                    sp.wait_ge(sem(f"chunk_lo{k % 2}"), k // 2)
                loaded = sem(f"chunk_loaded{k % 2}")
                src = chunks[k][0]
                if src is None:
                    n = DC * E
                    for layer, w in enumerate((rw0, rw1_t)):
                        sp.dma_start(STG[:, k % 2, layer * n:(layer + 1) * n].rearrange("p (c e) -> p c e", c=DC),
                                     w.rearrange("(c p) e -> p c e", p=P)).then_inc(
                            loaded if layer else sem("router_loaded"), 16)
                    return
                dst = STG[:, k % 2, 0:product(src.shape[1:])]
                if len(src.shape) == 3:
                    dst = dst.rearrange("p (a b) -> p a b", a=src.shape[1])
                if len(src.shape) == 4:
                    dst = dst.rearrange("p (e a b) -> p e a b", e=src.shape[1], a=src.shape[2])
                    sp.dma_start(dst[:, 0], src[:, 0]).then_inc(sem(f"chunk_part{k % 2}"), 16)
                    sp.dma_start(dst[:, 1], src[:, 1]).then_inc(loaded, 16)
                    return
                sp.dma_start(dst, src).then_inc(loaded, 16)

            load(ctx_s, ctx_t.rearrange("(c p) n -> p c n", p=P), "ctx_loaded")
            load(wk_s, wk.rearrange("(c p) n -> p c n", p=P), "wk_loaded")
            for h in range(2):
                load(sks[h * DH:(h + 1) * DH, 0:1], scale_q.rearrange("(e o) -> e o", o=1), "scales_loaded")
                load(sks[h * DH:(h + 1) * DH, 1:2], scale_k.rearrange("(e o) -> e o", o=1), "scales_loaded")
            load(wv_s, wv.rearrange("(c p) n -> p c n", p=P), "wv_loaded")
            load(cw2, cw2_t.rearrange("(c p) n -> p c n", p=P), "cw2_loaded")
            q4 = NT // 4
            xv = x.rearrange("(t p) d -> p t d", p=P)
            load(X[:, 0:q4, :], xv[:, 0:q4, :], "x_loaded0")
            stage(0)
            stage(1)
            load(wo_s, wo.rearrange("(j p) n -> p j n", p=P), "wo_loaded")
            for b in range(NB):
                load(ctx_bias[:, b, :], cb.partition_broadcast(P), "cb_loaded")
            sp.wait_ge(sem("bo_zeroed"), 1)
            load(bo_row[NS % P:NS % P + 1, :], bo.rearrange("(o n) -> o n", o=1), "bo_loaded")
            for g in range(1, 4):
                load(X[:, g * q4:(g + 1) * q4, :], xv[:, g * q4:(g + 1) * q4, :], f"x_loaded{g}")
            for k in range(2, PRE):
                stage(k)
            load(b_in0_s[:, :], b_in0, "b_in0_loaded")
            load(b1_s[:, :], b1, "b1_loaded")
            load(rbb[:, :], rb1.partition_broadcast(P), "rb_loaded")
            sp.wait_ge(sem("vw_done"), NB * KC)

            rows_v = rows_dram.rearrange("(t p) d -> t p d", p=P)

            def keep_rows(o, i):
                sp.wait_ge(o.lo, i + 1)
                sp.dma_start(rows_v[i], o.rows[:, i % 2, :]).then_inc(sem(f"rows_kept{o.n}_{i % 2}"), 16)

            stage(PRE)
            stage(PRE + 1)
            for i in range(NT):
                keep_rows(ln1, i)
                stage(PRE + 2 + i)

            yv = y_dram.rearrange("(j a p) d -> j p a d", a=2, p=P)

            def keep_y(layer, j):
                sp.wait_ge(sem(f"y_ready{layer}"), j + 1)
                sp.dma_start(yv[j], moes[layer].y[:, j % 2]).then_inc(sem(f"y_kept{layer}_{j % 2}"), 16)

            sp.wait_ge(sem("routed"), 1)
            load(moes[0].b2, b_out0.partition_broadcast(P), "b2_loaded0")
            for j in range(NSLOT + 3):
                if PRE + A_CH + 2 + j < NCH - LATE:
                    stage(PRE + A_CH + 2 + j)
                if j >= 3:
                    keep_y(0, j - 3)
            load(moes[1].b2, b2.partition_broadcast(P), "b2_loaded1")
            for k in range(NCH - LATE, NCH):
                stage(k)
            for i in range(NT):
                keep_rows(ln3, i)
            for j in range(NSLOT):
                keep_y(1, j)
            ov = out.rearrange("(t p) d -> p t d", p=P)
            for i in range(NT):
                sp.wait_ge(sem("y_used1"), 2 * (i + 1))
                sp.dma_start(ov[:, i, :], X[:, i, :]).then_inc(sem("out_stored"), 16)
            sp.wait_ge(sem("out_stored"), 16 * NT)

        @block.gpsimd
        def _(pool):
            g = nc.gpsimd
            chain = [0]

            def link(ins):
                chain[0] += 1
                ins.then_inc(sem("pool_chain"), 1)
                pool.wait_ge(sem("pool_chain"), chain[0])

            link(g.memset(neghalf[:, :], -0.5))
            link(g.memset(heads2, 0.0))
            link(g.memset(heads2[0:DH, 0:DH], 1.0))
            g.memset(heads2[DH:P, DH:P], 1.0).then_inc(sem("heads_ready"), 1)
            pool.wait_ge(sem("heads_ready"), 1)
            g.memset(zt, 0.0).then_inc(sem("zt_zeroed"), 1)
            g.memset(kbh, 0.0)
            g.memset(kbl, 0.0)
            g.memset(bo_row, 0.0).then_inc(sem("bo_zeroed"), 1)
            link(g.memset(pb01[:, :, NS:KC * P], 0.0))
            link(g.memset(pb2[:, NS:KC * P], 0.0))
            g.memset(pb2[:, NS:NS + 1], PS)
            g.memset(pb01[:, :, NS:NS + 1], PS).then_inc(sem("kb_zeroed"), 1)
            for t in (ident_h[:, :], ident_f):
                link(g.memset(t, 0.0))
                link(g.affine_select(out=t, in_=t, compare_op=ALU.not_equal, fill=1.0, base=0,
                                     pattern=[[-1, P]], channel_multiplier=1))
            link(g.memset(ones[:, :], 1.0))
            link(g.affine_select(out=before[:, :], in_=ones[:, :], compare_op=ALU.is_gt, fill=0.0, base=0,
                                 pattern=[[1, P]], channel_multiplier=-1))
            link(g.iota(first8[:, :], pattern=[[-1, E]], base=E, channel_multiplier=0,
                        allow_small_or_imprecise_dtypes=True))
            link(g.iota(iota_t[:, :], pattern=[[P, NT]], base=0, channel_multiplier=1,
                        allow_small_or_imprecise_dtypes=True))
            g.iota(iota_r[:, :], pattern=[[1, P]], base=0, channel_multiplier=0,
                   allow_small_or_imprecise_dtypes=True).then_inc(sem("consts_ready"), 1)

            def split_lo(k):
                pool.wait_ge(sem("chunk_scaled"), k // 2 + 1)
                g.tensor_tensor(chunks[k][2], staged(k), chunks[k][1], ALU.subtract).then_inc(sem("chunk_lo0"), 1)

            def vw_lo(n):
                pool.wait_ge(sem("vw_hi"), n + 1)
                g.tensor_tensor(vw[:, n // KC, n % KC, 1, :], vwf[:, n % 2, :], vw[:, n // KC, n % KC, 0, :],
                                ALU.subtract).then_inc(sem("vw_ready"), 1)

            def norm(o, i):
                pool.wait_ge(o.var, i + 1)
                r = rv[:, o.n, i % 2, :]
                link(g.tensor_tensor(r[:, 0:1], mv[:, o.n, i % 2, 1:2], neghalf[:, :], ALU.pow))
                link(g.tensor_scalar(r[:, 1:2], mv[:, o.n, i % 2, 0:1], -1.0, 1.0, ALU.mult, ALU.mult))
                if i >= 2:
                    pool.wait_ge(o.lo, i - 1)
                g.tensor_scalar(o.full32[:, i % 2, :], X[:, i, :], r[:, 1:2], r[:, 0:1], ALU.add, ALU.mult).then_inc(
                    o.full, 1)

            def q_rms(i):
                pool.wait_ge(sem("q_ms"), i + 1)
                v = rq[:, i % 2, :]
                link(g.tensor_tensor(v, v, neghalf[:, 0:1].to_broadcast([P, NH]), ALU.pow))

            def p_rows(i):
                return pb[i % 3][:, 0:NS].rearrange("p (h k) -> p h k", k=L)

            def scale_scores(i):
                pool.wait_ge(sem("scores_shifted"), i + 1)
                g.tensor_tensor(p_rows(i), p_rows(i), rq[:, i % 2, :, None].to_broadcast([P, NH, L]),
                                ALU.mult).then_inc(sem("scores_scaled"), 1)

            def norm_weights(i):
                pool.wait_ge(sem("row_sums"), i + 1)
                g.tensor_tensor(p_rows(i), p_rows(i), rs[:, :, None].to_broadcast([P, NH, L]),
                                ALU.mult).then_inc(sem("weights_ready"), 1)

            for s in range(NT + 9):
                if 0 <= s - 3 < NT:
                    q_rms(s - 3)
                    scale_scores(s - 3)
                if s < NT:
                    norm(ln0, s)
                if 0 <= s - 6 < NT:
                    norm(ln1, s - 6)
                if s < 4:
                    for n in range(5 * s, 5 * s + 5):
                        vw_lo(n)
                if s < PRE and s % 2 == 0:
                    split_lo(s)
                if 0 <= s - 4 < NT:
                    norm_weights(s - 4)
                if 0 <= s - 6 < NT and (PRE + s - 6) % 2 == 0:
                    split_lo(PRE + s - 6)

            def gather_rows(layer, j):
                m = moes[layer]
                for a in range(2):
                    if j >= RING:
                        pool.wait_ge(sem(f"slot_tr{layer}"), j - RING + 1)
                    q = 2 * j + a
                    g.indirect_dma_start(
                        out=m.rows[:, j % RING, a, :], out_offset=None, in_=rows_dram,
                        in_offset=bass.IndirectOffsetOnAxis(ap=index[:, q:q + 1], axis=0)).then_inc(
                        sem(f"rows_gathered{layer}_{j % RING}"), 16)

            def slot_rows(layer):
                pool.wait_ge(sem("routed"), layer + 1)
                for b in range(2):
                    pool.wait_ge(sem(f"rows_kept{1 + 2 * layer}_{b}"), 16 * (NT // 2))
                for j in range(NSLOT):
                    gather_rows(layer, j)
                    if layer == 0:
                        k = PRE + A_CH + j
                        if k < NCH - LATE and k % 2 == 0:
                            split_lo(k)
                for b in range(2):
                    pool.wait_ge(sem(f"y_kept{layer}_{b}"), 16 * ((NSLOT + 1 - b) // 2))

            def gather_y(layer, i, ring):
                n = ring.shape[1]
                for c in range(2):
                    if i >= n:
                        pool.wait_ge(sem(f"y_used{layer}"), 2 * (i - n) + c + 1)
                    g.indirect_dma_start(
                        out=ring[:, i % n, c, :], out_offset=None, in_=y_dram,
                        in_offset=bass.IndirectOffsetOnAxis(ap=slots[:, i, c:c + 1], axis=0)).then_inc(
                        sem(f"y_gathered{layer}_{i % n}"), 16)

            slot_rows(0)
            late = list(range(NCH - LATE, NCH))
            for s in range(NT + 5):
                if s < NT:
                    gather_y(0, s, yg)
                if 0 <= s - 2 < NT:
                    norm(ln2, s - 2)
                if 0 <= s - 5 < NT:
                    norm(ln3, s - 5)
                if s < len(late) and late[s] % 2 == 0:
                    split_lo(late[s])
            slot_rows(1)
            for i in range(NT):
                gather_y(1, i, yg1)

        @block.scalar
        def _(act):
            s_ = nc.scalar

            def split_hi(k):
                act.wait_ge(sem(f"chunk_loaded{k % 2}"), 16 * (k // 2 + 1))
                if chunks[k][0] is None:
                    act.wait_ge(sem("router_loaded"), 16)
                elif len(chunks[k][0].shape) == 4:
                    n = sum(1 for c in range(k % 2, k + 1, 2) if chunks[c][0] is not None and len(chunks[c][0].shape) == 4)
                    act.wait_ge(sem(f"chunk_part{k % 2}"), 16 * n)
                s_.activation(chunks[k][1], staged(k), ACT.Copy, scale=WS).then_inc(sem(f"chunk_hi{k % 2}"), 1)
                if k % 2 == 0:
                    act.wait_ge(sem("chunk_hi0"), k // 2 + 1)
                    s_.activation(staged(k), staged(k), ACT.Copy, scale=WS).then_inc(sem("chunk_scaled"), 1)

            for j in range(NP):
                act.wait_ge(sem("k_done"), j + 1)
                s_.activation(ksq[:, j, :], bank[3 + j % 2][:, 0:NB * L], ACT.Square).then_inc(sem("k_sq"), 1)
            for k in range(2):
                split_hi(k)
            act.wait_ge(sem("zt_zeroed"), 1)
            for j in range(NP):
                act.wait_ge(sem("vt_done"), j + 1)
                for h in range(2):
                    rows = slice(h * DH, (h + 1) * DH)
                    s_.activation(zt[rows, j, :, P + h * L:P + (h + 1) * L], bank[1 + j % 2][rows, 0:NB * L].rearrange(
                        "p (b k) -> p b k", b=NB), ACT.Copy).then_inc(sem("vt_copied"), 1)

            def k_hi():
                act.wait_ge(sem("k_normed"), 1)
                act.wait_ge(sem("kb_zeroed"), 1)
                for h in range(2):
                    rows = slice(h * DH, (h + 1) * DH)
                    s_.activation(kbh[rows, :, :, h, :], kf[rows].rearrange("p j (b k) -> p j b k", b=NB),
                                  ACT.Copy).then_inc(sem("kb_hi"), 1)

            def vw_hi(n):
                act.wait_ge(sem("vw_done"), n + 1)
                if n >= 2:
                    act.wait_ge(sem("vw_ready"), n - 1)
                s_.activation(vwf[:, n % 2, :], bank[6 + n % 2][:, 0:D], ACT.Copy, scale=WS)
                s_.activation(vw[:, n // KC, n % KC, 0, :], bank[6 + n % 2][:, 0:D], ACT.Copy, scale=WS).then_inc(
                    sem("vw_hi"), 1)

            def norm_hi(o, i):
                act.wait_ge(o.full, i + 1)
                if i >= 2:
                    act.wait_ge(o.tr, i - 1)
                    if o.n in (1, 3):
                        act.wait_ge(sem(f"rows_kept{o.n}_{i % 2}"), 16 * (i // 2))
                s_.activation(o.rows[:, i % 2, 0:D], o.full32[:, i % 2, :], ACT.Copy).then_inc(o.hi, 1)

            def columns(o, i, user):
                act.wait_ge(o.tr, i + 1)
                if i >= 2:
                    act.wait_ge(sem(user), i - 1)
                s_.activation(o.xT[:, i % 2], o.ps, ACT.Copy).then_inc(o.cols, 1)

            def q_hi(i):
                act.wait_ge(sem("q_done"), i + 1)
                if i >= 1:
                    act.wait_ge(sem("scores_done"), i)
                s_.activation(qh, q_ps, ACT.Copy).then_inc(sem("q_hi"), 1)
                if i >= 1:
                    act.wait_ge(sem("ssq_done"), i)
                s_.activation(qsq, q_ps, ACT.Square, scale=1.0 / WS).then_inc(sem("q_sq"), 1)

            def exp(i):
                act.wait_ge(sem("scores_scaled"), i + 1)
                v = pb[i % 3][:, 0:NS]
                s_.activation(v, v, ACT.Exp, scale=1.0 / (WS * WS)).then_inc(sem("exp_done"), 1)

            def pt_hi(i, n):
                a, b = groups[n]
                act.wait_ge(sem("weights_tr"), NG * i + n + 1)
                if i >= 1:
                    act.wait_ge(sem("attn_done"), i)
                s_.activation(pth[:, a:b, :], bank[6 + (NG * i + n) % 2][:, 0:(b - a) * P].rearrange(
                    "p (c t) -> p c t", t=P), ACT.Copy).then_inc(sem("pt_hi"), 1)

            for s in range(NT + 9):
                if 0 <= s - 2 < NT:
                    q_hi(s - 2)
                if 0 <= s - 5 < NT:
                    pt_hi(s - 5, 0)
                    pt_hi(s - 5, 1)
                if 0 <= s - 1 < NT:
                    if s - 1 >= 6:
                        act.wait_ge(ln1.tr, s - 6)
                    columns(ln0, s - 1, "q_done")
                if 0 <= s - 7 < NT:
                    columns(ln1, s - 7, "logits_done0")
                if 0 <= s - 5 < NT:
                    pt_hi(s - 5, 2)
                if s < NT:
                    norm_hi(ln0, s)
                if 0 <= s - 6 < NT:
                    norm_hi(ln1, s - 6)
                if s < 4:
                    for n in range(5 * s, 5 * s + 5):
                        vw_hi(n)
                if s == 1:
                    k_hi()
                if 0 <= s - 3 < NT:
                    exp(s - 3)
                if 2 <= s < PRE:
                    split_hi(s)
                if 0 <= s - 6 < NT:
                    split_hi(PRE + s - 6)

            def route(layer):
                act.wait_ge(sem("route_shift"), layer + 1)
                r = routes[layer]
                s_.activation(r[:, 0:NT * E], r[:, 0:NT * E], ACT.Exp).then_inc(sem("route_exp"), 1)
                s_.activation(r[:, 1152:1152 + NT], r[:, 1152:1152 + NT], ACT.Exp).then_inc(sem("route_exp"), 1)

            def gelu(layer, j, a):
                m = moes[layer]
                v = m.g[:, a]
                act.wait_ge(sem(f"h_biased{layer}"), 2 * j + a + 1)
                s_.activation(v, v, ACT.Gelu_apprx_tanh).then_inc(sem(f"gelu{layer}"), 1)
                act.wait_ge(sem(f"gelu{layer}"), 2 * j + a + 1)
                if j >= 2:
                    act.wait_ge(sem(f"slot_y{layer}"), j - 1)
                s_.activation(m.hh[:, j % 2, a * m.HH:(a + 1) * m.HH, :], v, ACT.Copy).then_inc(sem(f"h_hi{layer}"), 1)

            route(0)
            act.wait_ge(sem("routed"), 1)
            for s in range(NSLOT + 1):
                if s < NSLOT and PRE + A_CH + s < NCH - LATE:
                    split_hi(PRE + A_CH + s)
                if s >= 1:
                    gelu(0, s - 1, 0)
                    gelu(0, s - 1, 1)
            late = list(range(NCH - LATE, NCH))
            act.wait_ge(sem("y_ready0"), NSLOT)
            for s in range(NT + 7):
                if 0 <= s - 3 < NT:
                    columns(ln2, s - 3, "linear_done")
                if 0 <= s - 6 < NT:
                    columns(ln3, s - 6, "logits_done1")
                if 0 <= s - 2 < NT:
                    norm_hi(ln2, s - 2)
                if 0 <= s - 5 < NT:
                    norm_hi(ln3, s - 5)
                if s < len(late):
                    split_hi(late[s])
            route(1)
            for j in range(NSLOT):
                gelu(1, j, 0)
                gelu(1, j, 1)

        @block.vector
        def _(dve):
            v = nc.vector
            chain = [0]

            def link(ins):
                chain[0] += 1
                ins.then_inc(sem("dve_chain"), 1)
                dve.wait_ge(sem("dve_chain"), chain[0])

            dve.wait_ge(sem("scales_loaded"), 4 * 16)
            link(v.tensor_tensor(sks[:, 2:3], sks[:, 0:1], sks[:, 1:2], ALU.mult))
            link(v.tensor_scalar(sks[:, 3:4], sks[:, 2:3], WS / math.sqrt(DH), None, ALU.mult))
            dve.wait_ge(sem("ctx_loaded"), 16)
            link(v.tensor_reduce(cmean, ctx_s.rearrange("p c (b k) -> p c b k", b=NB), axis=AX.X, op=ALU.add))
            v.tensor_scalar(cmb, cmean[:, :, :, None].to_broadcast([P, DC, NB, P]), 1.0 / L, None,
                            ALU.mult).then_inc(sem("mean_ready"), 1)
            for j in range(NP):
                dve.wait_ge(sem("k_sq"), j + 1)
                v.tensor_copy(kf[:, j, :], bank[3 + j % 2][:, 0:NB * L]).then_inc(sem("k_copied"), 1)
                dve.wait_ge(sem("k_ssq"), j + 1)
                v.tensor_scalar(ksq[:, j, :], bank[5][:, 0:NB * L], 1.0 / DH, RMS_EPS, ALU.mult, ALU.add).then_inc(
                    sem("k_ms"), 1)
            kv = pb[1][:, 0:NP * NB * L]
            half_n = NP * NB * L // 2
            y, t = k_tmp[:, 0, :], k_tmp[:, 1, :]
            dve.wait_ge(sem("k_ms"), NP)
            for part in range(2):
                kp = kv[:, part * half_n:(part + 1) * half_n]
                link(v.tensor_scalar(y.bitcast(I32), kp.bitcast(I32), -0.5, float(RSQRT_SEED), ALU.mult, ALU.add))
                for n in range(3):
                    link(v.tensor_tensor(t, y, y, ALU.mult))
                    link(v.scalar_tensor_tensor(out=t, in0=t, scalar=-0.5, in1=kp, op0=ALU.mult, op1=ALU.mult))
                    link(v.scalar_tensor_tensor(out=y if n < 2 else kp, in0=t, scalar=1.5, in1=y, op0=ALU.add,
                                                op1=ALU.mult))
            v.scalar_tensor_tensor(out=pb[0][:, 0:NS], in0=pb[0][:, 0:NS], scalar=sks[:, 3:4], in1=kv,
                                   op0=ALU.mult, op1=ALU.mult).then_inc(sem("k_normed"), 1)
            for b in range(NB):
                dve.wait_ge(sem("mean_done"), b + 1)
                dve.wait_ge(sem("cb_loaded"), 32)
                v.tensor_tensor(ctx_bias[:, b, :], bank[3 + b][:, 0:D], ctx_bias[:, b, :], ALU.add).then_inc(
                    sem("ctx_bias_ready"), 1)

            def k_lo():
                for h in range(2):
                    dve.wait_ge(sem("kb_hi"), h + 1)
                    rows = slice(h * DH, (h + 1) * DH)
                    v.tensor_tensor(kbl[rows, :, :, h, :], kf[rows].rearrange("p j (b k) -> p j b k", b=NB),
                                    kbh[rows, :, :, h, :], ALU.subtract).then_inc(sem("kb_ready"), 1)

            def split_lo(k):
                dve.wait_ge(sem("chunk_hi1"), k // 2 + 1)
                v.scalar_tensor_tensor(out=chunks[k][2], in0=staged(k), scalar=WS, in1=chunks[k][1],
                                       op0=ALU.mult, op1=ALU.subtract).then_inc(sem("chunk_lo1"), 1)

            def stats(o, i):
                link(v.bn_stats(st6[:, o.n, :], X[:, i, :]))
                if i >= 2:
                    dve.wait_ge(o.full, i - 1)
                link(v.bn_aggr(mv[:, o.n, i % 2, :], st6[:, o.n, :]))
                v.tensor_scalar_add(mv[:, o.n, i % 2, 1:2], mv[:, o.n, i % 2, 1:2], LN_EPS).then_inc(o.var, 1)

            def norm_lo(o, i):
                dve.wait_ge(o.hi, i + 1)
                r = o.rows[:, i % 2, :]
                v.tensor_tensor(r[:, D:2 * D], o.full32[:, i % 2, :], r[:, 0:D], ALU.subtract).then_inc(o.lo, 1)

            def q_ms(i):
                dve.wait_ge(sem("ssq_done"), i + 1)
                if i >= 6:
                    dve.wait_ge(sem("logits_done0"), i - 5)
                if i >= 2:
                    dve.wait_ge(sem("scores_scaled"), i - 1)
                v.tensor_scalar(rq[:, i % 2, :], SSQ, 1.0 / DH, RMS_EPS, ALU.mult, ALU.add).then_inc(sem("q_ms"), 1)

            def shift(i):
                dve.wait_ge(sem("scores_done"), i + 1)
                full = score_banks[:, 0:FULL, :, :]
                last = score_banks[:, FULL, 0:NH - FULL * 6, :]
                v.tensor_reduce(mxs[:, 0:FULL * 6].rearrange("p (b h) -> p b h", b=FULL), full, axis=AX.X, op=ALU.max)
                link(v.tensor_reduce(mxs[:, LAST], last, axis=AX.X, op=ALU.max))
                if i == 0:
                    dve.wait_ge(sem("kb_ready"), 2)
                if i >= 3:
                    dve.wait_ge(sem("weights_tr"), NG * (i - 2))
                row = pb[i % 3][:, 0:NS].rearrange("p (h k) -> p h k", k=L)
                v.tensor_tensor(row[:, 0:FULL * 6, :].rearrange("p (b h) k -> p b h k", b=FULL), full,
                                mxs[:, 0:FULL * 6].rearrange("p (b h) -> p b h", b=FULL)[:, :, :, None].to_broadcast(
                                    [P, FULL, 6, L]), ALU.subtract)
                v.tensor_tensor(row[:, LAST, :], last, mxs[:, LAST][:, :, None].to_broadcast([P, NH - FULL * 6, L]),
                                ALU.subtract).then_inc(sem("scores_shifted"), 1)

            def sums(i):
                dve.wait_ge(sem("exp_done"), i + 1)
                if i >= 1:
                    dve.wait_ge(sem("weights_ready"), i)
                link(v.tensor_reduce(rs[:, :], pb[i % 3][:, 0:NS].rearrange("p (h k) -> p h k", k=L), axis=AX.X,
                                     op=ALU.add))
                link(v.reciprocal(rs[:, :], rs[:, :]))
                v.tensor_scalar(rs[:, :], rs[:, :], PS, None, ALU.mult).then_inc(sem("row_sums"), 1)

            def pt_lo(i, n):
                a, b = groups[n]
                dve.wait_ge(sem("pt_hi"), NG * i + n + 1)
                v.tensor_tensor(ptl[:, a:b, :], bank[6 + (NG * i + n) % 2][:, 0:(b - a) * P].rearrange(
                    "p (c t) -> p c t", t=P), pth[:, a:b, :], ALU.subtract).then_inc(sem("pt_lo"), 1)

            def q_lo(i):
                dve.wait_ge(sem("q_sq"), i + 1)
                v.tensor_tensor(ql, q_ps, qh, ALU.subtract).then_inc(sem("q_lo"), 1)

            def add_attn(i):
                dve.wait_ge(sem("attn_done"), i + 1)
                dve.wait_ge(ln0.full, i + 1)
                v.scalar_tensor_tensor(out=X[:, i, :], in0=o_ps, scalar=1.0 / (WS * PS), in1=X[:, i, :],
                                       op0=ALU.mult, op1=ALU.add).then_inc(sem("attn_added"), 1)
                dve.wait_ge(sem("attn_added"), i + 1)

            def logits(layer, i):
                dve.wait_ge(sem(f"logits_done{layer}"), i + 1)
                if layer == 0:
                    v.tensor_scalar(lg[:, i, :], LOG, 1.0 / WS, None, ALU.mult).then_inc(sem("logits_read0"), 1)
                else:
                    if i == 0:
                        dve.wait_ge(sem("rb_loaded"), 16)
                    v.scalar_tensor_tensor(out=lg[:, i, :], in0=LOG, scalar=1.0 / WS, in1=rbb[:, :],
                                           op0=ALU.mult, op1=ALU.add).then_inc(sem("logits_read1"), 1)

            for s in range(NT + 9):
                if 0 <= s - 6 < NT:
                    add_attn(s - 6)
                if 0 <= s - 2 < NT:
                    q_lo(s - 2)
                if s < NT:
                    if s % (NT // 4) == 0:
                        dve.wait_ge(sem(f"x_loaded{s // (NT // 4)}"), 16)
                    stats(ln0, s)
                if 0 <= s - 6 < NT:
                    stats(ln1, s - 6)
                if 0 <= s - 5 < NT:
                    pt_lo(s - 5, 0)
                    pt_lo(s - 5, 1)
                if 0 <= s - 4 < NT:
                    sums(s - 4)
                if 0 <= s - 5 < NT:
                    pt_lo(s - 5, 2)
                if 0 <= s - 2 < NT:
                    q_ms(s - 2)
                if 0 <= s - 8 < NT:
                    logits(0, s - 8)
                if 0 <= s - 2 < NT:
                    shift(s - 2)
                if s == 0:
                    split_lo(1)
                if s < NT:
                    norm_lo(ln0, s)
                if 0 <= s - 6 < NT:
                    norm_lo(ln1, s - 6)
                if s == 1:
                    k_lo()
                if s == 3:
                    split_lo(3)
                if 0 <= s - 6 < NT and (PRE + s - 6) % 2:
                    split_lo(PRE + s - 6)

            def route(layer):
                r = routes[layer]

                def cut(n):
                    return r[:, n * P:n * P + NT * E]

                def te(a):
                    return a.rearrange("p (t e) -> p t e", e=E)

                def et(a):
                    return a.rearrange("p (e t) -> p e t", e=E)

                ex, m1, m2, best = cut(0), r[:, 1024:1024 + NT], r[:, 1152:1152 + NT], r[:, 1088:1088 + NT]
                oh = [cut(1), cut(2)]
                cand, masked, hot, tot = cut(3), cut(4), cut(5), cut(6)
                counts = r[:, 1216:1216 + 64]
                dve.wait_ge(sem(f"logits_read{layer}"), NT)
                if layer == 0:
                    dve.wait_ge(sem("consts_ready"), 1)
                cur = lg[:, :, :]
                f8 = first8[:, None, :].to_broadcast([P, NT, E])
                for c, m in enumerate((m1, m2)):
                    link(v.tensor_reduce(m, cur, axis=AX.X, op=ALU.max))
                    link(v.tensor_tensor(te(cand), cur, m[:, :, None].to_broadcast([P, NT, E]), ALU.is_equal))
                    link(v.tensor_tensor(te(cand), te(cand), f8, ALU.mult))
                    link(v.tensor_reduce(best, te(cand), axis=AX.X, op=ALU.max))
                    link(v.tensor_tensor(te(oh[c]), f8, best[:, :, None].to_broadcast([P, NT, E]), ALU.is_equal))
                    if c == 0:
                        link(v.scalar_tensor_tensor(out=te(masked), in0=te(oh[0]), scalar=NEG, in1=cur,
                                                    op0=ALU.mult, op1=ALU.add))
                        cur = te(masked)
                v.tensor_tensor(hot, oh[0], oh[1], ALU.add).then_inc(sem("hot"), 1)
                link(v.tensor_tensor(te(ex), lg[:, :, :], m1[:, :, None].to_broadcast([P, NT, E]), ALU.subtract))
                v.tensor_tensor(m2, m2, m1, ALU.subtract).then_inc(sem("route_shift"), 1)
                dve.wait_ge(sem("counts_done"), layer + 1)
                link(v.tensor_copy(et(tot), bank[7][:, 128:128 + NT * E].rearrange("p (t e) -> p e t", e=E)))
                incl = cand
                link(v.tensor_tensor_scan(incl, ones[:, 0:NT * E], tot, 0.0, ALU.mult, ALU.add))
                ends = et(incl)[:, :, NT - 1]
                start, cnt, tiles, tend, base = (counts[:, 8 * k:8 * k + 8] for k in range(5))
                link(v.memset(start[:, 0:1], 0.0))
                link(v.tensor_copy(start[:, 1:E], ends[:, 0:E - 1]))
                link(v.tensor_tensor(cnt, ends, start, ALU.subtract))
                ci = counts[:, 40:48].bitcast(I32)
                link(v.tensor_scalar(ci, cnt, float(SW - 1), None, ALU.add))
                link(v.tensor_scalar(ci, ci, SW.bit_length() - 1, None, ALU.logical_shift_right))
                link(v.tensor_copy(tiles, ci))
                link(v.tensor_tensor_scan(tend, ones[:, 0:E], tiles, 0.0, ALU.mult, ALU.add))
                link(v.tensor_tensor(base, tend, tiles, ALU.subtract))
                link(v.scalar_tensor_tensor(out=base, in0=base, scalar=float(SW), in1=start, op0=ALU.mult,
                                            op1=ALU.subtract))
                link(v.tensor_tensor(masked, incl, tot, ALU.subtract))
                link(v.tensor_tensor(et(masked), et(masked), base[:, :, None].to_broadcast([P, E, NT]), ALU.add))
                pos = cand
                link(v.tensor_tensor(te(pos), bank[7][:, 256:256 + NT * E].rearrange("p (t e) -> p t e", e=E),
                                     masked.rearrange("p (e t) -> p t e", e=E), ALU.add))
                for c in range(2):
                    link(v.tensor_tensor(hot, oh[c], pos, ALU.mult))
                    link(v.tensor_reduce(best, te(hot), axis=AX.X, op=ALU.add))
                    link(v.tensor_copy(slots[:, :, c], best))
                rr, qq, num = (r[:, k:k + 2 * NT] for k in (1280, 1312, 1344))
                sv = slots[:, :, :].rearrange("p t c -> p (t c)")
                link(v.tensor_scalar(hot[:, 0:2 * NT].bitcast(U32), sv, P - 1, None, ALU.bitwise_and))
                link(v.tensor_scalar(tot[:, 0:2 * NT].bitcast(U32), sv, P.bit_length() - 1, None, ALU.logical_shift_right))
                link(v.tensor_copy(rr, hot[:, 0:2 * NT].bitcast(U32)))
                link(v.tensor_copy(qq, tot[:, 0:2 * NT].bitcast(U32)))
                v.tensor_tensor(onehots[layer], iota_r[:, None, :].to_broadcast([P, 2 * NT, P]),
                                rr[:, :, None].to_broadcast([P, 2 * NT, P]), ALU.is_equal)
                at_q = r[:, 128:128 + NT * NQ].bitcast(F16).rearrange("p (n q) -> p n q", q=NQ)
                link(v.tensor_tensor(at_q, iota_r[:, None, 0:NQ].to_broadcast([P, 2 * NT, NQ]),
                                     qq[:, :, None].to_broadcast([P, 2 * NT, NQ]), ALU.is_equal))
                link(v.tensor_copy(num.rearrange("p (t c) -> p t c", c=2), iota_t[:, :, None].to_broadcast([P, NT, 2])))
                v.tensor_tensor(at_q, at_q, num[:, :, None].to_broadcast([P, 2 * NT, NQ]), ALU.mult).then_inc(
                    sem("places"), 1)
                ge_e = r[:, 1376:1376 + NSLOT * (E - 1)].rearrange("p (s e) -> p s e", e=E - 1)
                link(v.tensor_tensor(ge_e, iota_r[:, 0:NSLOT, None].to_broadcast([P, NSLOT, E - 1]),
                                     tend[:, None, 0:E - 1].to_broadcast([P, NSLOT, E - 1]), ALU.is_ge))
                es = r[:, 1540:1540 + NSLOT]
                link(v.tensor_reduce(es, ge_e, axis=AX.X, op=ALU.add))
                link(v.tensor_copy(expert[:, 0, :], es))
                link(v.tensor_scalar(expert[:, 1, :], es, float(2 * DC * moes[layer].H), None, ALU.mult))
                dve.wait_ge(sem("route_exp"), 2 * layer + 2)
                link(v.tensor_reduce(best, te(ex), axis=AX.X, op=ALU.add))
                link(v.reciprocal(gates[:, 0, :], best))
                link(v.tensor_tensor(gates[:, 1, :], gates[:, 0, :], m2, ALU.mult))
                dve.wait_ge(sem("tokens_done"), layer + 1)
                v.tensor_copy(index[:, :], bank[6][:, 0:NQ]).then_inc(sem("routed"), 1)

            def slot_cols(layer, j):
                m = moes[layer]
                dve.wait_ge(sem(f"slot_tr{layer}"), j + 1)
                if j >= 2:
                    dve.wait_ge(sem(f"slot_h{layer}"), 2 * (j - 1))
                v.tensor_copy(m.xT[:, j % 2], bank[7 * (j % 2)].bitcast(F16).rearrange("p (c t) -> p c t", t=SW)).then_inc(
                    sem(f"slot_cols{layer}"), 1)

            def slot_bias(layer, j, a):
                m = moes[layer]
                if a == 0:
                    expert_of[j] = dve.value_load(expert[0:1, 0, j:j + 1], min_val=0, max_val=E - 1)
                dve.wait_ge(sem(f"slot_h{layer}"), 2 * j + a + 1)
                if j >= 1:
                    dve.wait_ge(sem(f"h_lo{layer}"), 2 * j + a - 1)
                bias = m.b[:, bass.ds(expert_of[j] * m.HC + a * m.HH, m.HH)]
                v.scalar_tensor_tensor(out=m.g[:, a], in0=hidden(m, a), scalar=1.0 / WS,
                                       in1=bias[:, :, None].to_broadcast([P, m.HH, SW]),
                                       op0=ALU.mult, op1=ALU.add).then_inc(sem(f"h_biased{layer}"), 1)

            def slot_lo(layer, j, a):
                m = moes[layer]
                dve.wait_ge(sem(f"h_hi{layer}"), 2 * j + a + 1)
                c = slice(a * m.HH, (a + 1) * m.HH)
                v.tensor_tensor(m.hl[:, j % 2, c, :], m.g[:, a], m.hh[:, j % 2, c, :], ALU.subtract).then_inc(
                    sem(f"h_lo{layer}"), 1)

            def slot_out(layer, j):
                m = moes[layer]
                dve.wait_ge(sem(f"slot_y{layer}"), j + 1)
                if j >= 2:
                    dve.wait_ge(sem(f"y_kept{layer}_{j % 2}"), 16 * (j // 2))
                b2 = m.b2[:, bass.ds(expert_of[j] * D, D)]
                v.scalar_tensor_tensor(out=m.y[:, j % 2], in0=PSUM[:, 5:7, 0:D], scalar=1.0 / WS,
                                       in1=b2[:, None, :].to_broadcast([P, 2, D]),
                                       op0=ALU.mult, op1=ALU.add).then_inc(sem(f"y_ready{layer}"), 1)

            expert_of = {}

            def slots_of(layer):
                dve.wait_ge(sem("b_in0_loaded" if layer == 0 else "b1_loaded"), 16)
                dve.wait_ge(sem(f"b2_loaded{layer}"), 16)
                for s in range(NSLOT + 3):
                    if 0 <= s - 3 < NSLOT:
                        slot_out(layer, s - 3)
                    if s < NSLOT:
                        slot_cols(layer, s)
                    if 0 <= s - 1 < NSLOT:
                        slot_bias(layer, s - 1, 0)
                        slot_bias(layer, s - 1, 1)
                        slot_lo(layer, s - 1, 0)
                        slot_lo(layer, s - 1, 1)
                    if layer == 0 and s < NSLOT:
                        k = PRE + A_CH + s
                        if k < NCH - LATE and k % 2:
                            split_lo(k)

            def combine(layer, i, ring):
                n = ring.shape[1]
                dve.wait_ge(sem(f"y_gathered{layer}_{i % n}"), 32 * (i // n + 1))
                for c in range(2):
                    if c:
                        dve.wait_ge(sem(f"y_used{layer}"), 2 * i + 1)
                    v.scalar_tensor_tensor(out=X[:, i, :], in0=ring[:, i % n, c, :], scalar=gates[:, c, i:i + 1],
                                           in1=X[:, i, :], op0=ALU.mult, op1=ALU.add).then_inc(sem(f"y_used{layer}"), 1)
                dve.wait_ge(sem(f"y_used{layer}"), 2 * i + 2)

            def add_linear(i):
                dve.wait_ge(ln2.full, i + 1)
                link(v.tensor_tensor(X[:, i, :], X[:, i, :], ctx_bias[:, i // (NT // NB), :], ALU.add))
                dve.wait_ge(sem("linear_done"), i + 1)
                v.scalar_tensor_tensor(out=X[:, i, :], in0=c_ps, scalar=1.0 / WS, in1=X[:, i, :],
                                       op0=ALU.mult, op1=ALU.add).then_inc(sem("linear_added"), 1)
                dve.wait_ge(sem("linear_added"), i + 1)

            route(0)
            slots_of(0)
            late = list(range(NCH - LATE, NCH))
            for s in range(NT + 8):
                if 0 <= s - 2 < NT:
                    combine(0, s - 2, yg)
                    stats(ln2, s - 2)
                if 0 <= s - 4 < NT:
                    add_linear(s - 4)
                if 0 <= s - 5 < NT:
                    stats(ln3, s - 5)
                if 0 <= s - 7 < NT:
                    logits(1, s - 7)
                if 0 <= s - 2 < NT:
                    norm_lo(ln2, s - 2)
                if 0 <= s - 5 < NT:
                    norm_lo(ln3, s - 5)
                if s < len(late) and late[s] % 2:
                    split_lo(late[s])
            route(1)
            slots_of(1)
            for i in range(NT):
                combine(1, i, yg1)

        @block.tensor
        def _(pe):
            t = nc.tensor

            def mm(o, a, b, start, stop):
                return t.matmul(o, a, b, start=start, stop=stop)

            def three(o, ah, al, bh, bl, first, last):
                mm(o, ah, bh, first, False)
                mm(o, ah, bl, False, False)
                return mm(o, al, bh, False, last)

            pe.wait_ge(sem("ctx_loaded"), 16)
            pe.wait_ge(sem("wk_loaded"), 16)
            pe.wait_ge(sem("heads_ready"), 1)
            for s in range(NP + 1):
                if s < NP:
                    if s >= 2:
                        pe.wait_ge(sem("k_copied"), s - 1)
                    for dc in range(DC):
                        last = mm(bank[3 + s % 2][:, 0:NB * L], wk_s[:, dc, s * P:(s + 1) * P], ctx_s[:, dc, :],
                                  dc == 0, dc == DC - 1)
                    last.then_inc(sem("k_done"), 1)
                if s >= 1:
                    pe.wait_ge(sem("k_sq"), s)
                    if s >= 2:
                        pe.wait_ge(sem("k_ms"), s - 1)
                    mm(bank[5][:, 0:NB * L], heads2, ksq[:, s - 1, :], True, True).then_inc(sem("k_ssq"), 1)
            pe.wait_ge(sem("wv_loaded"), 16)
            for j in range(NP):
                if j >= 2:
                    pe.wait_ge(sem("vt_copied"), 2 * (j - 1))
                for dc in range(DC):
                    last = mm(bank[1 + j % 2][:, 0:NB * L], wv_s[:, dc, j * P:(j + 1) * P], ctx_s[:, dc, :],
                              dc == 0, dc == DC - 1)
                last.then_inc(sem("vt_done"), 1)
            pe.wait_ge(sem("mean_ready"), 1)
            pe.wait_ge(sem("cw2_loaded"), 16)
            pe.wait_ge(sem("k_copied"), NP)
            for b in range(NB):
                for dc in range(DC):
                    last = mm(bank[3 + b][:, 0:D], cmb[:, dc, b, :], cw2[:, dc, :], dc == 0, dc == DC - 1)
                last.then_inc(sem("mean_done"), 1)
            pe.wait_ge(sem("wo_loaded"), 16)
            pe.wait_ge(sem("vt_copied"), NH)
            pe.wait_ge(sem("consts_ready"), 1)

            def v_wo(n):
                b, c = divmod(n, KC)
                if n >= 2:
                    pe.wait_ge(sem("vw_ready"), n - 1)
                js = [j for j in range(NP) if -P < P * c - PW * j < PW]
                for j in js:
                    o = P + P * c - PW * j
                    last = mm(bank[6 + n % 2][:, 0:D], zt[:, j, b, o:o + P], wo_s[:, j, :],
                              j == js[0], j == js[-1] and c < KC - 1)
                if c == KC - 1:
                    pe.wait_ge(sem("bo_loaded"), 16)
                    last = mm(bank[6 + n % 2][:, 0:D], ident_f, bo_row, False, True)
                last.then_inc(sem("vw_done"), 1)

            def transposed(o, i):
                pe.wait_ge(o.lo, i + 1)
                if i >= 1:
                    pe.wait_ge(o.cols, i)
                for c in range(2 * DC):
                    last = t.transpose(o.ps[:, c, :], o.rows[:, i % 2, c * P:(c + 1) * P], ident_h[:, :])
                last.then_inc(o.tr, 1)

            def q_proj(i):
                pe.wait_ge(ln0.cols, i + 1)
                if i == 0:
                    pe.wait_ge(sem("chunk_lo0"), 1)
                    pe.wait_ge(sem("chunk_lo1"), 1)
                if i >= 1:
                    pe.wait_ge(sem("q_lo"), i)
                xT = ln0.xT[:, i % 2]
                for j in range(NP):
                    w = slice(j * P, (j + 1) * P)
                    for dc in range(DC):
                        last = three(q_ps[:, j, :], wq_h[:, dc, w], wq_l[:, dc, w], xT[:, dc, :], xT[:, DC + dc, :],
                                     dc == 0, dc == DC - 1)
                last.then_inc(sem("q_done"), 1)

            def scores(i):
                pe.wait_ge(sem("q_lo"), i + 1)
                if i == 0:
                    pe.wait_ge(sem("kb_ready"), 2)
                    pe.wait_ge(sem("ctx_bias_ready"), NB)
                if i >= 1:
                    pe.wait_ge(sem("scores_shifted"), i)
                if i >= 7:
                    pe.wait_ge(sem("logits_read0"), i - 6)
                b = i // (NT // NB)
                for j in range(NP):
                    kh = kbh[:, j, b].rearrange("p a k -> p (a k)")
                    kl = kbl[:, j, b].rearrange("p a k -> p (a k)")
                    last = three(bank[3 + j // 3][:, PW * (j % 3):PW * (j % 3 + 1)], qh[:, j, :], ql[:, j, :], kh, kl,
                                 True, True)
                last.then_inc(sem("scores_done"), 1)

            def q_squares(i):
                pe.wait_ge(sem("q_sq"), i + 1)
                for j in range(NP):
                    last = mm(SSQ[:, 2 * j:2 * j + 2], qsq[:, j, :], heads2[:, 0:DH + 1:DH], True, True)
                last.then_inc(sem("ssq_done"), 1)

            def weights_t(i, n):
                if n == 0:
                    pe.wait_ge(sem("weights_ready"), i + 1)
                if i == 0 and n == 0:
                    pe.wait_ge(sem("vw_ready"), NB * KC)
                if NG * i + n >= 2:
                    pe.wait_ge(sem("pt_lo"), NG * i + n - 1)
                a, b = groups[n]
                for c in range(a, b):
                    last = t.transpose(bank[6 + (NG * i + n) % 2][:, (c - a) * P:(c - a + 1) * P],
                                       pb[i % 3][:, c * P:(c + 1) * P], ident_f)
                last.then_inc(sem("weights_tr"), 1)

            def attn(i):
                pe.wait_ge(sem("pt_lo"), NG * (i + 1))
                pe.wait_ge(ln0.cols, min(NT, i + 5))
                if i >= 2:
                    pe.wait_ge(ln1.cols, i - 1)
                if i >= 1:
                    pe.wait_ge(sem("attn_added"), i)
                b = i // (NT // NB)
                for c in range(KC):
                    last = three(o_ps, pth[:, c, :], ptl[:, c, :], vw[:, b, c, 0, :], vw[:, b, c, 1, :],
                                 c == 0, c == KC - 1)
                last.then_inc(sem("attn_done"), 1)

            def logits(layer, o, i):
                pe.wait_ge(o.cols, i + 1)
                if i == 0:
                    pe.wait_ge(sem("chunk_lo0"), PRE // 2)
                    pe.wait_ge(sem("chunk_lo1"), PRE // 2)
                if i >= 1:
                    pe.wait_ge(sem(f"logits_read{layer}"), i)
                if layer == 0:
                    pe.wait_ge(sem("scores_shifted"), min(NT, i + 6))
                for dc in range(DC):
                    last = three(LOG, o.xT[:, i % 2, dc, :], o.xT[:, i % 2, DC + dc, :], rws[:, 0, layer, dc, :],
                                 rws[:, 1, layer, dc, :], dc == 0, dc == DC - 1)
                last.then_inc(sem(f"logits_done{layer}"), 1)

            for s in range(NT + 9):
                if 0 <= s - 5 < NT:
                    weights_t(s - 5, 0)
                    weights_t(s - 5, 1)
                if 0 <= s - 1 < NT:
                    if s - 1 >= 5:
                        pe.wait_ge(sem("attn_added"), s - 5)
                    if s - 1 >= 7:
                        pe.wait_ge(ln1.cols, s - 7)
                    transposed(ln0, s - 1)
                if 0 <= s - 7 < NT:
                    pe.wait_ge(sem("attn_added"), min(NT, s - 5))
                    if s - 1 >= NT:
                        pe.wait_ge(ln0.cols, NT)
                    transposed(ln1, s - 7)
                if 0 <= s - 2 < NT:
                    scores(s - 2)
                if 0 <= s - 5 < NT:
                    weights_t(s - 5, 2)
                if 0 <= s - 2 < NT:
                    q_squares(s - 2)
                if 0 <= s - 8 < NT:
                    logits(0, ln1, s - 8)
                if s < 4:
                    for n in range(5 * s, 5 * s + 5):
                        v_wo(n)
                if 0 <= s - 1 < NT:
                    q_proj(s - 1)
                if 0 <= s - 5 < NT:
                    attn(s - 5)

            def route(layer):
                r = routes[layer]
                hot = r[:, 5 * P:5 * P + NT * E]
                pe.wait_ge(sem("hot"), layer + 1)
                if layer == 0:
                    pe.wait_ge(sem("pt_lo"), NG * NT)
                mm(bank[7][:, 128:128 + NT * E], ones[:, :], hot, True, True)
                mm(bank[7][:, 256:256 + NT * E], before[:, :], hot, True, True).then_inc(sem("counts_done"), 1)
                pe.wait_ge(sem("places"), layer + 1)
                at_q = r[:, 128:128 + NT * NQ].bitcast(F16).rearrange("p (n q) -> p n q", q=NQ)
                for n in range(2 * NT):
                    last = mm(bank[6][:, 0:NQ], onehots[layer][:, n, :], at_q[:, n, :], n == 0, n == 2 * NT - 1)
                last.then_inc(sem("tokens_done"), 1)

            weights_at = {}

            def slot_tr(layer, j):
                m = moes[layer]
                pe.wait_ge(sem(f"rows_gathered{layer}_{j % RING}"), 32 * (j // RING + 1))
                if j >= 2:
                    pe.wait_ge(sem(f"slot_cols{layer}"), j - 1)
                cols = bank[7 * (j % 2)].bitcast(F16).rearrange("p (c t) -> p c t", t=SW)
                for a in range(2):
                    for c in range(2 * DC):
                        last = t.transpose(cols[:, c, a * P:(a + 1) * P], m.rows[:, j % RING, a, c * P:(c + 1) * P],
                                           ident_h[:, :])
                last.then_inc(sem(f"slot_tr{layer}"), 1)

            def slot_up(layer, j):
                m = moes[layer]
                per = DC * m.H
                e = weights_at[j]
                pe.wait_ge(sem(f"slot_cols{layer}"), j + 1)
                xT = m.xT[:, j % 2]
                for a in range(2):
                    if j >= 1:
                        pe.wait_ge(sem(f"h_biased{layer}"), 2 * j + a - 1)
                    ps = hidden(m, a)
                    for hc in range(m.HH):
                        for dc in range(DC):
                            o = dc * m.H + (a * m.HH + hc) * P
                            last = three(ps[:, hc, :], m.wa[:, bass.ds(e + o, P)], m.wa[:, bass.ds(e + (per + o), P)],
                                         xT[:, dc, :], xT[:, DC + dc, :], dc == 0, dc == DC - 1)
                    last.then_inc(sem(f"slot_h{layer}"), 1)

            def slot_down(layer, j):
                m = moes[layer]
                per = DC * m.H
                e = weights_at[j]
                pe.wait_ge(sem(f"h_lo{layer}"), 2 * (j + 1))
                if j >= 1:
                    pe.wait_ge(sem(f"y_ready{layer}"), j)
                for hc in range(m.HC):
                    wh = m.wb[:, bass.ds(e + hc * D, D)]
                    wl = m.wb[:, bass.ds(e + (per + hc * D), D)]
                    for a in range(2):
                        c = slice(a * P, (a + 1) * P)
                        last = three(bank[5 + a][:, 0:D], m.hh[:, j % 2, hc, c], m.hl[:, j % 2, hc, c], wh, wl,
                                     hc == 0, hc == m.HC - 1)
                last.then_inc(sem(f"slot_y{layer}"), 1)

            def slots_of(layer):
                m = moes[layer]
                pe.wait_ge(sem("routed"), layer + 1)
                n = B_CH if layer == 0 else NCH
                pe.wait_ge(sem("chunk_lo0"), n // 2)
                pe.wait_ge(sem("chunk_lo1"), n // 2)
                for s in range(NSLOT + 2):
                    if s < NSLOT:
                        weights_at[s] = pe.value_load(expert[0:1, 1, s:s + 1], min_val=0, max_val=(E - 1) * 2 * DC * m.H)
                        slot_tr(layer, s)
                    if 0 <= s - 1 < NSLOT:
                        slot_up(layer, s - 1)
                    if 0 <= s - 2 < NSLOT:
                        slot_down(layer, s - 2)

            def linear(i):
                pe.wait_ge(ln2.cols, i + 1)
                if i >= 1:
                    pe.wait_ge(sem("linear_added"), i)
                xT = ln2.xT[:, i % 2]
                for dc in range(DC):
                    last = three(c_ps, xT[:, dc, :], xT[:, DC + dc, :], wc[:, 0, dc, :], wc[:, 1, dc, :],
                                 dc == 0, dc == DC - 1)
                last.then_inc(sem("linear_done"), 1)

            route(0)
            slots_of(0)
            for s in range(NT + 8):
                if 0 <= s - 3 < NT:
                    transposed(ln2, s - 3)
                if 0 <= s - 6 < NT:
                    transposed(ln3, s - 6)
                if 0 <= s - 7 < NT:
                    logits(1, ln3, s - 7)
                if 0 <= s - 3 < NT:
                    linear(s - 3)
            route(1)
            slots_of(1)


def kernel(**inputs):
    import numpy as np
    import concourse.bacc as bacc
    from concourse.bass_utils import run_bass_kernel_spmd

    a = {k: np.asarray(v) for k, v in inputs.items()}
    D = a["x"].shape[-1]
    P_ = 128
    E = a["L0_ffn_b_in"].shape[0]

    def per_part(b):
        return b.reshape(E, -1, P_).transpose(2, 0, 1).reshape(P_, -1)

    arrays = {
        "x": a["x"].reshape(-1, D),
        "ctx_t": a["ctx_1024"].reshape(-1, D).T,
        "wq": a["L0_xattn_Wq"].reshape(D, -1),
        "wk": a["L0_xattn_Wk"].reshape(D, -1),
        "wv": a["L0_xattn_Wv"].reshape(D, -1),
        "scale_q": a["L0_xattn_scale_q"],
        "scale_k": a["L0_xattn_scale_k"],
        "wo": a["L0_xattn_Wo"].reshape(-1, D),
        "bo": a["L0_xattn_bo"],
        "rw0": a["L0_ffn_router_w"],
        "w_in0": a["L0_ffn_w_in"],
        "b_in0": per_part(a["L0_ffn_b_in"]),
        "w_out0": a["L0_ffn_w_out"],
        "b_out0": a["L0_ffn_b_out"].reshape(-1),
        "cw1_t": a["L1_xattn_W"][:, :D].T,
        "cw2_t": a["L1_xattn_W"][:, D:].T,
        "cb": a["L1_xattn_b"],
        "rw1_t": a["L1_ffn_router_w"].T,
        "rb1": a["L1_ffn_router_b"],
        "w1_t": a["L1_ffn_w1"].transpose(0, 2, 1),
        "b1": per_part(a["L1_ffn_b1"]),
        "w2_t": a["L1_ffn_w2"].transpose(0, 2, 1),
        "b2": a["L1_ffn_b2"].reshape(-1),
    }
    arrays = {k: np.ascontiguousarray(v) for k, v in arrays.items()}
    nc = bacc.Bacc("TRN2", target_bir_lowering=False, num_devices=1)
    args = [nc.dram_tensor(k, v.shape, mybir.dt.from_np(v.dtype), kind="ExternalInput").ap() for k, v in arrays.items()]
    out = nc.dram_tensor("out", arrays["x"].shape, F32, kind="ExternalOutput").ap()
    build(nc, *args, out)
    r = run_bass_kernel_spmd(nc, [arrays], core_ids=[0])
    return r.results[0]["out"].reshape(a["x"].shape)
```

```python
import math
from contextlib import ExitStack

import concourse.bass as bass
from concourse import mybir

F32, F16, I32, U32 = mybir.dt.float32, mybir.dt.float16, mybir.dt.int32, mybir.dt.uint32
ALU = mybir.AluOpType
ACT = mybir.ActivationFunctionType
AX = mybir.AxisListType

P = 128
RSQRT_SEED = 0x5F3759DF


def product(shape):
    r = 1
    for n in shape:
        r *= n
    return r


def carve(region, at, shape, dt):
    size = 2 if dt == F16 else 4
    end = at + product(shape) * size
    v = region[:, at // 4:(end + 3) // 4]
    if dt != F32:
        v = v.bitcast(dt)
    if len(shape) > 1:
        names = [f"d{n}" for n in range(len(shape))]
        v = v.rearrange(f"p ({' '.join(names)}) -> p {' '.join(names)}", **dict(zip(names[1:], shape[1:])))
    return v, end


class LayerNorm:

    def __init__(self, n, sem, region, at, ps, D):
        self.n, self.ps = n, ps
        self.full32, at = carve(region, at, [2, D], F32)
        self.rows, at = carve(region, at, [2, 2 * D], F16)
        self.xT, at = carve(region, at, [2, 2 * D // P, P], F16)
        self.end = at
        self.var = sem(f"ln{n}_variance")
        self.full = sem(f"ln{n}_normed")
        self.rstd = sem(f"ln{n}_rstd") if n >= 2 else None
        self.hi = sem(f"ln{n}_hi")
        self.lo = sem(f"ln{n}_lo")
        self.tr = sem(f"ln{n}_transposed")
        self.cols = sem(f"ln{n}_columns")


class Moe:
    pass


def build(nc, x, ctx_t, wq, wk, wv, scale_q, scale_k, wo, bo, rw0, w_in0, b_in0, w_out0, b_out0,
          cw1_t, cw2_t, cb, rw1_t, rb1, w1_t, b1, w2_t, b2, out):
    T, D = x.shape
    DC = D // P
    NT = T // P
    NB = 2
    L = ctx_t.shape[1] // NB
    DH = scale_q.shape[0]
    HE = wq.shape[1]
    NH = HE // DH
    NP = NH // 2
    PW = 2 * L
    NS = NH * L
    KC = math.ceil(NS / P)
    E = rw0.shape[1]
    H0, H1 = w_in0.shape[2], w1_t.shape[2]
    SW = 2 * P
    NSLOT = (2 * T + E * (SW - 1)) // SW
    NQ = 2 * NSLOT
    WS = 64.0
    PS = 1024.0
    LN_EPS, RMS_EPS = 1e-5, 1e-6
    CH = 1024
    NEG = -3.0e38
    VW_FIRST = 12
    VW_STEP = 4
    AHEAD = 2
    RING = 4

    with ExitStack() as ctx:
        def sb(name, shape, dt):
            return ctx.enter_context(nc.sbuf_tensor(name, shape, dt))

        sems = {}

        def sem(name):
            if name not in sems:
                sems[name] = ctx.enter_context(nc.semaphore(name))
            return sems[name]

        W1R = sb("w1_region", [P, 16384], F32)
        W2R = sb("w2_region", [P, 16384], F32)
        WBR = sb("wb_region", [P, 8192], F32)
        X = sb("x_res", [P, NT, D], F32)
        SLR = sb("slot_region", [P, 4096], F32)
        STG = sb("staging", [P, 2, CH], F32)

        w1s, _ = carve(W1R, 0, [E * 2 * DC * H1], F16)
        w2s, _ = carve(W2R, 0, [E * 2 * (H1 // P) * D], F16)
        wb_in, at = carve(WBR, 0, [E * 2 * DC * H0], F16)
        wb_out, at = carve(WBR, at, [E * 2 * (H0 // P) * D], F16)

        PSUM = ctx.enter_context(nc.psum_tensor("banks", [P, 8, 512], F32))
        bank = [PSUM[:, i, :] for i in range(8)]

        def half(k, n):
            return bank[k][:, 256 * n:256 * n + 256].bitcast(F16).rearrange("p (a b) -> p a b", b=P)

        zt, at = carve(W1R, 0, [NP, NB, 2 * P + PW], F32)
        pb2, at = carve(W1R, at, [KC * P], F32)
        vwf, at = carve(W1R, at, [2, D], F32)
        onehot0, _ = carve(W1R, 32768, [2 * NT, P], F16)
        ln0 = LayerNorm(0, sem, W1R, at, half(0, 0), D)
        ln1 = LayerNorm(1, sem, W1R, ln0.end, half(0, 1), D)
        ctx_s, at = carve(W1R, ln1.end, [DC, NB * L], F32)
        cw2, at = carve(W1R, at, [DC, D], F32)
        cmb, at = carve(W1R, at, [DC, NB, P], F32)
        cmean, at = carve(W1R, at, [DC, NB], F32)
        cb_s, at = carve(W1R, at, [NB, D], F32)
        route0, _ = carve(W1R, ln1.end, [1600], F32)
        assert at <= 65536
        wk_s, at = carve(WBR, 0, [DC, HE], F32)
        wv_s, at = carve(WBR, at, [DC, HE], F32)
        wo_s, at = carve(WBR, at, [NP, D], F32)
        assert at <= 32768
        wq_h, at = carve(W2R, 0, [DC, HE], F16)
        wq_l, at = carve(W2R, at, [DC, HE], F16)
        kbh, at = carve(W2R, at, [NP, NB, 2, L], F16)
        kbl, at = carve(W2R, at, [NP, NB, 2, L], F16)
        vw, at = carve(W2R, at, [NB, KC, 2, D], F16)
        qsq, at = carve(W2R, at, [NP, P], F32)
        pb01, at = carve(W2R, at, [2, KC * P], F32)
        qh, at = carve(W2R, at, [NP, P], F16)
        ql, at = carve(W2R, at, [NP, P], F16)
        pth_at = at
        pth, at = carve(W2R, at, [KC, P], F16)
        ptl, at = carve(W2R, at, [KC, P], F16)
        bo_row, at = carve(W2R, at, [D], F32)
        ident_f, at = carve(W2R, at, [P], F32)
        heads2, at = carve(W2R, at, [P], F32)
        assert at <= 65536
        pb = [pb01[:, 0, :], pb01[:, 1, :], pb2]
        kf = pb[0][:, 0:NP * NB * L].rearrange("p (j c) -> p j c", j=NP)
        k_tmp, _ = carve(W2R, pth_at, [2, NP * NB * L // 2], F32)
        ksq = pb[1][:, 0:NP * NB * L].rearrange("p (j c) -> p j c", j=NP)

        ident_h = sb("ident_h", [P, P], F16)
        before = sb("before", [P, P], F32)
        ones = sb("ones", [P, P], F32)
        first8 = sb("first8", [P, E], F32)
        iota_r = sb("iota_r", [P, P], F16)
        tokens = sb("tokens", [P, NT, 2], F32)
        ctx_bias = sb("ctx_bias", [P, NB, 2, D], F16)
        wc = sb("wc", [P, 2, DC, D], F16)
        rws = sb("rws", [P, 2, 2, DC, E], F16)
        rbb = sb("rbb", [P, E], F32)
        b_in0_s = sb("b_in0_s", [P, E * (H0 // P)], F32)
        b1_s = sb("b1_s", [P, E * (H1 // P)], F32)
        sks = sb("sks", [P, 4], F32)
        neghalf = sb("neghalf", [P, 1], F32)
        st6 = sb("st6", [P, 4, 6], F32)
        mv = sb("mv", [P, 4, 2, 2], F32)
        rv = sb("rv", [P, 4, 2, 2], F32)
        mxs = sb("mxs", [P, NH], F32)
        rq = sb("rq", [P, 2, NH], F32)
        rs = sb("rs", [P, NH], F32)
        lg = sb("lg", [P, NT, E], F32)
        gates = sb("gates", [P, 2, NT], F32)
        slots = sb("slots", [P, NT, 2], U32)
        index = sb("index", [P, NQ], U32)
        back = lg[:, :, :].rearrange("p t e -> p (t e)")[:, 0:NQ].bitcast(U32)
        expert = sb("expert", [P, 2, NSLOT], I32)

        rows_dram = nc.dram_tensor("normed_rows", [T, 2 * D], F16).ap()
        y_dram = nc.dram_tensor("sorted_y", [NQ * P, D], F32).ap()
        y_token = nc.dram_tensor("token_y", [2 * (T + 1) + NQ * P, D], F32).ap()

        chunks = []
        for dc in range(DC):
            chunks.append((wq[dc * P:(dc + 1) * P, :], wq_h[:, dc, :], wq_l[:, dc, :]))
        chunks.append((cw1_t.rearrange("(c p) n -> p c n", p=P), wc[:, 0, :, :], wc[:, 1, :, :]))
        chunks.append((None, rws[:, 0, :, :, :].rearrange("p a b c -> p (a b c)"),
                       rws[:, 1, :, :, :].rearrange("p a b c -> p (a b c)")))
        PRE = len(chunks)
        per = DC * H0
        for store, src in ((wb_in, w_in0), (wb_out, w_out0)):
            v = store.rearrange("p (e s n) -> p e s n", s=2, n=per)
            g = CH // per
            for e in range(0, E, g):
                chunks.append((src[e:e + g].rearrange("e (c p) n -> p e c n", p=P), v[:, e:e + g, 0, :], v[:, e:e + g, 1, :]))
        B_CH = len(chunks)
        per = DC * H1
        big = []
        for store, src in ((w1s, w1_t), (w2s, w2_t)):
            v = store.rearrange("p (e s n) -> p e s n", s=2, n=per)
            w = src.rearrange("e (c p) n -> p e c n", p=P)
            cs = w.shape[2] * CH // per
            for e in range(E):
                for part in range(per // CH):
                    c = slice(part * CH, (part + 1) * CH)
                    big.append((e, (w[:, e, part * cs:(part + 1) * cs, :], v[:, e, 0, c], v[:, e, 1, c])))
        chunks += [c for e, c in big if e < E - 1] + [c for e, c in big if e == E - 1]
        NCH = len(chunks)
        A_CH = 16
        LATE = 2 * (per // CH)

        def staged(k):
            hi = chunks[k][1]
            v = STG[:, k % 2, 0:product(hi.shape[1:])]
            if len(hi.shape) == 3:
                v = v.rearrange("p (a b) -> p a b", a=hi.shape[1])
            return v

        moes = []
        for layer, (H, wa, wb, b_s) in enumerate(((H0, wb_in, wb_out, b_in0_s), (H1, w1s, w2s, b1_s))):
            m = Moe()
            m.H, m.HC, m.wa, m.wb, m.b = H, H // P, wa, wb, b_s
            m.PARTS = 1 if layer == 0 else 2
            m.HH = m.HC // m.PARTS
            m.LAG = 2 - layer
            m.rows, at = carve(SLR, 0, [RING, 2, 2 * D], F16)
            m.xT, at = carve(SLR, at, [2, 2 * DC, SW], F16)
            m.y, at = carve(SLR, at, [2, 2, D], F32)
            if layer == 0:
                m.g, at = carve(W1R, 65536 - 8192, [2, m.HH, SW], F32)
                m.hh, at = carve(W1R, at, [2, m.HC, SW], F16)
                m.hl, at = carve(W1R, at, [2, m.HC, SW], F16)
                m.b2, _ = carve(W2R, 65536 - 8192, [E * D], F32)
            else:
                m.hh, at = carve(WBR, 0, [2, m.HC, SW], F16)
                m.hl, at = carve(WBR, at, [2, m.HC, SW], F16)
                m.g, at = carve(WBR, at, [2, m.HH, SW], F32)
                m.b2, at = carve(WBR, at, [E * D], F32)
                assert at <= 32768
            moes.append(m)
        NG_BUF = 3
        yg, at = carve(WBR, 0, [NG_BUF, 2, D], F32)
        ln2 = LayerNorm(2, sem, WBR, at, half(0, 0), D)
        ln3 = LayerNorm(3, sem, WBR, ln2.end, half(1, 0), D)
        onehot1, at = carve(SLR, 0, [2 * NT, P], F16)
        route1, at = carve(SLR, at, [1600], F32)
        assert ln3.end <= 24576 and at <= 16384
        yg1, _ = carve(WBR, 0, [6, 2, D], F32)
        behind = route1[:, 1040:1040 + NQ]
        routes = [route0, route1]
        onehots = [onehot0, onehot1]

        GP = 4
        groups = [(a, min(a + GP, KC)) for a in range(0, KC, GP)]
        NG = len(groups)
        score_banks = PSUM[:, 3:6, 0:6 * L].rearrange("p b (h k) -> p b h k", k=L)
        SSQ = bank[5][:, 320:320 + NH]
        LOG = bank[5][:, 400:400 + E]
        q_ps = PSUM[:, 1:3, :].rearrange("p b (j t) -> p (b j) t", t=P)
        o_ps = bank[0][:, 0:D]
        c_ps = bank[6][:, 0:D]
        FULL = NP // 3
        LAST = slice(FULL * 6, NH)


        def hidden(m, u):
            b = 1 + 2 * (u % 2)
            return PSUM[:, b:b + 2, :].rearrange("p b (c t) -> p (b c) t", t=SW)[:, 0:m.HH, :]

        block = ctx.enter_context(nc.Block())

        @block.sync
        def _(sp):
            def load(dst, src, name):
                sp.dma_start(dst, src).then_inc(sem(name), 16)

            def stage(k):
                if k >= 2:
                    sp.wait_ge(sem(f"chunk_lo{k % 2}"), k // 2)
                loaded = sem(f"chunk_loaded{k % 2}")
                src = chunks[k][0]
                if src is None:
                    n = DC * E
                    for layer, w in enumerate((rw0, rw1_t)):
                        sp.dma_start(STG[:, k % 2, layer * n:(layer + 1) * n].rearrange("p (c e) -> p c e", c=DC),
                                     w.rearrange("(c p) e -> p c e", p=P)).then_inc(
                            loaded if layer else sem("router_loaded"), 16)
                    return
                dst = STG[:, k % 2, 0:product(src.shape[1:])]
                if len(src.shape) == 3:
                    dst = dst.rearrange("p (a b) -> p a b", a=src.shape[1])
                if len(src.shape) == 4:
                    dst = dst.rearrange("p (e a b) -> p e a b", e=src.shape[1], a=src.shape[2])
                    sp.dma_start(dst[:, 0], src[:, 0]).then_inc(sem(f"chunk_part{k % 2}"), 16)
                    sp.dma_start(dst[:, 1], src[:, 1]).then_inc(loaded, 16)
                    return
                sp.dma_start(dst, src).then_inc(loaded, 16)

            load(ctx_s, ctx_t.rearrange("(c p) n -> p c n", p=P), "ctx_loaded")
            load(wk_s, wk.rearrange("(c p) n -> p c n", p=P), "wk_loaded")
            for h in range(2):
                load(sks[h * DH:(h + 1) * DH, 0:1], scale_q.rearrange("(e o) -> e o", o=1), "scales_loaded")
                load(sks[h * DH:(h + 1) * DH, 1:2], scale_k.rearrange("(e o) -> e o", o=1), "scales_loaded")
            load(wv_s, wv.rearrange("(c p) n -> p c n", p=P), "wv_loaded")
            load(cw2, cw2_t.rearrange("(c p) n -> p c n", p=P), "cw2_loaded")
            q4 = NT // 4
            xv = x.rearrange("(t p) d -> p t d", p=P)
            load(X[:, 0:q4, :], xv[:, 0:q4, :], "x_loaded0")
            stage(0)
            stage(1)
            load(wo_s, wo.rearrange("(j p) n -> p j n", p=P), "wo_loaded")
            for b in range(NB):
                load(cb_s[:, b, :], cb.partition_broadcast(P), "cb_loaded")
            sp.wait_ge(sem("bo_zeroed"), 1)
            load(bo_row[NS % P:NS % P + 1, :], bo.rearrange("(o n) -> o n", o=1), "bo_loaded")
            for g in range(1, 4):
                load(X[:, g * q4:(g + 1) * q4, :], xv[:, g * q4:(g + 1) * q4, :], f"x_loaded{g}")
            for k in range(2, PRE):
                stage(k)
            load(b_in0_s[:, :], b_in0, "b_in0_loaded")
            load(b1_s[:, :], b1, "b1_loaded")
            load(rbb[:, :], rb1.partition_broadcast(P), "rb_loaded")
            sp.wait_ge(sem("vw_done"), NB * KC)

            rows_v = rows_dram.rearrange("(t p) d -> t p d", p=P)

            def keep_rows(o, i):
                sp.wait_ge(o.lo, i + 1)
                sp.dma_start(rows_v[i], o.rows[:, i % 2, :]).then_inc(sem(f"rows_kept{o.n}_{i % 2}"), 16)

            stage(PRE)
            stage(PRE + 1)
            for i in range(NT):
                keep_rows(ln1, i)
                stage(PRE + 2 + i)

            yv = y_dram.rearrange("(j a p) d -> j p a d", a=2, p=P)

            def keep_y(layer, j):
                sp.wait_ge(sem(f"y_ready{layer}"), j + 1)
                sp.dma_start(yv[j], moes[layer].y[:, j % 2]).then_inc(sem(f"y_kept{layer}_{j % 2}"), 16)

            sp.wait_ge(sem("routed"), 1)
            load(moes[0].b2, b_out0.partition_broadcast(P), "b2_loaded0")
            for j in range(NSLOT + 4):
                if PRE + A_CH + 2 + j < NCH - LATE + 2:
                    stage(PRE + A_CH + 2 + j)
                if j >= 4:
                    keep_y(0, j - 4)
            for k in range(NCH - LATE + 2, NCH):
                stage(k)
            load(moes[1].b2, b2.partition_broadcast(P), "b2_loaded1")
            for i in range(NT):
                keep_rows(ln3, i)
            ov = out.rearrange("(t p) d -> p t d", p=P)
            for i in range(NT):
                sp.wait_ge(sem("y_used1"), 2 * (i + 1))
                sp.dma_start(ov[:, i, :], X[:, i, :]).then_inc(sem("out_stored"), 16)
            sp.wait_ge(sem("out_stored"), 16 * NT)

        @block.gpsimd
        def _(pool):
            g = nc.gpsimd
            chain = [0]

            def link(ins):
                chain[0] += 1
                ins.then_inc(sem("pool_chain"), 1)
                pool.wait_ge(sem("pool_chain"), chain[0])

            link(g.memset(neghalf[:, :], -0.5))
            link(g.memset(heads2, 0.0))
            link(g.memset(heads2[0:DH, 0:DH], 1.0))
            g.memset(heads2[DH:P, DH:P], 1.0).then_inc(sem("heads_ready"), 1)
            pool.wait_ge(sem("heads_ready"), 1)
            g.memset(zt, 0.0).then_inc(sem("zt_zeroed"), 1)
            g.memset(kbh, 0.0)
            g.memset(kbl, 0.0)
            g.memset(bo_row, 0.0).then_inc(sem("bo_zeroed"), 1)
            link(g.memset(pb01[:, :, NS:KC * P], 0.0))
            link(g.memset(pb2[:, NS:KC * P], 0.0))
            g.memset(pb2[:, NS:NS + 1], PS)
            g.memset(pb01[:, :, NS:NS + 1], PS).then_inc(sem("kb_zeroed"), 1)
            for t in (ident_h[:, :], ident_f):
                link(g.memset(t, 0.0))
                link(g.affine_select(out=t, in_=t, compare_op=ALU.not_equal, fill=1.0, base=0,
                                     pattern=[[-1, P]], channel_multiplier=1))
            link(g.memset(ones[:, :], 1.0))
            link(g.affine_select(out=before[:, :], in_=ones[:, :], compare_op=ALU.is_gt, fill=0.0, base=0,
                                 pattern=[[1, P]], channel_multiplier=-1))
            link(g.iota(first8[:, :], pattern=[[-1, E]], base=E, channel_multiplier=0,
                        allow_small_or_imprecise_dtypes=True))
            link(g.iota(tokens[:, :, 0], pattern=[[P, NT]], base=1, channel_multiplier=1,
                        allow_small_or_imprecise_dtypes=True))
            link(g.iota(tokens[:, :, 1], pattern=[[-P, NT]], base=-1, channel_multiplier=-1,
                        allow_small_or_imprecise_dtypes=True))
            g.iota(iota_r[:, :], pattern=[[1, P]], base=0, channel_multiplier=0,
                   allow_small_or_imprecise_dtypes=True).then_inc(sem("consts_ready"), 1)

            def split_lo(k):
                pool.wait_ge(sem("chunk_scaled"), k // 2 + 1)
                g.tensor_tensor(chunks[k][2], staged(k), chunks[k][1], ALU.subtract).then_inc(sem("chunk_lo0"), 1)

            def vw_lo(n):
                pool.wait_ge(sem("vw_hi"), n + 1)
                g.tensor_tensor(vw[:, n // KC, n % KC, 1, :], vwf[:, n % 2, :], vw[:, n // KC, n % KC, 0, :],
                                ALU.subtract).then_inc(sem("vw_ready"), 1)

            def norm(o, i):
                pool.wait_ge(o.var, i + 1)
                r = rv[:, o.n, i % 2, :]
                link(g.tensor_tensor(r[:, 0:1], mv[:, o.n, i % 2, 1:2], neghalf[:, :], ALU.pow))
                link(g.tensor_scalar(r[:, 1:2], mv[:, o.n, i % 2, 0:1], -1.0, 1.0, ALU.mult, ALU.mult))
                if i >= 2:
                    pool.wait_ge(o.lo, i - 1)
                g.tensor_scalar(o.full32[:, i % 2, :], X[:, i, :], r[:, 1:2], r[:, 0:1], ALU.add, ALU.mult).then_inc(
                    o.full, 1)

            def rstd(o, i):
                pool.wait_ge(o.var, i + 1)
                if i >= 2:
                    pool.wait_ge(o.full, i - 1)
                r = rv[:, o.n, i % 2, :]
                link(g.tensor_tensor(r[:, 0:1], mv[:, o.n, i % 2, 1:2], neghalf[:, :], ALU.pow))
                g.tensor_scalar(r[:, 1:2], mv[:, o.n, i % 2, 0:1], r[:, 0:1], -1.0, ALU.mult, ALU.mult).then_inc(o.rstd, 1)

            def q_rms(i):
                pool.wait_ge(sem("q_ms"), i + 1)
                v = rq[:, i % 2, :]
                link(g.tensor_tensor(v, v, neghalf[:, 0:1].to_broadcast([P, NH]), ALU.pow))

            def p_rows(i):
                return pb[i % 3][:, 0:NS].rearrange("p (h k) -> p h k", k=L)

            def scale_scores(i):
                pool.wait_ge(sem("scores_shifted"), i + 1)
                g.tensor_tensor(p_rows(i), p_rows(i), rq[:, i % 2, :, None].to_broadcast([P, NH, L]),
                                ALU.mult).then_inc(sem("scores_scaled"), 1)

            def norm_weights(i):
                pool.wait_ge(sem("row_sums"), i + 1)
                g.tensor_tensor(p_rows(i), p_rows(i), rs[:, :, None].to_broadcast([P, NH, L]),
                                ALU.mult).then_inc(sem("weights_ready"), 1)

            for n in range(VW_FIRST):
                vw_lo(n)
            for s in range(NT + 9):
                if 0 <= s - 3 < NT:
                    q_rms(s - 3)
                    scale_scores(s - 3)
                if s < NT:
                    norm(ln0, s)
                if 0 <= s - 6 < NT:
                    norm(ln1, s - 6)
                for n in range(VW_FIRST + VW_STEP * s, min(NB * KC, VW_FIRST + VW_STEP * (s + 1))):
                    vw_lo(n)
                if s < PRE and s % 2 == 0:
                    split_lo(s)
                if 0 <= s - 4 < NT:
                    norm_weights(s - 4)
                if 0 <= s - 6 < NT and (PRE + s - 6) % 2 == 0:
                    split_lo(PRE + s - 6)

            def number_tokens(layer):
                at_q = routes[layer][:, 128:128 + NT * NQ].bitcast(F16).rearrange("p (n q) -> p n q", q=NQ)
                num = tokens[:, :, :].rearrange("p t c -> p (t c)")[:, :, None].to_broadcast([P, 2 * NT, NQ])
                pool.wait_ge(sem("tiles_hot"), layer + 1)
                g.tensor_tensor(at_q, at_q, num, ALU.mult).then_inc(sem("places"), 1)

            def gather_rows(layer, j):
                m = moes[layer]
                for a in range(2):
                    if j >= RING:
                        pool.wait_ge(sem(f"slot_tr{layer}"), j - RING + 1)
                    q = 2 * j + a
                    g.indirect_dma_start(
                        out=m.rows[:, j % RING, a, :], out_offset=None, in_=rows_dram,
                        in_offset=bass.IndirectOffsetOnAxis(ap=index[:, q:q + 1], axis=0)).then_inc(
                        sem(f"rows_gathered{layer}_{j % RING}"), 16)

            def slot_rows(layer):
                number_tokens(layer)
                pool.wait_ge(sem("routed"), layer + 1)
                for b in range(2):
                    pool.wait_ge(sem(f"rows_kept{1 + 2 * layer}_{b}"), 16 * (NT // 2))
                for j in range(AHEAD):
                    gather_rows(layer, j)
                if layer == 1:
                    pool.wait_ge(sem("back_ready"), 1)
                for j in range(NSLOT + 3 * layer):
                    if j + AHEAD < NSLOT:
                        gather_rows(layer, j + AHEAD)
                    if layer == 1 and j >= 3:
                        scatter_y(j - 3)
                    if layer == 0:
                        k = PRE + A_CH + j
                        if k < NCH - LATE and k % 2 == 0:
                            split_lo(k)
                if layer == 0:
                    for b in range(2):
                        pool.wait_ge(sem(f"y_kept0_{b}"), 16 * ((NSLOT + 1 - b) // 2))

            def gather_y(layer, i, ring):
                n = ring.shape[1]
                for c in range(2):
                    if i >= n:
                        pool.wait_ge(sem(f"y_used{layer}"), 2 * (i - n) + c + 1)
                    g.indirect_dma_start(
                        out=ring[:, i % n, c, :], out_offset=None, in_=y_dram,
                        in_offset=bass.IndirectOffsetOnAxis(ap=slots[:, i, c:c + 1], axis=0)).then_inc(
                        sem(f"y_gathered{layer}_{i % n}"), 16)

            def scatter_y(j):
                for a in range(2):
                    pool.wait_ge(sem("y_ready1"), j + 1)
                    q = 2 * j + a
                    g.indirect_dma_start(
                        out=y_token, out_offset=bass.IndirectOffsetOnAxis(ap=back[:, q:q + 1], axis=0),
                        in_=moes[1].y[:, j % 2, a, :], in_offset=None).then_inc(sem(f"y_kept1_{j % 2}"), 16)

            slot_rows(0)
            g.iota(behind, pattern=[[P, NQ]], base=2 * (T + 1), channel_multiplier=1,
                   allow_small_or_imprecise_dtypes=True).then_inc(sem("behind_ready"), 1)
            for s in range(NT + 5):
                if s < NT:
                    gather_y(0, s, yg)
                if 0 <= s - 2 < NT:
                    rstd(ln2, s - 2)
                if 0 <= s - 5 < NT:
                    rstd(ln3, s - 5)
                if 0 <= s - 2 < LATE and (NCH - LATE + s) % 2 == 0:
                    split_lo(NCH - LATE + s - 2)
            slot_rows(1)

        @block.scalar
        def _(act):
            s_ = nc.scalar

            def split_hi(k):
                act.wait_ge(sem(f"chunk_loaded{k % 2}"), 16 * (k // 2 + 1))
                if chunks[k][0] is None:
                    act.wait_ge(sem("router_loaded"), 16)
                elif len(chunks[k][0].shape) == 4:
                    n = sum(1 for c in range(k % 2, k + 1, 2) if chunks[c][0] is not None and len(chunks[c][0].shape) == 4)
                    act.wait_ge(sem(f"chunk_part{k % 2}"), 16 * n)
                s_.activation(chunks[k][1], staged(k), ACT.Copy, scale=WS).then_inc(sem(f"chunk_hi{k % 2}"), 1)
                if k % 2 == 0:
                    act.wait_ge(sem("chunk_hi0"), k // 2 + 1)
                    s_.activation(staged(k), staged(k), ACT.Copy, scale=WS).then_inc(sem("chunk_scaled"), 1)

            for j in range(NP):
                act.wait_ge(sem("k_done"), j + 1)
                s_.activation(ksq[:, j, :], bank[3 + j % 2][:, 0:NB * L], ACT.Square).then_inc(sem("k_sq"), 1)
            for k in range(2):
                split_hi(k)
            act.wait_ge(sem("zt_zeroed"), 1)
            for j in range(NP):
                act.wait_ge(sem("vt_done"), j + 1)
                for h in range(2):
                    rows = slice(h * DH, (h + 1) * DH)
                    s_.activation(zt[rows, j, :, P + h * L:P + (h + 1) * L], bank[1 + j % 2][rows, 0:NB * L].rearrange(
                        "p (b k) -> p b k", b=NB), ACT.Copy).then_inc(sem("vt_copied"), 1)

            def k_hi():
                act.wait_ge(sem("k_normed"), 1)
                act.wait_ge(sem("kb_zeroed"), 1)
                for h in range(2):
                    rows = slice(h * DH, (h + 1) * DH)
                    s_.activation(kbh[rows, :, :, h, :], kf[rows].rearrange("p j (b k) -> p j b k", b=NB),
                                  ACT.Copy).then_inc(sem("kb_hi"), 1)

            def vw_hi(n):
                act.wait_ge(sem("vw_done"), n + 1)
                if n >= 2:
                    act.wait_ge(sem("vw_ready"), n - 1)
                s_.activation(vwf[:, n % 2, :], bank[6 + n % 2][:, 0:D], ACT.Copy, scale=WS)
                s_.activation(vw[:, n // KC, n % KC, 0, :], bank[6 + n % 2][:, 0:D], ACT.Copy, scale=WS).then_inc(
                    sem("vw_hi"), 1)

            def norm(o, i):
                act.wait_ge(o.rstd, i + 1)
                if i >= 2:
                    act.wait_ge(o.lo, i - 1)
                r = rv[:, o.n, i % 2, :]
                s_.activation(o.full32[:, i % 2, :], X[:, i, :], ACT.Identity, bias=r[:, 1:2], scale=r[:, 0:1]).then_inc(
                    o.full, 1)

            def norm_hi(o, i):
                act.wait_ge(o.full, i + 1)
                if i >= 2:
                    act.wait_ge(o.tr, i - 1)
                    if o.n in (1, 3):
                        act.wait_ge(sem(f"rows_kept{o.n}_{i % 2}"), 16 * (i // 2))
                s_.activation(o.rows[:, i % 2, 0:D], o.full32[:, i % 2, :], ACT.Copy).then_inc(o.hi, 1)

            def columns(o, i, user):
                act.wait_ge(o.tr, i + 1)
                if i >= 2:
                    act.wait_ge(sem(user), i - 1)
                s_.activation(o.xT[:, i % 2], o.ps, ACT.Copy).then_inc(o.cols, 1)

            def q_hi(i):
                act.wait_ge(sem("q_done"), i + 1)
                if i >= 1:
                    act.wait_ge(sem("scores_done"), i)
                s_.activation(qh, q_ps, ACT.Copy).then_inc(sem("q_hi"), 1)
                if i >= 1:
                    act.wait_ge(sem("ssq_done"), i)
                s_.activation(qsq, q_ps, ACT.Square, scale=1.0 / WS).then_inc(sem("q_sq"), 1)

            def exp(i):
                act.wait_ge(sem("scores_scaled"), i + 1)
                v = pb[i % 3][:, 0:NS]
                s_.activation(v, v, ACT.Exp, scale=1.0 / (WS * WS)).then_inc(sem("exp_done"), 1)

            def pt_hi(i, n):
                a, b = groups[n]
                act.wait_ge(sem("weights_tr"), NG * i + n + 1)
                if i >= 1:
                    act.wait_ge(sem("attn_done"), i)
                s_.activation(pth[:, a:b, :], bank[6 + (NG * i + n) % 2][:, 0:(b - a) * P].rearrange(
                    "p (c t) -> p c t", t=P), ACT.Copy).then_inc(sem("pt_hi"), 1)

            for n in range(VW_FIRST):
                vw_hi(n)
            for s in range(NT + 9):
                if 0 <= s - 2 < NT:
                    q_hi(s - 2)
                if 0 <= s - 5 < NT:
                    pt_hi(s - 5, 0)
                    pt_hi(s - 5, 1)
                if 0 <= s - 1 < NT:
                    if s - 1 >= 6:
                        act.wait_ge(ln1.tr, s - 6)
                    columns(ln0, s - 1, "q_done")
                if 0 <= s - 7 < NT:
                    columns(ln1, s - 7, "logits_done0")
                if 0 <= s - 5 < NT:
                    pt_hi(s - 5, 2)
                if s < NT:
                    norm_hi(ln0, s)
                if 0 <= s - 6 < NT:
                    norm_hi(ln1, s - 6)
                for n in range(VW_FIRST + VW_STEP * s, min(NB * KC, VW_FIRST + VW_STEP * (s + 1))):
                    vw_hi(n)
                if s == 1:
                    k_hi()
                if 0 <= s - 3 < NT:
                    exp(s - 3)
                if 2 <= s < PRE:
                    split_hi(s)
                if 0 <= s - 6 < NT:
                    split_hi(PRE + s - 6)

            def route(layer):
                act.wait_ge(sem("route_shift"), layer + 1)
                r = routes[layer]
                s_.activation(r[:, 0:NT * E], r[:, 0:NT * E], ACT.Exp).then_inc(sem("route_exp"), 1)
                s_.activation(r[:, 1152:1152 + NT], r[:, 1152:1152 + NT], ACT.Exp).then_inc(sem("route_exp"), 1)

            def gelu(layer, j):
                m = moes[layer]
                for a in range(m.PARTS):
                    u = m.PARTS * j + a
                    v = m.g[:, u % 2]
                    act.wait_ge(sem(f"h_biased{layer}"), u + 1)
                    s_.activation(v, v, ACT.Gelu_apprx_tanh).then_inc(sem("gelu"), 1)
                    act.wait_ge(sem("gelu"), NSLOT * layer + u + 1)
                    if j >= 2:
                        act.wait_ge(sem(f"slot_y{layer}"), j - 1)
                    s_.activation(m.hh[:, j % 2, a * m.HH:(a + 1) * m.HH, :], v, ACT.Copy).then_inc(
                        sem(f"h_hi{layer}"), 1)

            route(0)
            act.wait_ge(sem("gates_ready"), 1)
            for s in range(NSLOT + 1):
                if s < NSLOT and PRE + A_CH + s < NCH - LATE:
                    split_hi(PRE + A_CH + s)
                if s >= 1:
                    gelu(0, s - 1)
            act.wait_ge(sem("y_ready0"), NSLOT)
            for s in range(NT + 7):
                if 0 <= s - 3 < NT:
                    columns(ln2, s - 3, "linear_done")
                if 0 <= s - 2 < NT:
                    norm(ln2, s - 2)
                    norm_hi(ln2, s - 2)
                if 0 <= s - 6 < NT:
                    columns(ln3, s - 6, "logits_done1")
                if 0 <= s - 5 < NT:
                    norm(ln3, s - 5)
                    norm_hi(ln3, s - 5)
                if 0 <= s - 2 < LATE:
                    split_hi(NCH - LATE + s - 2)
            route(1)
            for j in range(NSLOT):
                gelu(1, j)
            for b in range(2):
                act.wait_ge(sem(f"y_kept1_{b}"), 32 * ((NSLOT + 1 - b) // 2))
            for i in range(NT):
                n = yg1.shape[1]
                if i >= n:
                    act.wait_ge(sem("y_used1"), 2 * (i - n + 1))
                for c in range(2):
                    row = c * (T + 1) + 1 + i * P
                    act.dma_start(yg1[:, i % n, c, :], y_token[row:row + P, :]).then_inc(sem(f"y_gathered1_{i % n}"), 16)

        @block.vector
        def _(dve):
            v = nc.vector
            chain = [0]

            def link(ins):
                chain[0] += 1
                ins.then_inc(sem("dve_chain"), 1)
                dve.wait_ge(sem("dve_chain"), chain[0])

            dve.wait_ge(sem("scales_loaded"), 4 * 16)
            link(v.tensor_tensor(sks[:, 2:3], sks[:, 0:1], sks[:, 1:2], ALU.mult))
            link(v.tensor_scalar(sks[:, 3:4], sks[:, 2:3], WS / math.sqrt(DH), None, ALU.mult))
            dve.wait_ge(sem("ctx_loaded"), 16)
            link(v.tensor_reduce(cmean, ctx_s.rearrange("p c (b k) -> p c b k", b=NB), axis=AX.X, op=ALU.add))
            v.tensor_scalar(cmb, cmean[:, :, :, None].to_broadcast([P, DC, NB, P]), 1.0 / L, None,
                            ALU.mult).then_inc(sem("mean_ready"), 1)
            for j in range(NP):
                dve.wait_ge(sem("k_sq"), j + 1)
                v.tensor_copy(kf[:, j, :], bank[3 + j % 2][:, 0:NB * L]).then_inc(sem("k_copied"), 1)
                dve.wait_ge(sem("k_ssq"), j + 1)
                v.tensor_scalar(ksq[:, j, :], bank[5][:, 0:NB * L], 1.0 / DH, RMS_EPS, ALU.mult, ALU.add).then_inc(
                    sem("k_ms"), 1)
            def stats(o, i):
                link(v.bn_stats(st6[:, o.n, :], X[:, i, :]))
                if i >= 2:
                    dve.wait_ge(o.full, i - 1)
                link(v.bn_aggr(mv[:, o.n, i % 2, :], st6[:, o.n, :]))
                v.tensor_scalar_add(mv[:, o.n, i % 2, 1:2], mv[:, o.n, i % 2, 1:2], LN_EPS).then_inc(o.var, 1)

            dve.wait_ge(sem("x_loaded0"), 16)
            stats(ln0, 0)
            kv = pb[1][:, 0:NP * NB * L]
            half_n = NP * NB * L // 2
            y, t = k_tmp[:, 0, :], k_tmp[:, 1, :]
            dve.wait_ge(sem("k_ms"), NP)
            for part in range(2):
                kp = kv[:, part * half_n:(part + 1) * half_n]
                link(v.tensor_scalar(y.bitcast(I32), kp.bitcast(I32), -0.5, float(RSQRT_SEED), ALU.mult, ALU.add))
                for n in range(3):
                    link(v.tensor_tensor(t, y, y, ALU.mult))
                    link(v.scalar_tensor_tensor(out=t, in0=t, scalar=-0.5, in1=kp, op0=ALU.mult, op1=ALU.mult))
                    link(v.scalar_tensor_tensor(out=y if n < 2 else kp, in0=t, scalar=1.5, in1=y, op0=ALU.add,
                                                op1=ALU.mult))
            v.scalar_tensor_tensor(out=pb[0][:, 0:NS], in0=pb[0][:, 0:NS], scalar=sks[:, 3:4], in1=kv,
                                   op0=ALU.mult, op1=ALU.mult).then_inc(sem("k_normed"), 1)
            for b in range(NB):
                dve.wait_ge(sem("mean_done"), b + 1)
                dve.wait_ge(sem("cb_loaded"), 32)
                v.tensor_tensor(cb_s[:, b, :], bank[3 + b][:, 0:D], cb_s[:, b, :], ALU.add).then_inc(
                    sem("ctx_bias_ready"), 1)
                dve.wait_ge(sem("ctx_bias_ready"), b + 1)
                link(v.tensor_scalar(ctx_bias[:, b, 0, :], cb_s[:, b, :], WS, None, ALU.mult))
                link(v.scalar_tensor_tensor(out=ctx_bias[:, b, 1, :], in0=cb_s[:, b, :], scalar=WS,
                                            in1=ctx_bias[:, b, 0, :], op0=ALU.mult, op1=ALU.subtract))

            def k_lo():
                for h in range(2):
                    dve.wait_ge(sem("kb_hi"), h + 1)
                    rows = slice(h * DH, (h + 1) * DH)
                    v.tensor_tensor(kbl[rows, :, :, h, :], kf[rows].rearrange("p j (b k) -> p j b k", b=NB),
                                    kbh[rows, :, :, h, :], ALU.subtract).then_inc(sem("kb_ready"), 1)

            def split_lo(k):
                dve.wait_ge(sem("chunk_hi1"), k // 2 + 1)
                v.scalar_tensor_tensor(out=chunks[k][2], in0=staged(k), scalar=WS, in1=chunks[k][1],
                                       op0=ALU.mult, op1=ALU.subtract).then_inc(sem("chunk_lo1"), 1)

            def norm_lo(o, i):
                dve.wait_ge(o.hi, i + 1)
                r = o.rows[:, i % 2, :]
                v.tensor_tensor(r[:, D:2 * D], o.full32[:, i % 2, :], r[:, 0:D], ALU.subtract).then_inc(o.lo, 1)

            def q_ms(i):
                dve.wait_ge(sem("ssq_done"), i + 1)
                if i >= 6:
                    dve.wait_ge(sem("logits_done0"), i - 5)
                if i >= 2:
                    dve.wait_ge(sem("scores_scaled"), i - 1)
                v.tensor_scalar(rq[:, i % 2, :], SSQ, 1.0 / DH, RMS_EPS, ALU.mult, ALU.add).then_inc(sem("q_ms"), 1)

            def shift(i):
                dve.wait_ge(sem("scores_done"), i + 1)
                full = score_banks[:, 0:FULL, :, :]
                last = score_banks[:, FULL, 0:NH - FULL * 6, :]
                v.tensor_reduce(mxs[:, 0:FULL * 6].rearrange("p (b h) -> p b h", b=FULL), full, axis=AX.X, op=ALU.max)
                link(v.tensor_reduce(mxs[:, LAST], last, axis=AX.X, op=ALU.max))
                if i == 0:
                    dve.wait_ge(sem("kb_ready"), 2)
                if i >= 3:
                    dve.wait_ge(sem("weights_tr"), NG * (i - 2))
                row = pb[i % 3][:, 0:NS].rearrange("p (h k) -> p h k", k=L)
                v.tensor_tensor(row[:, 0:FULL * 6, :].rearrange("p (b h) k -> p b h k", b=FULL), full,
                                mxs[:, 0:FULL * 6].rearrange("p (b h) -> p b h", b=FULL)[:, :, :, None].to_broadcast(
                                    [P, FULL, 6, L]), ALU.subtract)
                v.tensor_tensor(row[:, LAST, :], last, mxs[:, LAST][:, :, None].to_broadcast([P, NH - FULL * 6, L]),
                                ALU.subtract).then_inc(sem("scores_shifted"), 1)

            def sums(i):
                dve.wait_ge(sem("exp_done"), i + 1)
                if i >= 1:
                    dve.wait_ge(sem("weights_ready"), i)
                link(v.tensor_reduce(rs[:, :], pb[i % 3][:, 0:NS].rearrange("p (h k) -> p h k", k=L), axis=AX.X,
                                     op=ALU.add))
                link(v.reciprocal(rs[:, :], rs[:, :]))
                v.tensor_scalar(rs[:, :], rs[:, :], PS, None, ALU.mult).then_inc(sem("row_sums"), 1)

            def pt_lo(i, n):
                a, b = groups[n]
                dve.wait_ge(sem("pt_hi"), NG * i + n + 1)
                v.tensor_tensor(ptl[:, a:b, :], bank[6 + (NG * i + n) % 2][:, 0:(b - a) * P].rearrange(
                    "p (c t) -> p c t", t=P), pth[:, a:b, :], ALU.subtract).then_inc(sem("pt_lo"), 1)

            def q_lo(i):
                dve.wait_ge(sem("q_sq"), i + 1)
                v.tensor_tensor(ql, q_ps, qh, ALU.subtract).then_inc(sem("q_lo"), 1)

            def add_attn(i):
                dve.wait_ge(sem("attn_done"), i + 1)
                dve.wait_ge(ln0.full, i + 1)
                v.scalar_tensor_tensor(out=X[:, i, :], in0=o_ps, scalar=1.0 / (WS * PS), in1=X[:, i, :],
                                       op0=ALU.mult, op1=ALU.add).then_inc(sem("attn_added"), 1)
                dve.wait_ge(sem("attn_added"), i + 1)

            def logits(layer, i):
                dve.wait_ge(sem(f"logits_done{layer}"), i + 1)
                if layer == 0:
                    v.tensor_scalar(lg[:, i, :], LOG, 1.0 / WS, None, ALU.mult).then_inc(sem("logits_read0"), 1)
                else:
                    if i == 0:
                        dve.wait_ge(sem("rb_loaded"), 16)
                    v.scalar_tensor_tensor(out=lg[:, i, :], in0=LOG, scalar=1.0 / WS, in1=rbb[:, :],
                                           op0=ALU.mult, op1=ALU.add).then_inc(sem("logits_read1"), 1)

            for s in range(NT + 9):
                if 0 <= s - 6 < NT:
                    add_attn(s - 6)
                if 0 <= s - 2 < NT:
                    q_lo(s - 2)
                if 1 <= s < NT:
                    if s % (NT // 4) == 0:
                        dve.wait_ge(sem(f"x_loaded{s // (NT // 4)}"), 16)
                    stats(ln0, s)
                if 0 <= s - 6 < NT:
                    stats(ln1, s - 6)
                if 0 <= s - 5 < NT:
                    pt_lo(s - 5, 0)
                    pt_lo(s - 5, 1)
                if 0 <= s - 4 < NT:
                    sums(s - 4)
                if 0 <= s - 5 < NT:
                    pt_lo(s - 5, 2)
                if 0 <= s - 2 < NT:
                    q_ms(s - 2)
                if 0 <= s - 8 < NT:
                    logits(0, s - 8)
                if 0 <= s - 2 < NT:
                    shift(s - 2)
                if s == 0:
                    split_lo(1)
                if s < NT:
                    norm_lo(ln0, s)
                if 0 <= s - 6 < NT:
                    norm_lo(ln1, s - 6)
                if s == 1:
                    k_lo()
                if s == 3:
                    split_lo(3)
                if 0 <= s - 6 < NT and (PRE + s - 6) % 2:
                    split_lo(PRE + s - 6)

            def route(layer):
                r = routes[layer]

                def cut(n):
                    return r[:, n * P:n * P + NT * E]

                def te(a):
                    return a.rearrange("p (t e) -> p t e", e=E)

                def et(a):
                    return a.rearrange("p (e t) -> p e t", e=E)

                ex, m1, m2, best = cut(0), r[:, 1024:1024 + NT], r[:, 1152:1152 + NT], r[:, 1088:1088 + NT]
                oh = [cut(1), cut(2)]
                cand, masked, hot, tot = cut(3), cut(4), cut(5), cut(6)
                counts = r[:, 1216:1216 + 64]
                dve.wait_ge(sem(f"logits_read{layer}"), NT)
                if layer == 0:
                    dve.wait_ge(sem("consts_ready"), 1)
                cur = lg[:, :, :]
                f8 = first8[:, None, :].to_broadcast([P, NT, E])
                for c, m in enumerate((m1, m2)):
                    link(v.tensor_reduce(m, cur, axis=AX.X, op=ALU.max))
                    link(v.tensor_tensor(te(cand), cur, m[:, :, None].to_broadcast([P, NT, E]), ALU.is_equal))
                    link(v.tensor_tensor(te(cand), te(cand), f8, ALU.mult))
                    link(v.tensor_reduce(best, te(cand), axis=AX.X, op=ALU.max))
                    link(v.tensor_tensor(te(oh[c]), f8, best[:, :, None].to_broadcast([P, NT, E]), ALU.is_equal))
                    if c == 0:
                        link(v.scalar_tensor_tensor(out=te(masked), in0=te(oh[0]), scalar=NEG, in1=cur,
                                                    op0=ALU.mult, op1=ALU.add))
                        cur = te(masked)
                v.tensor_tensor(hot, oh[0], oh[1], ALU.add).then_inc(sem("hot"), 1)
                link(v.tensor_tensor(te(ex), lg[:, :, :], m1[:, :, None].to_broadcast([P, NT, E]), ALU.subtract))
                v.tensor_tensor(m2, m2, m1, ALU.subtract).then_inc(sem("route_shift"), 1)
                dve.wait_ge(sem("counts_done"), layer + 1)
                link(v.tensor_copy(et(tot), bank[7][:, 128:128 + NT * E].rearrange("p (t e) -> p e t", e=E)))
                incl = cand
                link(v.tensor_tensor_scan(incl, ones[:, 0:NT * E], tot, 0.0, ALU.mult, ALU.add))
                ends = et(incl)[:, :, NT - 1]
                start, cnt, tiles, tend, base = (counts[:, 8 * k:8 * k + 8] for k in range(5))
                link(v.memset(start[:, 0:1], 0.0))
                link(v.tensor_copy(start[:, 1:E], ends[:, 0:E - 1]))
                link(v.tensor_tensor(cnt, ends, start, ALU.subtract))
                ci = counts[:, 40:48].bitcast(I32)
                link(v.tensor_scalar(ci, cnt, float(SW - 1), None, ALU.add))
                link(v.tensor_scalar(ci, ci, SW.bit_length() - 1, None, ALU.logical_shift_right))
                link(v.tensor_copy(tiles, ci))
                link(v.tensor_tensor_scan(tend, ones[:, 0:E], tiles, 0.0, ALU.mult, ALU.add))
                link(v.tensor_tensor(base, tend, tiles, ALU.subtract))
                link(v.scalar_tensor_tensor(out=base, in0=base, scalar=float(SW), in1=start, op0=ALU.mult,
                                            op1=ALU.subtract))
                link(v.tensor_tensor(masked, incl, tot, ALU.subtract))
                link(v.tensor_tensor(et(masked), et(masked), base[:, :, None].to_broadcast([P, E, NT]), ALU.add))
                pos = cand
                link(v.tensor_tensor(te(pos), bank[7][:, 256:256 + NT * E].rearrange("p (t e) -> p t e", e=E),
                                     masked.rearrange("p (e t) -> p t e", e=E), ALU.add))
                both = r[:, P:3 * P].rearrange("p (c n) -> p c n", c=2)
                link(v.tensor_tensor(both, both, pos[:, None, :].to_broadcast([P, 2, NT * E]), ALU.mult))
                link(v.tensor_reduce(hot[:, 0:2 * NT].rearrange("p (c t) -> p c t", c=2),
                                     both.rearrange("p c (t e) -> p c t e", e=E), axis=AX.X, op=ALU.add))
                link(v.tensor_copy(slots[:, :, :], hot[:, 0:2 * NT].rearrange("p (c t) -> p t c", c=2)))
                rr, qq = (r[:, k:k + 2 * NT] for k in (1280, 1312))
                sv = slots[:, :, :].rearrange("p t c -> p (t c)")
                link(v.tensor_scalar(hot[:, 0:2 * NT].bitcast(U32), sv, P - 1, None, ALU.bitwise_and))
                link(v.tensor_scalar(tot[:, 0:2 * NT].bitcast(U32), sv, P.bit_length() - 1, None, ALU.logical_shift_right))
                link(v.tensor_copy(rr, hot[:, 0:2 * NT].bitcast(U32)))
                link(v.tensor_copy(qq, tot[:, 0:2 * NT].bitcast(U32)))
                at_q = r[:, 128:128 + NT * NQ].bitcast(F16).rearrange("p (n q) -> p n q", q=NQ)
                v.tensor_tensor(at_q, iota_r[:, None, 0:NQ].to_broadcast([P, 2 * NT, NQ]),
                                qq[:, :, None].to_broadcast([P, 2 * NT, NQ]), ALU.is_equal).then_inc(sem("tiles_hot"), 1)
                for half in range(2):
                    n = slice(half * NT, (half + 1) * NT)
                    v.tensor_tensor(onehots[layer][:, n, :], iota_r[:, None, :].to_broadcast([P, NT, P]),
                                    rr[:, n, None].to_broadcast([P, NT, P]), ALU.is_equal).then_inc(sem("rows_hot"), 1)
                ge_e = r[:, 1376:1376 + NSLOT * (E - 1)].rearrange("p (s e) -> p s e", e=E - 1)
                link(v.tensor_tensor(ge_e, iota_r[:, 0:NSLOT, None].to_broadcast([P, NSLOT, E - 1]),
                                     tend[:, None, 0:E - 1].to_broadcast([P, NSLOT, E - 1]), ALU.is_ge))
                es = r[:, 1540:1540 + NSLOT]
                link(v.tensor_reduce(es, ge_e, axis=AX.X, op=ALU.add))
                link(v.tensor_copy(expert[:, 0, :], es))
                link(v.tensor_scalar(expert[:, 1, :], es, float(2 * DC * moes[layer].H), None, ALU.mult))
                dve.wait_ge(sem("tokens_done"), layer + 1)
                sign, which = (r[:, k:k + NQ] for k in (1344, 1408))
                link(v.tensor_scalar(sign, bank[6][:, 0:NQ], 0.0, -2.0, ALU.is_lt, ALU.mult))
                link(v.scalar_tensor_tensor(out=which, in0=sign, scalar=1.0, in1=bank[6][:, 0:NQ], op0=ALU.add,
                                            op1=ALU.mult))
                v.tensor_scalar(index[:, :], which, -1.0, 0.0, ALU.add, ALU.max).then_inc(sem("routed"), 1)
                if layer == 1:
                    dve.wait_ge(sem("behind_ready"), 1)
                    link(v.scalar_tensor_tensor(out=sign, in0=sign, scalar=-0.5 * (T + 1), in1=which, op0=ALU.mult,
                                                op1=ALU.add))
                    link(v.scalar_tensor_tensor(out=which, in0=which, scalar=0.0, in1=behind, op0=ALU.is_equal,
                                                op1=ALU.mult))
                    v.tensor_tensor(back, sign, which, ALU.add).then_inc(sem("back_ready"), 1)
                dve.wait_ge(sem("route_exp"), 2 * layer + 2)
                link(v.tensor_reduce(best, te(ex), axis=AX.X, op=ALU.add))
                link(v.reciprocal(gates[:, 0, :], best))
                v.tensor_tensor(gates[:, 1, :], gates[:, 0, :], m2, ALU.mult).then_inc(sem("gates_ready"), 1)
                dve.wait_ge(sem("gates_ready"), layer + 1)

            def slot_cols(layer, j):
                m = moes[layer]
                dve.wait_ge(sem(f"slot_tr{layer}"), j + 1)
                if j >= 2:
                    dve.wait_ge(sem(f"slot_h{layer}"), m.PARTS * (j - 1))
                v.tensor_copy(m.xT[:, j % 2], bank[7 * (j % 2)].bitcast(F16).rearrange("p (c t) -> p c t", t=SW)).then_inc(
                    sem(f"slot_cols{layer}"), 1)

            def slot_bias(layer, j, a):
                m = moes[layer]
                u = m.PARTS * j + a
                if a == 0:
                    expert_of[j] = dve.value_load(expert[0:1, 0, j:j + 1], min_val=0, max_val=E - 1)
                dve.wait_ge(sem(f"slot_h{layer}"), u + 1)
                if u >= 2:
                    dve.wait_ge(sem(f"h_lo{layer}"), u - 1)
                bias = m.b[:, bass.ds(expert_of[j] * m.HC + a * m.HH, m.HH)]
                v.scalar_tensor_tensor(out=m.g[:, u % 2], in0=hidden(m, u), scalar=1.0 / WS,
                                       in1=bias[:, :, None].to_broadcast([P, m.HH, SW]),
                                       op0=ALU.mult, op1=ALU.add).then_inc(sem(f"h_biased{layer}"), 1)

            def slot_lo(layer, j, a):
                m = moes[layer]
                u = m.PARTS * j + a
                dve.wait_ge(sem(f"h_hi{layer}"), u + 1)
                c = slice(a * m.HH, (a + 1) * m.HH)
                v.tensor_tensor(m.hl[:, j % 2, c, :], m.g[:, u % 2], m.hh[:, j % 2, c, :], ALU.subtract).then_inc(
                    sem(f"h_lo{layer}"), 1)

            def slot_out(layer, j):
                m = moes[layer]
                dve.wait_ge(sem(f"slot_y{layer}"), j + 1)
                if j >= 2:
                    dve.wait_ge(sem(f"y_kept{layer}_{j % 2}"), 16 * (1 + layer) * (j // 2))
                b2 = m.b2[:, bass.ds(expert_of[j] * D, D)]
                v.scalar_tensor_tensor(out=m.y[:, j % 2], in0=PSUM[:, 5:7, 0:D], scalar=1.0 / WS,
                                       in1=b2[:, None, :].to_broadcast([P, 2, D]),
                                       op0=ALU.mult, op1=ALU.add).then_inc(sem(f"y_ready{layer}"), 1)

            expert_of = {}

            def slots_of(layer):
                dve.wait_ge(sem("b_in0_loaded" if layer == 0 else "b1_loaded"), 16)
                dve.wait_ge(sem(f"b2_loaded{layer}"), 16)
                m = moes[layer]
                for s in range(NSLOT + m.LAG + 2):
                    if 0 <= s - m.LAG - 2 < NSLOT:
                        slot_out(layer, s - m.LAG - 2)
                    if s < NSLOT:
                        slot_cols(layer, s)
                    for a in range(m.PARTS):
                        if 0 <= s - 1 < NSLOT:
                            slot_bias(layer, s - 1, a)
                    for a in range(m.PARTS):
                        if 0 <= s - m.LAG < NSLOT:
                            slot_lo(layer, s - m.LAG, a)
                    k = PRE + A_CH + s
                    if layer == 0 and k < NCH - LATE and k % 2:
                        split_lo(k)

            def combine(layer, i, ring):
                n = ring.shape[1]
                dve.wait_ge(sem(f"y_gathered{layer}_{i % n}"), 32 * (i // n + 1))
                for c in range(2):
                    if c:
                        dve.wait_ge(sem(f"y_used{layer}"), 2 * i + 1)
                    v.scalar_tensor_tensor(out=X[:, i, :], in0=ring[:, i % n, c, :], scalar=gates[:, c, i:i + 1],
                                           in1=X[:, i, :], op0=ALU.mult, op1=ALU.add).then_inc(sem(f"y_used{layer}"), 1)
                dve.wait_ge(sem(f"y_used{layer}"), 2 * i + 2)

            def add_linear(i):
                dve.wait_ge(ln2.full, i + 1)
                dve.wait_ge(sem("linear_done"), i + 1)
                v.scalar_tensor_tensor(out=X[:, i, :], in0=c_ps, scalar=1.0 / WS, in1=X[:, i, :],
                                       op0=ALU.mult, op1=ALU.add).then_inc(sem("linear_added"), 1)
                dve.wait_ge(sem("linear_added"), i + 1)

            route(0)
            slots_of(0)
            for s in range(NT + 8):
                if 0 <= s - 8 < NT:
                    logits(1, s - 8)
                if 0 <= s - 3 < NT:
                    norm_lo(ln2, s - 3)
                if 0 <= s - 2 < NT:
                    combine(0, s - 2, yg)
                    stats(ln2, s - 2)
                if 0 <= s - 6 < NT:
                    norm_lo(ln3, s - 6)
                if 0 <= s - 4 < NT:
                    add_linear(s - 4)
                if 0 <= s - 5 < NT:
                    stats(ln3, s - 5)
                if 0 <= s - 2 < LATE and (NCH - LATE + s) % 2:
                    split_lo(NCH - LATE + s - 2)
            route(1)
            slots_of(1)
            for i in range(NT):
                combine(1, i, yg1)

        @block.tensor
        def _(pe):
            t = nc.tensor

            def mm(o, a, b, start, stop):
                return t.matmul(o, a, b, start=start, stop=stop)

            def three(o, ah, al, bh, bl, first, last):
                mm(o, ah, bh, first, False)
                mm(o, ah, bl, False, False)
                return mm(o, al, bh, False, last)

            pe.wait_ge(sem("ctx_loaded"), 16)
            pe.wait_ge(sem("wk_loaded"), 16)
            pe.wait_ge(sem("heads_ready"), 1)
            for s in range(NP + 1):
                if s < NP:
                    if s >= 2:
                        pe.wait_ge(sem("k_copied"), s - 1)
                    for dc in range(DC):
                        last = mm(bank[3 + s % 2][:, 0:NB * L], wk_s[:, dc, s * P:(s + 1) * P], ctx_s[:, dc, :],
                                  dc == 0, dc == DC - 1)
                    last.then_inc(sem("k_done"), 1)
                if s >= 1:
                    pe.wait_ge(sem("k_sq"), s)
                    if s >= 2:
                        pe.wait_ge(sem("k_ms"), s - 1)
                    mm(bank[5][:, 0:NB * L], heads2, ksq[:, s - 1, :], True, True).then_inc(sem("k_ssq"), 1)
            pe.wait_ge(sem("wv_loaded"), 16)
            for j in range(NP):
                if j >= 2:
                    pe.wait_ge(sem("vt_copied"), 2 * (j - 1))
                for dc in range(DC):
                    last = mm(bank[1 + j % 2][:, 0:NB * L], wv_s[:, dc, j * P:(j + 1) * P], ctx_s[:, dc, :],
                              dc == 0, dc == DC - 1)
                last.then_inc(sem("vt_done"), 1)
            pe.wait_ge(sem("mean_ready"), 1)
            pe.wait_ge(sem("cw2_loaded"), 16)
            pe.wait_ge(sem("k_copied"), NP)
            for b in range(NB):
                for dc in range(DC):
                    last = mm(bank[3 + b][:, 0:D], cmb[:, dc, b, :], cw2[:, dc, :], dc == 0, dc == DC - 1)
                last.then_inc(sem("mean_done"), 1)
            pe.wait_ge(sem("wo_loaded"), 16)
            pe.wait_ge(sem("vt_copied"), NH)
            pe.wait_ge(sem("consts_ready"), 1)

            def v_wo(n):
                b, c = divmod(n, KC)
                if n >= 2:
                    pe.wait_ge(sem("vw_ready"), n - 1)
                js = [j for j in range(NP) if -P < P * c - PW * j < PW]
                for j in js:
                    o = P + P * c - PW * j
                    last = mm(bank[6 + n % 2][:, 0:D], zt[:, j, b, o:o + P], wo_s[:, j, :],
                              j == js[0], j == js[-1] and c < KC - 1)
                if c == KC - 1:
                    pe.wait_ge(sem("bo_loaded"), 16)
                    last = mm(bank[6 + n % 2][:, 0:D], ident_f, bo_row, False, True)
                last.then_inc(sem("vw_done"), 1)

            def transposed(o, i):
                pe.wait_ge(o.lo, i + 1)
                if i >= 1:
                    pe.wait_ge(o.cols, i)
                for c in range(2 * DC):
                    last = t.transpose(o.ps[:, c, :], o.rows[:, i % 2, c * P:(c + 1) * P], ident_h[:, :])
                last.then_inc(o.tr, 1)

            def q_proj(i):
                pe.wait_ge(ln0.cols, i + 1)
                if i == 0:
                    pe.wait_ge(sem("chunk_lo0"), 1)
                    pe.wait_ge(sem("chunk_lo1"), 1)
                if i >= 1:
                    pe.wait_ge(sem("q_lo"), i)
                xT = ln0.xT[:, i % 2]
                for j in range(NP):
                    w = slice(j * P, (j + 1) * P)
                    for dc in range(DC):
                        last = three(q_ps[:, j, :], wq_h[:, dc, w], wq_l[:, dc, w], xT[:, dc, :], xT[:, DC + dc, :],
                                     dc == 0, dc == DC - 1)
                last.then_inc(sem("q_done"), 1)

            def scores(i):
                pe.wait_ge(sem("q_lo"), i + 1)
                if i == 0:
                    pe.wait_ge(sem("kb_ready"), 2)
                    pe.wait_ge(sem("ctx_bias_ready"), NB)
                if i >= 1:
                    pe.wait_ge(sem("scores_shifted"), i)
                if i >= 7:
                    pe.wait_ge(sem("logits_read0"), i - 6)
                b = i // (NT // NB)
                for j in range(NP):
                    kh = kbh[:, j, b].rearrange("p a k -> p (a k)")
                    kl = kbl[:, j, b].rearrange("p a k -> p (a k)")
                    last = three(bank[3 + j // 3][:, PW * (j % 3):PW * (j % 3 + 1)], qh[:, j, :], ql[:, j, :], kh, kl,
                                 True, True)
                last.then_inc(sem("scores_done"), 1)

            def q_squares(i):
                pe.wait_ge(sem("q_sq"), i + 1)
                for j in range(NP):
                    last = mm(SSQ[:, 2 * j:2 * j + 2], qsq[:, j, :], heads2[:, 0:DH + 1:DH], True, True)
                last.then_inc(sem("ssq_done"), 1)

            def weights_t(i, n):
                if n == 0:
                    pe.wait_ge(sem("weights_ready"), i + 1)
                if i == 0 and n == 0:
                    pe.wait_ge(sem("vw_ready"), NB * KC)
                if NG * i + n >= 2:
                    pe.wait_ge(sem("pt_lo"), NG * i + n - 1)
                a, b = groups[n]
                for c in range(a, b):
                    last = t.transpose(bank[6 + (NG * i + n) % 2][:, (c - a) * P:(c - a + 1) * P],
                                       pb[i % 3][:, c * P:(c + 1) * P], ident_f)
                last.then_inc(sem("weights_tr"), 1)

            def attn(i):
                pe.wait_ge(sem("pt_lo"), NG * (i + 1))
                pe.wait_ge(ln0.cols, min(NT, i + 5))
                if i >= 2:
                    pe.wait_ge(ln1.cols, i - 1)
                if i >= 1:
                    pe.wait_ge(sem("attn_added"), i)
                b = i // (NT // NB)
                for c in range(KC):
                    last = three(o_ps, pth[:, c, :], ptl[:, c, :], vw[:, b, c, 0, :], vw[:, b, c, 1, :],
                                 c == 0, c == KC - 1)
                last.then_inc(sem("attn_done"), 1)

            def logits(layer, o, i):
                pe.wait_ge(o.cols, i + 1)
                if i == 0:
                    pe.wait_ge(sem("chunk_lo0"), PRE // 2)
                    pe.wait_ge(sem("chunk_lo1"), PRE // 2)
                if i >= 1:
                    pe.wait_ge(sem(f"logits_read{layer}"), i)
                if layer == 0:
                    pe.wait_ge(sem("scores_shifted"), min(NT, i + 6))
                for dc in range(DC):
                    last = three(LOG, o.xT[:, i % 2, dc, :], o.xT[:, i % 2, DC + dc, :], rws[:, 0, layer, dc, :],
                                 rws[:, 1, layer, dc, :], dc == 0, dc == DC - 1)
                last.then_inc(sem(f"logits_done{layer}"), 1)

            for n in range(VW_FIRST):
                v_wo(n)
            for s in range(NT + 9):
                if 0 <= s - 5 < NT:
                    weights_t(s - 5, 0)
                    weights_t(s - 5, 1)
                if 0 <= s - 1 < NT:
                    if s - 1 >= 5:
                        pe.wait_ge(sem("attn_added"), s - 5)
                    if s - 1 >= 7:
                        pe.wait_ge(ln1.cols, s - 7)
                    transposed(ln0, s - 1)
                if 0 <= s - 7 < NT:
                    pe.wait_ge(sem("attn_added"), min(NT, s - 5))
                    if s - 1 >= NT:
                        pe.wait_ge(ln0.cols, NT)
                    transposed(ln1, s - 7)
                if 0 <= s - 2 < NT:
                    scores(s - 2)
                if 0 <= s - 5 < NT:
                    weights_t(s - 5, 2)
                if 0 <= s - 2 < NT:
                    q_squares(s - 2)
                if 0 <= s - 8 < NT:
                    logits(0, ln1, s - 8)
                for n in range(VW_FIRST + VW_STEP * s, min(NB * KC, VW_FIRST + VW_STEP * (s + 1))):
                    v_wo(n)
                if 0 <= s - 1 < NT:
                    q_proj(s - 1)
                if 0 <= s - 5 < NT:
                    attn(s - 5)

            def route(layer):
                r = routes[layer]
                hot = r[:, 5 * P:5 * P + NT * E]
                pe.wait_ge(sem("hot"), layer + 1)
                if layer == 0:
                    pe.wait_ge(sem("pt_lo"), NG * NT)
                mm(bank[7][:, 128:128 + NT * E], ones[:, :], hot, True, True)
                mm(bank[7][:, 256:256 + NT * E], before[:, :], hot, True, True).then_inc(sem("counts_done"), 1)
                at_q = r[:, 128:128 + NT * NQ].bitcast(F16).rearrange("p (n q) -> p n q", q=NQ)
                pe.wait_ge(sem("places"), layer + 1)
                for n in range(2 * NT):
                    if n % NT == 0:
                        pe.wait_ge(sem("rows_hot"), 2 * layer + n // NT + 1)
                    last = mm(bank[6][:, 0:NQ], onehots[layer][:, n, :], at_q[:, n, :], n == 0, n == 2 * NT - 1)
                last.then_inc(sem("tokens_done"), 1)

            weights_at = {}

            def slot_tr(layer, j):
                m = moes[layer]
                pe.wait_ge(sem(f"rows_gathered{layer}_{j % RING}"), 32 * (j // RING + 1))
                if j >= 2:
                    pe.wait_ge(sem(f"slot_cols{layer}"), j - 1)
                cols = bank[7 * (j % 2)].bitcast(F16).rearrange("p (c t) -> p c t", t=SW)
                for a in range(2):
                    for c in range(2 * DC):
                        last = t.transpose(cols[:, c, a * P:(a + 1) * P], m.rows[:, j % RING, a, c * P:(c + 1) * P],
                                           ident_h[:, :])
                last.then_inc(sem(f"slot_tr{layer}"), 1)

            def slot_up(layer, j):
                m = moes[layer]
                per = DC * m.H
                e = weights_at[j]
                pe.wait_ge(sem(f"slot_cols{layer}"), j + 1)
                xT = m.xT[:, j % 2]
                for a in range(m.PARTS):
                    u = m.PARTS * j + a
                    if u >= 2:
                        pe.wait_ge(sem(f"h_biased{layer}"), u - 1)
                    ps = hidden(m, u)
                    for hc in range(m.HH):
                        for dc in range(DC):
                            o = dc * m.H + (a * m.HH + hc) * P
                            last = three(ps[:, hc, :], m.wa[:, bass.ds(e + o, P)], m.wa[:, bass.ds(e + (per + o), P)],
                                         xT[:, dc, :], xT[:, DC + dc, :], dc == 0, dc == DC - 1)
                    last.then_inc(sem(f"slot_h{layer}"), 1)

            def slot_down(layer, j):
                m = moes[layer]
                per = DC * m.H
                e = weights_at[j]
                pe.wait_ge(sem(f"h_lo{layer}"), m.PARTS * (j + 1))
                if j >= 1:
                    pe.wait_ge(sem(f"y_ready{layer}"), j)
                for hc in range(m.HC):
                    wh = m.wb[:, bass.ds(e + hc * D, D)]
                    wl = m.wb[:, bass.ds(e + (per + hc * D), D)]
                    for a in range(2):
                        c = slice(a * P, (a + 1) * P)
                        last = three(bank[5 + a][:, 0:D], m.hh[:, j % 2, hc, c], m.hl[:, j % 2, hc, c], wh, wl,
                                     hc == 0, hc == m.HC - 1)
                last.then_inc(sem(f"slot_y{layer}"), 1)

            def slots_of(layer):
                m = moes[layer]
                pe.wait_ge(sem("routed"), layer + 1)
                n = B_CH if layer == 0 else NCH
                pe.wait_ge(sem("chunk_lo0"), n // 2)
                pe.wait_ge(sem("chunk_lo1"), n // 2)
                for s in range(NSLOT + m.LAG + 1):
                    if s < NSLOT:
                        weights_at[s] = pe.value_load(expert[0:1, 1, s:s + 1], min_val=0, max_val=(E - 1) * 2 * DC * m.H)
                        slot_tr(layer, s)
                    if 0 <= s - 1 < NSLOT:
                        slot_up(layer, s - 1)
                    if 0 <= s - m.LAG - 1 < NSLOT:
                        slot_down(layer, s - m.LAG - 1)

            def linear(i):
                pe.wait_ge(ln2.cols, i + 1)
                if i >= 1:
                    pe.wait_ge(sem("linear_added"), i)
                xT = ln2.xT[:, i % 2]
                for dc in range(DC):
                    three(c_ps, xT[:, dc, :], xT[:, DC + dc, :], wc[:, 0, dc, :], wc[:, 1, dc, :], dc == 0, False)
                for n in range(2):
                    last = mm(c_ps, ident_h[:, :], ctx_bias[:, i // (NT // NB), n, :], False, n == 1)
                last.then_inc(sem("linear_done"), 1)

            route(0)
            slots_of(0)
            for s in range(NT + 8):
                if 0 <= s - 3 < NT:
                    transposed(ln2, s - 3)
                    linear(s - 3)
                if 0 <= s - 6 < NT:
                    transposed(ln3, s - 6)
                if 0 <= s - 7 < NT:
                    logits(1, ln3, s - 7)
            route(1)
            slots_of(1)


def kernel(**inputs):
    import numpy as np
    import concourse.bacc as bacc
    from concourse.bass_utils import run_bass_kernel_spmd

    a = {k: np.asarray(v) for k, v in inputs.items()}
    D = a["x"].shape[-1]
    P_ = 128
    E = a["L0_ffn_b_in"].shape[0]

    def per_part(b):
        return b.reshape(E, -1, P_).transpose(2, 0, 1).reshape(P_, -1)

    arrays = {
        "x": a["x"].reshape(-1, D),
        "ctx_t": a["ctx_1024"].reshape(-1, D).T,
        "wq": a["L0_xattn_Wq"].reshape(D, -1),
        "wk": a["L0_xattn_Wk"].reshape(D, -1),
        "wv": a["L0_xattn_Wv"].reshape(D, -1),
        "scale_q": a["L0_xattn_scale_q"],
        "scale_k": a["L0_xattn_scale_k"],
        "wo": a["L0_xattn_Wo"].reshape(-1, D),
        "bo": a["L0_xattn_bo"],
        "rw0": a["L0_ffn_router_w"],
        "w_in0": a["L0_ffn_w_in"],
        "b_in0": per_part(a["L0_ffn_b_in"]),
        "w_out0": a["L0_ffn_w_out"],
        "b_out0": a["L0_ffn_b_out"].reshape(-1),
        "cw1_t": a["L1_xattn_W"][:, :D].T,
        "cw2_t": a["L1_xattn_W"][:, D:].T,
        "cb": a["L1_xattn_b"],
        "rw1_t": a["L1_ffn_router_w"].T,
        "rb1": a["L1_ffn_router_b"],
        "w1_t": a["L1_ffn_w1"].transpose(0, 2, 1),
        "b1": per_part(a["L1_ffn_b1"]),
        "w2_t": a["L1_ffn_w2"].transpose(0, 2, 1),
        "b2": a["L1_ffn_b2"].reshape(-1),
    }
    arrays = {k: np.ascontiguousarray(v) for k, v in arrays.items()}
    nc = bacc.Bacc("TRN2", target_bir_lowering=False, num_devices=1)
    args = [nc.dram_tensor(k, v.shape, mybir.dt.from_np(v.dtype), kind="ExternalInput").ap() for k, v in arrays.items()]
    out = nc.dram_tensor("out", arrays["x"].shape, F32, kind="ExternalOutput").ap()
    build(nc, *args, out)
    r = run_bass_kernel_spmd(nc, [arrays], core_ids=[0])
    return r.results[0]["out"].reshape(a["x"].shape)
```

```python
import math
from contextlib import ExitStack

import concourse.bass as bass
from concourse import mybir

F32, F16, I32, U32 = mybir.dt.float32, mybir.dt.float16, mybir.dt.int32, mybir.dt.uint32
ALU = mybir.AluOpType
ACT = mybir.ActivationFunctionType
AX = mybir.AxisListType

P = 128
RSQRT_SEED = 0x5F3759DF


def product(shape):
    r = 1
    for n in shape:
        r *= n
    return r


def carve(region, at, shape, dt):
    size = 2 if dt == F16 else 4
    end = at + product(shape) * size
    v = region[:, at // 4:(end + 3) // 4]
    if dt != F32:
        v = v.bitcast(dt)
    if len(shape) > 1:
        names = [f"d{n}" for n in range(len(shape))]
        v = v.rearrange(f"p ({' '.join(names)}) -> p {' '.join(names)}", **dict(zip(names[1:], shape[1:])))
    return v, end


class LayerNorm:

    def __init__(self, n, sem, region, at, ps, D, tiles):
        self.n, self.ps = n, ps
        self.full32, at = carve(region, at, [2, D], F32)
        self.rows, at = carve(region, at, [2, 2 * D], F16)
        self.xT, at = carve(region, at, [2, 2 * D // P, P], F16)
        self.end = at
        self.var = sem(f"ln{n}_variance")
        self.full = sem(f"ln{n}_normed")
        self.rstd = sem(f"rstd{n % 2}")
        self.before = n // 2 * tiles
        self.hi = sem(f"ln{n}_hi")
        self.lo = sem(f"ln{n}_lo")
        self.tr = sem(f"ln{n}_transposed")
        self.cols = sem(f"ln{n}_columns")


class Moe:
    pass


def build(nc, x, ctx_t, wq, wk, wv, scale_q, scale_k, wo, bo, rw0, w_in0, b_in0, w_out0, b_out0,
          cw1_t, cw2_t, cb, rw1_t, rb1, w1_t, b1, w2_t, b2, out):
    T, D = x.shape
    DC = D // P
    NT = T // P
    NB = 2
    L = ctx_t.shape[1] // NB
    DH = scale_q.shape[0]
    HE = wq.shape[1]
    NH = HE // DH
    NP = NH // 2
    PW = 2 * L
    NS = NH * L
    KC = math.ceil(NS / P)
    E = rw0.shape[1]
    H0, H1 = w_in0.shape[2], w1_t.shape[2]
    A = 2
    SW = A * P
    NSLOT = (2 * T + E * (SW - 1)) // SW
    NQ = A * NSLOT
    WS = 64.0
    PS = 1024.0
    LN_EPS, RMS_EPS = 1e-5, 1e-6
    CH = 1024
    NEG = -3.0e38
    VW_FIRST = 12
    VW_STEP = 4
    AHEAD = 2
    RING = 4

    with ExitStack() as ctx:
        def sb(name, shape, dt):
            return ctx.enter_context(nc.sbuf_tensor(name, shape, dt))

        sems = {}

        def sem(name):
            if name not in sems:
                sems[name] = ctx.enter_context(nc.semaphore(name))
            return sems[name]

        W1R = sb("w1_region", [P, 16384], F32)
        W2R = sb("w2_region", [P, 16384], F32)
        WBR = sb("wb_region", [P, 8192], F32)
        X = sb("x_res", [P, NT, D], F32)
        SLR = sb("slot_region", [P, 4096], F32)
        STG = sb("staging", [P, 2, CH], F32)

        w1s, _ = carve(W1R, 0, [E * 2 * DC * H1], F16)
        w2s, _ = carve(W2R, 0, [E * 2 * (H1 // P) * D], F16)
        wb_in, at = carve(WBR, 0, [E * 2 * DC * H0], F16)
        wb_out, at = carve(WBR, at, [E * 2 * (H0 // P) * D], F16)

        PSUM = ctx.enter_context(nc.psum_tensor("banks", [P, 8, 512], F32))
        bank = [PSUM[:, i, :] for i in range(8)]

        def half(k, n):
            return bank[k][:, 256 * n:256 * n + 256].bitcast(F16).rearrange("p (a b) -> p a b", b=P)

        zt, at = carve(W1R, 0, [NP, NB, 2 * P + PW], F32)
        pb2, at = carve(W1R, at, [KC * P], F32)
        vwf, at = carve(W1R, at, [4, D], F32)
        onehot0, _ = carve(W1R, 32768, [2 * NT, P], F16)
        ln0 = LayerNorm(0, sem, W1R, at, half(0, 0), D, NT)
        ln1 = LayerNorm(1, sem, W1R, ln0.end, half(0, 1), D, NT)
        ctx_s, at = carve(W1R, ln1.end, [DC, NB * L], F32)
        cw2, at = carve(W1R, at, [DC, D], F32)
        cmb, at = carve(W1R, at, [DC, NB, P], F32)
        cmean, at = carve(W1R, at, [DC, NB], F32)
        cb_s, at = carve(W1R, at, [NB, D], F32)
        route0, _ = carve(W1R, ln1.end, [1600], F32)
        assert at <= 65536
        wk_s, at = carve(WBR, 0, [DC, HE], F32)
        wv_s, at = carve(WBR, at, [DC, HE], F32)
        wo_s, at = carve(WBR, at, [NP, D], F32)
        assert at <= 32768
        wq_h, at = carve(W2R, 0, [DC, HE], F16)
        wq_l, at = carve(W2R, at, [DC, HE], F16)
        kbh, at = carve(W2R, at, [NP, NB, 2, L], F16)
        kbl, at = carve(W2R, at, [NP, NB, 2, L], F16)
        vw, at = carve(W2R, at, [NB, KC, 2, D], F16)
        qsq, at = carve(W2R, at, [NP, P], F32)
        pb01, at = carve(W2R, at, [2, KC * P], F32)
        qh, at = carve(W2R, at, [NP, P], F16)
        ql, at = carve(W2R, at, [NP, P], F16)
        pth_at = at
        pth, at = carve(W2R, at, [KC, P], F16)
        ptl, at = carve(W2R, at, [KC, P], F16)
        bo_row, at = carve(W2R, at, [D], F32)
        ident_f, at = carve(W2R, at, [P], F32)
        heads2, at = carve(W2R, at, [P], F32)
        assert at <= 65536
        pb = [pb01[:, 0, :], pb01[:, 1, :], pb2]
        kf = pb[0][:, 0:NP * NB * L].rearrange("p (j c) -> p j c", j=NP)
        k_tmp, _ = carve(W2R, pth_at, [2, NP * NB * L // 2], F32)
        ksq = pb[1][:, 0:NP * NB * L].rearrange("p (j c) -> p j c", j=NP)

        ident_h = sb("ident_h", [P, P], F16)
        before = sb("before", [P, P], F32)
        ones = sb("ones", [P, P], F32)
        first8 = sb("first8", [P, E], F32)
        iota_r = sb("iota_r", [P, P], F16)
        tokens = sb("tokens", [P, NT, 2], F32)
        ctx_bias = sb("ctx_bias", [P, NB, 2, D], F16)
        wc = sb("wc", [P, 2, DC, D], F16)
        rws = sb("rws", [P, 2, 2, DC, E], F16)
        rbb = sb("rbb", [P, E], F32)
        b_in0_s = sb("b_in0_s", [P, E * (H0 // P)], F32)
        b1_s = sb("b1_s", [P, E * (H1 // P)], F32)
        sks = sb("sks", [P, 4], F32)
        neghalf = sb("neghalf", [P, 1], F32)
        st6 = sb("st6", [P, 4, 6], F32)
        mv = sb("mv", [P, 4, 2, 2], F32)
        rv = sb("rv", [P, 4, 2, 2], F32)
        mxs = sb("mxs", [P, NH], F32)
        rq = sb("rq", [P, 2, NH], F32)
        rs = sb("rs", [P, NH], F32)
        lg = sb("lg", [P, NT, E], F32)
        gates = sb("gates", [P, 2, NT], F32)
        slots = sb("slots", [P, NT, 2], U32)
        index = sb("index", [P, NQ], U32)
        back = lg[:, :, :].rearrange("p t e -> p (t e)")[:, 0:NQ].bitcast(U32)
        expert = sb("expert", [P, 2, NSLOT], I32)

        rows_dram = nc.dram_tensor("normed_rows", [T, 2 * D], F16).ap()
        y_dram = nc.dram_tensor("sorted_y", [NQ * P, D], F32).ap()
        y_token = nc.dram_tensor("token_y", [2 * (T + 1) + NQ * P, D], F32).ap()

        chunks = []
        for dc in range(DC):
            chunks.append((wq[dc * P:(dc + 1) * P, :], wq_h[:, dc, :], wq_l[:, dc, :]))
        chunks.append((cw1_t.rearrange("(c p) n -> p c n", p=P), wc[:, 0, :, :], wc[:, 1, :, :]))
        chunks.append((None, rws[:, 0, :, :, :].rearrange("p a b c -> p (a b c)"),
                       rws[:, 1, :, :, :].rearrange("p a b c -> p (a b c)")))
        PRE = len(chunks)
        per = DC * H0
        for store, src in ((wb_in, w_in0), (wb_out, w_out0)):
            v = store.rearrange("p (e s n) -> p e s n", s=2, n=per)
            g = CH // per
            for e in range(0, E, g):
                chunks.append((src[e:e + g].rearrange("e (c p) n -> p e c n", p=P), v[:, e:e + g, 0, :], v[:, e:e + g, 1, :]))
        B_CH = len(chunks)
        per = DC * H1
        big = []
        for store, src in ((w1s, w1_t), (w2s, w2_t)):
            v = store.rearrange("p (e s n) -> p e s n", s=2, n=per)
            w = src.rearrange("e (c p) n -> p e c n", p=P)
            cs = w.shape[2] * CH // per
            for e in range(E):
                for part in range(per // CH):
                    c = slice(part * CH, (part + 1) * CH)
                    big.append((e, (w[:, e, part * cs:(part + 1) * cs, :], v[:, e, 0, c], v[:, e, 1, c])))
        chunks += [c for e, c in big if e < E - 1] + [c for e, c in big if e == E - 1]
        NCH = len(chunks)
        A_CH = 16
        LATE = 2 * (per // CH)

        def scaled(k):
            return k // 2 + 1 if k < NCH - LATE else (NCH - LATE) // 2 + k - (NCH - LATE) + 1

        def staged(k):
            hi = chunks[k][1]
            v = STG[:, k % 2, 0:product(hi.shape[1:])]
            if len(hi.shape) == 3:
                v = v.rearrange("p (a b) -> p a b", a=hi.shape[1])
            return v

        moes = []
        for layer, (H, wa, wb, b_s) in enumerate(((H0, wb_in, wb_out, b_in0_s), (H1, w1s, w2s, b1_s))):
            m = Moe()
            m.H, m.HC, m.wa, m.wb, m.b = H, H // P, wa, wb, b_s
            m.PARTS = A if layer else 1
            m.HH = m.HC // m.PARTS
            m.LAG = 3 - m.PARTS
            m.rows, at = carve(SLR, 0, [RING, A, 2 * D], F16)
            m.xT, at = carve(SLR, at, [2, 2 * DC, SW], F16)
            m.y, at = carve(SLR, at, [2, A, D], F32)
            if layer == 0:
                m.g, at = carve(W1R, 65536 - 8192, [2, m.HH, SW], F32)
                m.hh, at = carve(W1R, at, [2, m.HC, SW], F16)
                m.hl, at = carve(W1R, at, [2, m.HC, SW], F16)
                m.b2, _ = carve(W2R, 65536 - 8192, [E * D], F32)
            else:
                m.hh, at = carve(WBR, 0, [2, m.HC, SW], F16)
                m.hl, at = carve(WBR, at, [2, m.HC, SW], F16)
                m.g, at = carve(WBR, at, [2, m.HH, SW], F32)
                assert at <= 24576
                m.b2, _ = carve(WBR, 24576, [E * D], F32)
            moes.append(m)
        NG_BUF = 3
        yg, at = carve(WBR, 0, [NG_BUF, 2, D], F32)
        ln2 = LayerNorm(2, sem, WBR, at, half(0, 0), D, NT)
        ln3 = LayerNorm(3, sem, WBR, ln2.end, half(1, 0), D, NT)
        onehot1, at = carve(SLR, 0, [2 * NT, P], F16)
        route1, at = carve(SLR, at, [1600], F32)
        assert ln3.end <= 24576 and at <= 16384
        yg1, _ = carve(W1R, 0, [NT, 2, D], F32)
        last_groups = [range(0, 1), range(1, 4), range(4, 8), range(8, 12), range(12, 15), range(15, NT)]
        behind = route1[:, 1040:1040 + NQ]
        routes = [route0, route1]
        onehots = [onehot0, onehot1]

        GP = 4
        groups = [(a, min(a + GP, KC)) for a in range(0, KC, GP)]
        NG = len(groups)
        score_banks = PSUM[:, 3:6, 0:6 * L].rearrange("p b (h k) -> p b h k", k=L)
        SSQ = bank[5][:, 320:320 + NH]
        LOG = [bank[5][:, 400:400 + E]] * 2
        LOG1 = [bank[4][:, 400:400 + E], bank[5][:, 400:400 + E]]
        q_ps = PSUM[:, 1:3, :].rearrange("p b (j t) -> p (b j) t", t=P)
        o_ps = bank[0][:, 0:D]
        c_ps = [bank[6][:, 0:D], bank[7][:, 0:D]]
        FULL = NP // 3
        LAST = slice(FULL * 6, NH)


        def slot_columns(j):
            return bank[7 * (j % 2)].bitcast(F16)[:, 0:2 * DC * SW].rearrange("p (c t) -> p c t", t=SW)

        def slot_banks(j):
            b = 5 if A == 2 else 5 + j % 2
            return PSUM[:, b:b + A, 0:D]

        def hidden(m, u):
            b = 1 + 2 * (u % 2)
            return PSUM[:, b:b + 2, :].rearrange("p b (c t) -> p (b c) t", t=SW)[:, 0:m.HH, :]

        block = ctx.enter_context(nc.Block())

        @block.sync
        def _(sp):
            def load(dst, src, name):
                sp.dma_start(dst, src).then_inc(sem(name), 16)

            def stage(k):
                if k >= 2:
                    sp.wait_ge(sem(f"chunk_lo{k % 2}"), k // 2)
                loaded = sem(f"chunk_loaded{k % 2}")
                src = chunks[k][0]
                if src is None:
                    n = DC * E
                    for layer, w in enumerate((rw0, rw1_t)):
                        sp.dma_start(STG[:, k % 2, layer * n:(layer + 1) * n].rearrange("p (c e) -> p c e", c=DC),
                                     w.rearrange("(c p) e -> p c e", p=P)).then_inc(
                            loaded if layer else sem("router_loaded"), 16)
                    return
                dst = STG[:, k % 2, 0:product(src.shape[1:])]
                if len(src.shape) == 3:
                    dst = dst.rearrange("p (a b) -> p a b", a=src.shape[1])
                if len(src.shape) == 4:
                    dst = dst.rearrange("p (e a b) -> p e a b", e=src.shape[1], a=src.shape[2])
                    sp.dma_start(dst[:, 0], src[:, 0]).then_inc(sem(f"chunk_part{k % 2}"), 16)
                    sp.dma_start(dst[:, 1], src[:, 1]).then_inc(loaded, 16)
                    return
                sp.dma_start(dst, src).then_inc(loaded, 16)

            load(ctx_s, ctx_t.rearrange("(c p) n -> p c n", p=P), "ctx_loaded")
            load(wk_s, wk.rearrange("(c p) n -> p c n", p=P), "wk_loaded")
            for h in range(2):
                load(sks[h * DH:(h + 1) * DH, 0:1], scale_q.rearrange("(e o) -> e o", o=1), "scales_loaded")
                load(sks[h * DH:(h + 1) * DH, 1:2], scale_k.rearrange("(e o) -> e o", o=1), "scales_loaded")
            load(wv_s, wv.rearrange("(c p) n -> p c n", p=P), "wv_loaded")
            load(cw2, cw2_t.rearrange("(c p) n -> p c n", p=P), "cw2_loaded")
            q4 = NT // 4
            xv = x.rearrange("(t p) d -> p t d", p=P)
            load(X[:, 0:q4, :], xv[:, 0:q4, :], "x_loaded0")
            stage(0)
            stage(1)
            load(wo_s, wo.rearrange("(j p) n -> p j n", p=P), "wo_loaded")
            for b in range(NB):
                load(cb_s[:, b, :], cb.partition_broadcast(P), "cb_loaded")
            sp.wait_ge(sem("bo_zeroed"), 1)
            load(bo_row[NS % P:NS % P + 1, :], bo.rearrange("(o n) -> o n", o=1), "bo_loaded")
            for g in range(1, 4):
                load(X[:, g * q4:(g + 1) * q4, :], xv[:, g * q4:(g + 1) * q4, :], f"x_loaded{g}")
            for k in range(2, PRE):
                stage(k)
            load(b_in0_s[:, :], b_in0, "b_in0_loaded")
            load(b1_s[:, :], b1, "b1_loaded")
            load(rbb[:, :], rb1.partition_broadcast(P), "rb_loaded")
            sp.wait_ge(sem("vw_done"), NB * KC)

            rows_v = rows_dram.rearrange("(t p) d -> t p d", p=P)

            def keep_rows(o, i):
                sp.wait_ge(o.lo, i + 1)
                sp.dma_start(rows_v[i], o.rows[:, i % 2, :]).then_inc(sem(f"rows_kept{o.n}_{i % 2}"), 16)

            stage(PRE)
            stage(PRE + 1)
            for i in range(NT):
                keep_rows(ln1, i)
                stage(PRE + 2 + i)

            yv = y_dram.rearrange("(j a p) d -> j p a d", a=A, p=P)

            def keep_y(layer, j):
                sp.wait_ge(sem(f"y_ready{layer}"), j + 1)
                sp.dma_start(yv[j], moes[layer].y[:, j % 2]).then_inc(sem(f"y_kept{layer}_{j % 2}"), 16)

            sp.wait_ge(sem("routed"), 1)
            load(moes[0].b2, b_out0.partition_broadcast(P), "b2_loaded0")
            for j in range(NSLOT + 4):
                if PRE + A_CH + 2 + j < NCH - LATE + 2:
                    stage(PRE + A_CH + 2 + j)
                if j >= 4:
                    keep_y(0, j - 4)
            load(moes[1].b2, b2.partition_broadcast(P), "b2_loaded1")
            for i in range(NT):
                keep_rows(ln3, i)
            for k in range(NCH - LATE + 2, NCH):
                stage(k)
            ov = out.rearrange("(t p) d -> p t d", p=P)
            for group in last_groups:
                t = slice(group.start, group.stop)
                sp.wait_ge(sem("y_used1"), 2 * group.stop)
                sp.dma_start(ov[:, t, :], X[:, t, :]).then_inc(sem("out_stored"), 16)
            sp.wait_ge(sem("out_stored"), 16 * len(last_groups))

        @block.gpsimd
        def _(pool):
            g = nc.gpsimd
            chain = [0]

            def link(ins):
                chain[0] += 1
                ins.then_inc(sem("pool_chain"), 1)
                pool.wait_ge(sem("pool_chain"), chain[0])

            link(g.memset(neghalf[:, :], -0.5))
            link(g.memset(heads2, 0.0))
            link(g.memset(heads2[0:DH, 0:DH], 1.0))
            g.memset(heads2[DH:P, DH:P], 1.0).then_inc(sem("heads_ready"), 1)
            pool.wait_ge(sem("heads_ready"), 1)
            g.memset(zt, 0.0).then_inc(sem("zt_zeroed"), 1)
            g.memset(kbh, 0.0)
            g.memset(kbl, 0.0)
            g.memset(bo_row, 0.0).then_inc(sem("bo_zeroed"), 1)
            link(g.memset(pb01[:, :, NS:KC * P], 0.0))
            link(g.memset(pb2[:, NS:KC * P], 0.0))
            g.memset(pb2[:, NS:NS + 1], PS)
            g.memset(pb01[:, :, NS:NS + 1], PS).then_inc(sem("kb_zeroed"), 1)
            for t in (ident_h[:, :], ident_f):
                link(g.memset(t, 0.0))
                link(g.affine_select(out=t, in_=t, compare_op=ALU.not_equal, fill=1.0, base=0,
                                     pattern=[[-1, P]], channel_multiplier=1))
            link(g.memset(ones[:, :], 1.0))
            link(g.affine_select(out=before[:, :], in_=ones[:, :], compare_op=ALU.is_gt, fill=0.0, base=0,
                                 pattern=[[1, P]], channel_multiplier=-1))
            link(g.iota(first8[:, :], pattern=[[-1, E]], base=E, channel_multiplier=0,
                        allow_small_or_imprecise_dtypes=True))
            link(g.iota(tokens[:, :, 0], pattern=[[P, NT]], base=1, channel_multiplier=1,
                        allow_small_or_imprecise_dtypes=True))
            link(g.iota(tokens[:, :, 1], pattern=[[-P, NT]], base=-1, channel_multiplier=-1,
                        allow_small_or_imprecise_dtypes=True))
            g.iota(iota_r[:, :], pattern=[[1, P]], base=0, channel_multiplier=0,
                   allow_small_or_imprecise_dtypes=True).then_inc(sem("consts_ready"), 1)

            def split_lo(k):
                pool.wait_ge(sem("chunk_scaled"), scaled(k))
                g.tensor_tensor(chunks[k][2], staged(k), chunks[k][1], ALU.subtract).then_inc(sem(f"chunk_lo{k % 2}"), 1)

            def vw_lo(n):
                pool.wait_ge(sem("vw_hi"), n + 1)
                g.tensor_tensor(vw[:, n // KC, n % KC, 1, :], vwf[:, n % 4, :], vw[:, n // KC, n % KC, 0, :],
                                ALU.subtract).then_inc(sem("vw_ready"), 1)

            def rstd(o, i):
                pool.wait_ge(o.var, i + 1)
                if i >= 2:
                    pool.wait_ge(o.full, i - 1)
                r = rv[:, o.n, i % 2, :]
                link(g.tensor_tensor(r[:, 0:1], mv[:, o.n, i % 2, 1:2], neghalf[:, :], ALU.pow))
                g.tensor_scalar(r[:, 1:2], mv[:, o.n, i % 2, 0:1], r[:, 0:1], -1.0, ALU.mult, ALU.mult).then_inc(o.rstd, 1)

            def rstd_both(a, b):
                for o, i in ((ln2, a), (ln3, b)):
                    pool.wait_ge(o.var, i + 1)
                    if i >= 2:
                        pool.wait_ge(o.full, i - 1)
                at2, at3 = 4 * ln2.n + 2 * (a % 2), 4 * ln3.n + 2 * (b % 2)
                rf, mf = (w.rearrange("p n b k -> p (n b k)") for w in (rv[:, :, :, :], mv[:, :, :, :]))
                link(g.tensor_tensor(rf[:, at2:at3 + 1:at3 - at2], mf[:, at2 + 1:at3 + 2:at3 - at2],
                                     neghalf[:, 0:1].to_broadcast([P, 2]), ALU.pow))
                for o, i in ((ln2, a), (ln3, b)):
                    r = rv[:, o.n, i % 2, :]
                    g.tensor_scalar(r[:, 1:2], mv[:, o.n, i % 2, 0:1], r[:, 0:1], -1.0, ALU.mult, ALU.mult).then_inc(
                        o.rstd, 1)

            def q_rms(i):
                pool.wait_ge(sem("q_ms"), i + 1)
                v = rq[:, i % 2, :]
                link(g.tensor_tensor(v, v, neghalf[:, 0:1].to_broadcast([P, NH]), ALU.pow))

            def p_rows(i):
                return pb[i % 3][:, 0:NS].rearrange("p (h k) -> p h k", k=L)

            def scale_scores(i):
                pool.wait_ge(sem("scores_shifted"), i + 1)
                g.tensor_tensor(p_rows(i), p_rows(i), rq[:, i % 2, :, None].to_broadcast([P, NH, L]),
                                ALU.mult).then_inc(sem("scores_scaled"), 1)

            def norm_weights(i):
                pool.wait_ge(sem("row_sums"), i + 1)
                g.tensor_tensor(p_rows(i), p_rows(i), rs[:, :, None].to_broadcast([P, NH, L]),
                                ALU.mult).then_inc(sem("weights_ready"), 1)

            split_lo(0)
            for n in range(VW_FIRST):
                vw_lo(n)
            for s in range(NT + 9):
                if 0 <= s - 3 < NT:
                    q_rms(s - 3)
                    scale_scores(s - 3)
                if s < NT:
                    rstd(ln0, s)
                if 0 <= s - 6 < NT:
                    rstd(ln1, s - 6)
                for n in range(VW_FIRST + VW_STEP * s, min(NB * KC, VW_FIRST + VW_STEP * (s + 1))):
                    vw_lo(n)
                if 0 < s < PRE and s % 2 == 0:
                    split_lo(s)
                if 0 <= s - 4 < NT:
                    norm_weights(s - 4)
                if 0 <= s - 6 < NT and (PRE + s - 6) % 2 == 0:
                    split_lo(PRE + s - 6)

            def number_tokens(layer):
                at_q = routes[layer][:, 128:128 + NT * NQ].bitcast(F16).rearrange("p (n q) -> p n q", q=NQ)
                num = tokens[:, :, :].rearrange("p t c -> p (t c)")[:, :, None].to_broadcast([P, 2 * NT, NQ])
                pool.wait_ge(sem("tiles_hot"), layer + 1)
                g.tensor_tensor(at_q, at_q, num, ALU.mult).then_inc(sem("places"), 1)

            def gather_rows(layer, j):
                m = moes[layer]
                for a in range(A):
                    if j >= RING:
                        pool.wait_ge(sem(f"slot_tr{layer}"), j - RING + 1)
                    q = A * j + a
                    g.indirect_dma_start(
                        out=m.rows[:, j % RING, a, :], out_offset=None, in_=rows_dram,
                        in_offset=bass.IndirectOffsetOnAxis(ap=index[:, q:q + 1], axis=0)).then_inc(
                        sem(f"rows_gathered{layer}_{j % RING}"), 16)

            def slot_rows(layer):
                number_tokens(layer)
                pool.wait_ge(sem("routed"), layer + 1)
                for b in range(2):
                    pool.wait_ge(sem(f"rows_kept{1 + 2 * layer}_{b}"), 16 * (NT // 2))
                for j in range(AHEAD):
                    gather_rows(layer, j)
                if layer == 1:
                    pool.wait_ge(sem("back_ready"), 1)
                for j in range(NSLOT + 3 * layer):
                    if j + AHEAD < NSLOT:
                        gather_rows(layer, j + AHEAD)
                    if layer == 1 and j >= 3:
                        scatter_y(j - 3)
                    if layer == 0:
                        k = PRE + A_CH + j
                        if k < NCH - LATE and k % 2 == 0:
                            split_lo(k)
                if layer == 0:
                    for b in range(2):
                        pool.wait_ge(sem(f"y_kept0_{b}"), 16 * ((NSLOT + 1 - b) // 2))

            def gather_y(layer, i, ring):
                n = ring.shape[1]
                for c in range(2):
                    if i >= n:
                        pool.wait_ge(sem(f"y_used{layer}"), 2 * (i - n) + c + 1)
                    g.indirect_dma_start(
                        out=ring[:, i % n, c, :], out_offset=None, in_=y_dram,
                        in_offset=bass.IndirectOffsetOnAxis(ap=slots[:, i, c:c + 1], axis=0)).then_inc(
                        sem(f"y_gathered{layer}_{i % n}"), 16)

            def scatter_y(j):
                for a in range(A):
                    pool.wait_ge(sem("y_ready1"), j + 1)
                    q = A * j + a
                    g.indirect_dma_start(
                        out=y_token, out_offset=bass.IndirectOffsetOnAxis(ap=back[:, q:q + 1], axis=0),
                        in_=moes[1].y[:, j % 2, a, :], in_offset=None).then_inc(sem(f"y_kept1_{j % 2}"), 16)

            slot_rows(0)
            g.iota(behind, pattern=[[P, NQ]], base=2 * (T + 1), channel_multiplier=1,
                   allow_small_or_imprecise_dtypes=True).then_inc(sem("behind_ready"), 1)
            for s in range(NT + 5):
                if s < NT:
                    gather_y(0, s, yg)
                if 0 <= s - 5 and s - 2 < NT:
                    rstd_both(s - 2, s - 5)
                elif 0 <= s - 5:
                    rstd(ln3, s - 5)
                elif 0 <= s - 2:
                    rstd(ln2, s - 2)
            for k in range(NCH - LATE, NCH):
                split_lo(k)
            slot_rows(1)

        @block.scalar
        def _(act):
            s_ = nc.scalar

            def split_hi(k):
                act.wait_ge(sem(f"chunk_loaded{k % 2}"), 16 * (k // 2 + 1))
                if chunks[k][0] is None:
                    act.wait_ge(sem("router_loaded"), 16)
                elif len(chunks[k][0].shape) == 4:
                    n = sum(1 for c in range(k % 2, k + 1, 2) if chunks[c][0] is not None and len(chunks[c][0].shape) == 4)
                    act.wait_ge(sem(f"chunk_part{k % 2}"), 16 * n)
                s_.activation(chunks[k][1], staged(k), ACT.Copy, scale=WS).then_inc(sem(f"chunk_hi{k % 2}"), 1)
                if k % 2 == 0 or k >= NCH - LATE:
                    act.wait_ge(sem(f"chunk_hi{k % 2}"), k // 2 + 1)
                    s_.activation(staged(k), staged(k), ACT.Copy, scale=WS).then_inc(sem("chunk_scaled"), 1)

            for j in range(NP):
                act.wait_ge(sem("k_done"), j + 1)
                s_.activation(ksq[:, j, :], bank[3 + j % 2][:, 0:NB * L], ACT.Square).then_inc(sem("k_sq"), 1)
            for k in range(2):
                split_hi(k)
            act.wait_ge(sem("zt_zeroed"), 1)
            for j in range(NP):
                act.wait_ge(sem("vt_done"), j + 1)
                for h in range(2):
                    rows = slice(h * DH, (h + 1) * DH)
                    s_.activation(zt[rows, j, :, P + h * L:P + (h + 1) * L], bank[1 + j % 2][rows, 0:NB * L].rearrange(
                        "p (b k) -> p b k", b=NB), ACT.Copy).then_inc(sem("vt_copied"), 1)

            def k_hi():
                act.wait_ge(sem("k_normed"), 1)
                act.wait_ge(sem("kb_zeroed"), 1)
                for h in range(2):
                    rows = slice(h * DH, (h + 1) * DH)
                    s_.activation(kbh[rows, :, :, h, :], kf[rows].rearrange("p j (b k) -> p j b k", b=NB),
                                  ACT.Copy).then_inc(sem("kb_hi"), 1)

            def vw_hi(n):
                act.wait_ge(sem("vw_done"), n + 1)
                if n >= 4:
                    act.wait_ge(sem("vw_ready"), n - 3)
                s_.activation(vwf[:, n % 4, :], bank[6 + n % 2][:, 0:D], ACT.Copy, scale=WS)
                s_.activation(vw[:, n // KC, n % KC, 0, :], bank[6 + n % 2][:, 0:D], ACT.Copy, scale=WS).then_inc(
                    sem("vw_hi"), 1)

            def norm(o, i):
                act.wait_ge(o.rstd, o.before + i + 1)
                if i >= 2:
                    act.wait_ge(o.lo, i - 1)
                r = rv[:, o.n, i % 2, :]
                s_.activation(o.full32[:, i % 2, :], X[:, i, :], ACT.Identity, bias=r[:, 1:2], scale=r[:, 0:1]).then_inc(
                    o.full, 1)

            def norm_hi(o, i):
                act.wait_ge(o.full, i + 1)
                if i >= 2:
                    act.wait_ge(o.tr, i - 1)
                    if o.n in (1, 3):
                        act.wait_ge(sem(f"rows_kept{o.n}_{i % 2}"), 16 * (i // 2))
                s_.activation(o.rows[:, i % 2, 0:D], o.full32[:, i % 2, :], ACT.Copy).then_inc(o.hi, 1)

            def columns(o, i, user):
                act.wait_ge(o.tr, i + 1)
                if i >= 2:
                    act.wait_ge(sem(user), i - 1)
                s_.activation(o.xT[:, i % 2], o.ps, ACT.Copy).then_inc(o.cols, 1)

            def q_hi(i):
                act.wait_ge(sem("q_done"), i + 1)
                if i >= 1:
                    act.wait_ge(sem("scores_done"), i)
                s_.activation(qh, q_ps, ACT.Copy).then_inc(sem("q_hi"), 1)
                if i >= 1:
                    act.wait_ge(sem("ssq_done"), i)
                s_.activation(qsq, q_ps, ACT.Square, scale=1.0 / WS).then_inc(sem("q_sq"), 1)

            def exp(i):
                act.wait_ge(sem("scores_scaled"), i + 1)
                v = pb[i % 3][:, 0:NS]
                s_.activation(v, v, ACT.Exp, scale=1.0 / (WS * WS)).then_inc(sem("exp_done"), 1)

            def pt_hi(i, n):
                a, b = groups[n]
                act.wait_ge(sem("weights_tr"), NG * i + n + 1)
                if i >= 1:
                    act.wait_ge(sem("attn_done"), i)
                s_.activation(pth[:, a:b, :], bank[6 + (NG * i + n) % 2][:, 0:(b - a) * P].rearrange(
                    "p (c t) -> p c t", t=P), ACT.Copy).then_inc(sem("pt_hi"), 1)

            for n in range(VW_FIRST):
                vw_hi(n)
            k_hi()
            for s in range(NT + 9):
                if 0 <= s - 2 < NT:
                    q_hi(s - 2)
                if 0 <= s - 5 < NT:
                    pt_hi(s - 5, 0)
                    pt_hi(s - 5, 1)
                if 0 <= s - 1 < NT:
                    if s - 1 >= 6:
                        act.wait_ge(ln1.tr, s - 6)
                    columns(ln0, s - 1, "q_done")
                if 0 <= s - 7 < NT:
                    columns(ln1, s - 7, "logits_done0")
                if 0 <= s - 3 < NT:
                    exp(s - 3)
                if 0 <= s - 5 < NT:
                    pt_hi(s - 5, 2)
                if 0 <= s - 6 < NT:
                    split_hi(PRE + s - 6)
                if s < NT:
                    norm(ln0, s)
                if 0 <= s - 6 < NT:
                    norm(ln1, s - 6)
                if s < NT:
                    norm_hi(ln0, s)
                if 0 <= s - 6 < NT:
                    norm_hi(ln1, s - 6)
                for n in range(VW_FIRST + VW_STEP * s, min(NB * KC, VW_FIRST + VW_STEP * (s + 1))):
                    vw_hi(n)
                if 2 <= s < PRE:
                    split_hi(s)

            def route(layer):
                act.wait_ge(sem("route_shift"), layer + 1)
                r = routes[layer]
                s_.activation(r[:, 0:NT * E], r[:, 0:NT * E], ACT.Exp).then_inc(sem("route_exp"), 1)
                s_.activation(r[:, 1152:1152 + NT], r[:, 1152:1152 + NT], ACT.Exp).then_inc(sem("route_exp"), 1)

            def gelu(layer, j):
                m = moes[layer]
                for a in range(m.PARTS):
                    u = m.PARTS * j + a
                    v = m.g[:, u % 2]
                    act.wait_ge(sem(f"h_biased{layer}"), u + 1)
                    s_.activation(v, v, ACT.Gelu_apprx_tanh).then_inc(sem("gelu"), 1)
                    act.wait_ge(sem("gelu"), NSLOT * layer + u + 1)
                    if j >= 2:
                        act.wait_ge(sem(f"slot_y{layer}"), j - 1)
                    s_.activation(m.hh[:, j % 2, a * m.HH:(a + 1) * m.HH, :], v, ACT.Copy).then_inc(
                        sem(f"h_hi{layer}"), 1)

            route(0)
            act.wait_ge(sem("gates_ready"), 1)
            for s in range(NSLOT + 1):
                if s < NSLOT and PRE + A_CH + s < NCH - LATE:
                    split_hi(PRE + A_CH + s)
                if s >= 1:
                    gelu(0, s - 1)
            act.wait_ge(sem("y_ready0"), NSLOT)
            for s in range(NT + 7):
                if 0 <= s - 5 < NT:
                    norm(ln3, s - 5)
                if 0 <= s - 2 < NT:
                    norm(ln2, s - 2)
                if 0 <= s - 5 < NT:
                    norm_hi(ln3, s - 5)
                if 0 <= s - 2 < NT:
                    norm_hi(ln2, s - 2)
                if 0 <= s - 3 < NT:
                    columns(ln2, s - 3, "linear_done")
                if 0 <= s - 6 < NT:
                    columns(ln3, s - 6, "logits_done1")
            for k in range(NCH - LATE, NCH):
                split_hi(k)
            route(1)
            for j in range(NSLOT):
                gelu(1, j)
            for b in range(2):
                act.wait_ge(sem(f"y_kept1_{b}"), 16 * A * ((NSLOT + 1 - b) // 2))
            yv = y_token[2:2 * (T + 1), :].rearrange("(t p c) d -> p t (c d)", p=P, c=2)
            for n, group in enumerate(last_groups):
                t = slice(group.start, group.stop)
                act.dma_start(yg1[:, t, :, :].rearrange("p t c d -> p t (c d)"), yv[:, t, :]).then_inc(
                    sem(f"y_gathered1_{n}"), 16)

        @block.vector
        def _(dve):
            v = nc.vector
            chain = [0]

            def link(ins):
                chain[0] += 1
                ins.then_inc(sem("dve_chain"), 1)
                dve.wait_ge(sem("dve_chain"), chain[0])

            dve.wait_ge(sem("scales_loaded"), 4 * 16)
            link(v.tensor_tensor(sks[:, 2:3], sks[:, 0:1], sks[:, 1:2], ALU.mult))
            link(v.tensor_scalar(sks[:, 3:4], sks[:, 2:3], WS / math.sqrt(DH), None, ALU.mult))
            dve.wait_ge(sem("ctx_loaded"), 16)
            link(v.tensor_reduce(cmean, ctx_s.rearrange("p c (b k) -> p c b k", b=NB), axis=AX.X, op=ALU.add))
            v.tensor_scalar(cmb, cmean[:, :, :, None].to_broadcast([P, DC, NB, P]), 1.0 / L, None,
                            ALU.mult).then_inc(sem("mean_ready"), 1)
            for j in range(NP):
                dve.wait_ge(sem("k_sq"), j + 1)
                v.tensor_copy(kf[:, j, :], bank[3 + j % 2][:, 0:NB * L]).then_inc(sem("k_copied"), 1)
                dve.wait_ge(sem("k_ssq"), j + 1)
                v.tensor_scalar(ksq[:, j, :], bank[5][:, 0:NB * L], 1.0 / DH, RMS_EPS, ALU.mult, ALU.add).then_inc(
                    sem("k_ms"), 1)
            def stats(o, i):
                link(v.bn_stats(st6[:, o.n, :], X[:, i, :]))
                if i >= 2:
                    dve.wait_ge(o.full, i - 1)
                link(v.bn_aggr(mv[:, o.n, i % 2, :], st6[:, o.n, :]))
                v.tensor_scalar_add(mv[:, o.n, i % 2, 1:2], mv[:, o.n, i % 2, 1:2], LN_EPS).then_inc(o.var, 1)

            dve.wait_ge(sem("x_loaded0"), 16)
            stats(ln0, 0)
            kv = pb[1][:, 0:NP * NB * L]
            half_n = NP * NB * L // 2
            y, t = k_tmp[:, 0, :], k_tmp[:, 1, :]
            dve.wait_ge(sem("k_ms"), NP)
            for part in range(2):
                kp = kv[:, part * half_n:(part + 1) * half_n]
                link(v.tensor_scalar(y.bitcast(I32), kp.bitcast(I32), -0.5, float(RSQRT_SEED), ALU.mult, ALU.add))
                for n in range(3):
                    link(v.tensor_tensor(t, y, y, ALU.mult))
                    link(v.scalar_tensor_tensor(out=t, in0=t, scalar=-0.5, in1=kp, op0=ALU.mult, op1=ALU.mult))
                    link(v.scalar_tensor_tensor(out=y if n < 2 else kp, in0=t, scalar=1.5, in1=y, op0=ALU.add,
                                                op1=ALU.mult))
            v.scalar_tensor_tensor(out=pb[0][:, 0:NS], in0=pb[0][:, 0:NS], scalar=sks[:, 3:4], in1=kv,
                                   op0=ALU.mult, op1=ALU.mult).then_inc(sem("k_normed"), 1)
            for b in range(NB):
                dve.wait_ge(sem("mean_done"), b + 1)
                dve.wait_ge(sem("cb_loaded"), 32)
                v.tensor_tensor(cb_s[:, b, :], bank[3 + b][:, 0:D], cb_s[:, b, :], ALU.add).then_inc(
                    sem("ctx_bias_ready"), 1)
                dve.wait_ge(sem("ctx_bias_ready"), b + 1)
                link(v.tensor_scalar(ctx_bias[:, b, 0, :], cb_s[:, b, :], WS, None, ALU.mult))
                link(v.scalar_tensor_tensor(out=ctx_bias[:, b, 1, :], in0=cb_s[:, b, :], scalar=WS,
                                            in1=ctx_bias[:, b, 0, :], op0=ALU.mult, op1=ALU.subtract))

            def k_lo():
                for h in range(2):
                    dve.wait_ge(sem("kb_hi"), h + 1)
                    rows = slice(h * DH, (h + 1) * DH)
                    v.tensor_tensor(kbl[rows, :, :, h, :], kf[rows].rearrange("p j (b k) -> p j b k", b=NB),
                                    kbh[rows, :, :, h, :], ALU.subtract).then_inc(sem("kb_ready"), 1)

            def split_lo(k):
                dve.wait_ge(sem("chunk_hi1"), k // 2 + 1)
                v.scalar_tensor_tensor(out=chunks[k][2], in0=staged(k), scalar=WS, in1=chunks[k][1],
                                       op0=ALU.mult, op1=ALU.subtract).then_inc(sem("chunk_lo1"), 1)

            def norm_lo(o, i):
                dve.wait_ge(o.hi, i + 1)
                r = o.rows[:, i % 2, :]
                v.tensor_tensor(r[:, D:2 * D], o.full32[:, i % 2, :], r[:, 0:D], ALU.subtract).then_inc(o.lo, 1)

            def q_ms(i):
                dve.wait_ge(sem("ssq_done"), i + 1)
                if i >= 6:
                    dve.wait_ge(sem("logits_done0"), i - 5)
                if i >= 2:
                    dve.wait_ge(sem("scores_scaled"), i - 1)
                v.tensor_scalar(rq[:, i % 2, :], SSQ, 1.0 / DH, RMS_EPS, ALU.mult, ALU.add).then_inc(sem("q_ms"), 1)

            def shift(i):
                dve.wait_ge(sem("scores_done"), i + 1)
                full = score_banks[:, 0:FULL, :, :]
                last = score_banks[:, FULL, 0:NH - FULL * 6, :]
                v.tensor_reduce(mxs[:, 0:FULL * 6].rearrange("p (b h) -> p b h", b=FULL), full, axis=AX.X, op=ALU.max)
                link(v.tensor_reduce(mxs[:, LAST], last, axis=AX.X, op=ALU.max))
                if i == 0:
                    dve.wait_ge(sem("kb_ready"), 2)
                if i >= 3:
                    dve.wait_ge(sem("weights_tr"), NG * (i - 2))
                row = pb[i % 3][:, 0:NS].rearrange("p (h k) -> p h k", k=L)
                v.tensor_tensor(row[:, 0:FULL * 6, :].rearrange("p (b h) k -> p b h k", b=FULL), full,
                                mxs[:, 0:FULL * 6].rearrange("p (b h) -> p b h", b=FULL)[:, :, :, None].to_broadcast(
                                    [P, FULL, 6, L]), ALU.subtract)
                v.tensor_tensor(row[:, LAST, :], last, mxs[:, LAST][:, :, None].to_broadcast([P, NH - FULL * 6, L]),
                                ALU.subtract).then_inc(sem("scores_shifted"), 1)

            def sums(i):
                dve.wait_ge(sem("exp_done"), i + 1)
                if i >= 1:
                    dve.wait_ge(sem("weights_ready"), i)
                link(v.tensor_reduce(rs[:, :], pb[i % 3][:, 0:NS].rearrange("p (h k) -> p h k", k=L), axis=AX.X,
                                     op=ALU.add))
                link(v.reciprocal(rs[:, :], rs[:, :]))
                v.tensor_scalar(rs[:, :], rs[:, :], PS, None, ALU.mult).then_inc(sem("row_sums"), 1)

            def pt_lo(i, n):
                a, b = groups[n]
                dve.wait_ge(sem("pt_hi"), NG * i + n + 1)
                v.tensor_tensor(ptl[:, a:b, :], bank[6 + (NG * i + n) % 2][:, 0:(b - a) * P].rearrange(
                    "p (c t) -> p c t", t=P), pth[:, a:b, :], ALU.subtract).then_inc(sem("pt_lo"), 1)

            def q_lo(i):
                dve.wait_ge(sem("q_sq"), i + 1)
                v.tensor_tensor(ql, q_ps, qh, ALU.subtract).then_inc(sem("q_lo"), 1)

            def add_attn(i):
                dve.wait_ge(sem("attn_done"), i + 1)
                dve.wait_ge(ln0.full, i + 1)
                v.scalar_tensor_tensor(out=X[:, i, :], in0=o_ps, scalar=1.0 / (WS * PS), in1=X[:, i, :],
                                       op0=ALU.mult, op1=ALU.add).then_inc(sem("attn_added"), 1)
                dve.wait_ge(sem("attn_added"), i + 1)

            def logits(layer, i):
                dve.wait_ge(sem(f"logits_done{layer}"), i + 1)
                if layer == 0:
                    v.tensor_scalar(lg[:, i, :], LOG[i % 2], 1.0 / WS, None, ALU.mult).then_inc(sem("logits_read0"), 1)
                else:
                    if i == 0:
                        dve.wait_ge(sem("rb_loaded"), 16)
                    v.scalar_tensor_tensor(out=lg[:, i, :], in0=LOG1[i % 2], scalar=1.0 / WS, in1=rbb[:, :],
                                           op0=ALU.mult, op1=ALU.add).then_inc(sem("logits_read1"), 1)

            for s in range(NT + 9):
                if 0 <= s - 2 < NT:
                    q_lo(s - 2)
                if 0 <= s - 6 < NT:
                    add_attn(s - 6)
                if 1 <= s < NT:
                    if s % (NT // 4) == 0:
                        dve.wait_ge(sem(f"x_loaded{s // (NT // 4)}"), 16)
                    stats(ln0, s)
                if 0 <= s - 6 < NT:
                    stats(ln1, s - 6)
                if 0 <= s - 5 < NT:
                    pt_lo(s - 5, 0)
                    pt_lo(s - 5, 1)
                if 0 <= s - 4 < NT:
                    sums(s - 4)
                if 0 <= s - 5 < NT:
                    pt_lo(s - 5, 2)
                if 0 <= s - 2 < NT:
                    q_ms(s - 2)
                if 0 <= s - 8 < NT:
                    logits(0, s - 8)
                if 0 <= s - 2 < NT:
                    shift(s - 2)
                if s == 0:
                    split_lo(1)
                if s < NT:
                    norm_lo(ln0, s)
                if 0 <= s - 6 < NT:
                    norm_lo(ln1, s - 6)
                if s == 0:
                    k_lo()
                if s == 3:
                    split_lo(3)
                if 0 <= s - 6 < NT and (PRE + s - 6) % 2:
                    split_lo(PRE + s - 6)

            def route(layer):
                r = routes[layer]

                def cut(n):
                    return r[:, n * P:n * P + NT * E]

                def te(a):
                    return a.rearrange("p (t e) -> p t e", e=E)

                def et(a):
                    return a.rearrange("p (e t) -> p e t", e=E)

                ex, m1, m2, best = cut(0), r[:, 1024:1024 + NT], r[:, 1152:1152 + NT], r[:, 1088:1088 + NT]
                oh = [cut(1), cut(2)]
                cand, masked, hot, tot = cut(3), cut(4), cut(5), cut(6)
                counts = r[:, 1216:1216 + 64]
                dve.wait_ge(sem(f"logits_read{layer}"), NT)
                if layer == 0:
                    dve.wait_ge(sem("consts_ready"), 1)
                cur = lg[:, :, :]
                f8 = first8[:, None, :].to_broadcast([P, NT, E])
                for c, m in enumerate((m1, m2)):
                    link(v.tensor_reduce(m, cur, axis=AX.X, op=ALU.max))
                    link(v.tensor_tensor(te(cand), cur, m[:, :, None].to_broadcast([P, NT, E]), ALU.is_equal))
                    link(v.tensor_tensor(te(cand), te(cand), f8, ALU.mult))
                    link(v.tensor_reduce(best, te(cand), axis=AX.X, op=ALU.max))
                    link(v.tensor_tensor(te(oh[c]), f8, best[:, :, None].to_broadcast([P, NT, E]), ALU.is_equal))
                    if c == 0:
                        link(v.scalar_tensor_tensor(out=te(masked), in0=te(oh[0]), scalar=NEG, in1=cur,
                                                    op0=ALU.mult, op1=ALU.add))
                        cur = te(masked)
                v.tensor_tensor(hot, oh[0], oh[1], ALU.add).then_inc(sem("hot"), 1)
                link(v.tensor_tensor(te(ex), lg[:, :, :], m1[:, :, None].to_broadcast([P, NT, E]), ALU.subtract))
                v.tensor_tensor(m2, m2, m1, ALU.subtract).then_inc(sem("route_shift"), 1)
                dve.wait_ge(sem("counts_done"), layer + 1)
                link(v.tensor_copy(et(tot), bank[7][:, 128:128 + NT * E].rearrange("p (t e) -> p e t", e=E)))
                incl = cand
                link(v.tensor_tensor_scan(incl, ones[:, 0:NT * E], tot, 0.0, ALU.mult, ALU.add))
                ends = et(incl)[:, :, NT - 1]
                start, cnt, tiles, tend, base = (counts[:, 8 * k:8 * k + 8] for k in range(5))
                link(v.memset(start[:, 0:1], 0.0))
                link(v.tensor_copy(start[:, 1:E], ends[:, 0:E - 1]))
                link(v.tensor_tensor(cnt, ends, start, ALU.subtract))
                ci = counts[:, 40:48].bitcast(I32)
                link(v.tensor_scalar(ci, cnt, float(SW - 1), None, ALU.add))
                link(v.tensor_scalar(ci, ci, SW.bit_length() - 1, None, ALU.logical_shift_right))
                link(v.tensor_copy(tiles, ci))
                link(v.tensor_tensor_scan(tend, ones[:, 0:E], tiles, 0.0, ALU.mult, ALU.add))
                link(v.tensor_tensor(base, tend, tiles, ALU.subtract))
                link(v.scalar_tensor_tensor(out=base, in0=base, scalar=float(SW), in1=start, op0=ALU.mult,
                                            op1=ALU.subtract))
                link(v.tensor_tensor(masked, incl, tot, ALU.subtract))
                link(v.tensor_tensor(et(masked), et(masked), base[:, :, None].to_broadcast([P, E, NT]), ALU.add))
                pos = cand
                link(v.tensor_tensor(te(pos), bank[7][:, 256:256 + NT * E].rearrange("p (t e) -> p t e", e=E),
                                     masked.rearrange("p (e t) -> p t e", e=E), ALU.add))
                both = r[:, P:3 * P].rearrange("p (c n) -> p c n", c=2)
                link(v.tensor_tensor(both, both, pos[:, None, :].to_broadcast([P, 2, NT * E]), ALU.mult))
                link(v.tensor_reduce(hot[:, 0:2 * NT].rearrange("p (c t) -> p c t", c=2),
                                     both.rearrange("p c (t e) -> p c t e", e=E), axis=AX.X, op=ALU.add))
                link(v.tensor_copy(slots[:, :, :], hot[:, 0:2 * NT].rearrange("p (c t) -> p t c", c=2)))
                rr, qq = (r[:, k:k + 2 * NT] for k in (1280, 1312))
                sv = slots[:, :, :].rearrange("p t c -> p (t c)")
                link(v.tensor_scalar(hot[:, 0:2 * NT].bitcast(U32), sv, P - 1, None, ALU.bitwise_and))
                link(v.tensor_scalar(tot[:, 0:2 * NT].bitcast(U32), sv, P.bit_length() - 1, None, ALU.logical_shift_right))
                link(v.tensor_copy(rr, hot[:, 0:2 * NT].bitcast(U32)))
                link(v.tensor_copy(qq, tot[:, 0:2 * NT].bitcast(U32)))
                at_q = r[:, 128:128 + NT * NQ].bitcast(F16).rearrange("p (n q) -> p n q", q=NQ)
                v.tensor_tensor(at_q, iota_r[:, None, 0:NQ].to_broadcast([P, 2 * NT, NQ]),
                                qq[:, :, None].to_broadcast([P, 2 * NT, NQ]), ALU.is_equal).then_inc(sem("tiles_hot"), 1)
                for half in range(2):
                    n = slice(half * NT, (half + 1) * NT)
                    v.tensor_tensor(onehots[layer][:, n, :], iota_r[:, None, :].to_broadcast([P, NT, P]),
                                    rr[:, n, None].to_broadcast([P, NT, P]), ALU.is_equal).then_inc(sem("rows_hot"), 1)
                ge_e = r[:, 1376:1376 + NSLOT * (E - 1)].rearrange("p (s e) -> p s e", e=E - 1)
                link(v.tensor_tensor(ge_e, iota_r[:, 0:NSLOT, None].to_broadcast([P, NSLOT, E - 1]),
                                     tend[:, None, 0:E - 1].to_broadcast([P, NSLOT, E - 1]), ALU.is_ge))
                es = r[:, 1540:1540 + NSLOT]
                link(v.tensor_reduce(es, ge_e, axis=AX.X, op=ALU.add))
                link(v.tensor_copy(expert[:, 0, :], es))
                link(v.tensor_scalar(expert[:, 1, :], es, float(2 * DC * moes[layer].H), None, ALU.mult))
                dve.wait_ge(sem("tokens_done"), layer + 1)
                sign, which = (r[:, k:k + NQ] for k in (1344, 1408))
                link(v.tensor_scalar(sign, bank[6][:, 0:NQ], 0.0, -2.0, ALU.is_lt, ALU.mult))
                link(v.scalar_tensor_tensor(out=which, in0=sign, scalar=1.0, in1=bank[6][:, 0:NQ], op0=ALU.add,
                                            op1=ALU.mult))
                v.tensor_scalar(index[:, :], which, -1.0, 0.0, ALU.add, ALU.max).then_inc(sem("routed"), 1)
                if layer == 1:
                    dve.wait_ge(sem("behind_ready"), 1)
                    link(v.scalar_tensor_tensor(out=sign, in0=sign, scalar=-0.5, in1=which, op0=ALU.mult, op1=ALU.add))
                    link(v.tensor_tensor(sign, sign, which, ALU.add))
                    link(v.scalar_tensor_tensor(out=which, in0=which, scalar=0.0, in1=behind, op0=ALU.is_equal,
                                                op1=ALU.mult))
                    v.tensor_tensor(back, sign, which, ALU.add).then_inc(sem("back_ready"), 1)
                dve.wait_ge(sem("route_exp"), 2 * layer + 2)
                link(v.tensor_reduce(best, te(ex), axis=AX.X, op=ALU.add))
                link(v.reciprocal(gates[:, 0, :], best))
                v.tensor_tensor(gates[:, 1, :], gates[:, 0, :], m2, ALU.mult).then_inc(sem("gates_ready"), 1)
                dve.wait_ge(sem("gates_ready"), layer + 1)

            def slot_cols(layer, j):
                m = moes[layer]
                dve.wait_ge(sem(f"slot_tr{layer}"), j + 1)
                if j >= 2:
                    dve.wait_ge(sem(f"slot_h{layer}"), m.PARTS * (j - 1))
                v.tensor_copy(m.xT[:, j % 2], slot_columns(j)).then_inc(
                    sem(f"slot_cols{layer}"), 1)

            def slot_bias(layer, j, a):
                m = moes[layer]
                u = m.PARTS * j + a
                if a == 0:
                    expert_of[j] = dve.value_load(expert[0:1, 0, j:j + 1], min_val=0, max_val=E - 1)
                dve.wait_ge(sem(f"slot_h{layer}"), u + 1)
                if u >= 2:
                    dve.wait_ge(sem(f"h_lo{layer}"), u - 1)
                bias = m.b[:, bass.ds(expert_of[j] * m.HC + a * m.HH, m.HH)]
                v.scalar_tensor_tensor(out=m.g[:, u % 2], in0=hidden(m, u), scalar=1.0 / WS,
                                       in1=bias[:, :, None].to_broadcast([P, m.HH, SW]),
                                       op0=ALU.mult, op1=ALU.add).then_inc(sem(f"h_biased{layer}"), 1)

            def slot_lo(layer, j, a):
                m = moes[layer]
                u = m.PARTS * j + a
                dve.wait_ge(sem(f"h_hi{layer}"), u + 1)
                c = slice(a * m.HH, (a + 1) * m.HH)
                v.tensor_tensor(m.hl[:, j % 2, c, :], m.g[:, u % 2], m.hh[:, j % 2, c, :], ALU.subtract).then_inc(
                    sem(f"h_lo{layer}"), 1)

            def slot_out(layer, j):
                m = moes[layer]
                dve.wait_ge(sem(f"slot_y{layer}"), j + 1)
                if j >= 2:
                    dve.wait_ge(sem(f"y_kept{layer}_{j % 2}"), 16 * (A if layer else 1) * (j // 2))
                b2 = m.b2[:, bass.ds(expert_of[j] * D, D)]
                v.scalar_tensor_tensor(out=m.y[:, j % 2], in0=slot_banks(j), scalar=1.0 / WS,
                                       in1=b2[:, None, :].to_broadcast([P, A, D]),
                                       op0=ALU.mult, op1=ALU.add).then_inc(sem(f"y_ready{layer}"), 1)

            expert_of = {}

            def slots_of(layer):
                dve.wait_ge(sem("b_in0_loaded" if layer == 0 else "b1_loaded"), 16)
                dve.wait_ge(sem(f"b2_loaded{layer}"), 16)
                m = moes[layer]
                for s in range(NSLOT + m.LAG + 2):
                    if 0 <= s - m.LAG - 2 < NSLOT:
                        slot_out(layer, s - m.LAG - 2)
                    if s < NSLOT:
                        slot_cols(layer, s)
                    for a in range(m.PARTS):
                        if 0 <= s - 1 < NSLOT:
                            slot_bias(layer, s - 1, a)
                    for a in range(m.PARTS):
                        if 0 <= s - m.LAG < NSLOT:
                            slot_lo(layer, s - m.LAG, a)
                    k = PRE + A_CH + s
                    if layer == 0 and k < NCH - LATE and k % 2:
                        split_lo(k)

            def combine(i):
                for c in range(2):
                    if c:
                        dve.wait_ge(sem("y_used1"), 2 * i + 1)
                    v.scalar_tensor_tensor(out=X[:, i, :], in0=yg1[:, i, c, :], scalar=gates[:, c, i:i + 1],
                                           in1=X[:, i, :], op0=ALU.mult, op1=ALU.add).then_inc(sem("y_used1"), 1)

            def add_linear(i):
                dve.wait_ge(ln2.full, i + 1)
                dve.wait_ge(sem("linear_done"), i + 1)
                v.scalar_tensor_tensor(out=X[:, i, :], in0=c_ps[i % 2], scalar=1.0 / WS, in1=X[:, i, :],
                                       op0=ALU.mult, op1=ALU.add).then_inc(sem("linear_added"), 1)

            route(0)
            slots_of(0)
            def mark(ins):
                chain[0] += 1
                ins.then_inc(sem("dve_chain"), 1)
                return chain[0]

            for s in range(NT + 9):
                a, b = s - 2, s - 5
                if 0 <= a < NT:
                    dve.wait_ge(sem(f"y_gathered0_{a % NG_BUF}"), 32 * (a // NG_BUF + 1))
                    v.scalar_tensor_tensor(out=X[:, a, :], in0=yg[:, a % NG_BUF, 0, :], scalar=gates[:, 0, a:a + 1],
                                           in1=X[:, a, :], op0=ALU.mult, op1=ALU.add).then_inc(sem("y_used0"), 1)
                if 0 <= b < NT:
                    add_linear(b)
                if 0 <= a < NT:
                    dve.wait_ge(sem("y_used0"), 2 * a + 1)
                    v.scalar_tensor_tensor(out=X[:, a, :], in0=yg[:, a % NG_BUF, 1, :], scalar=gates[:, 1, a:a + 1],
                                           in1=X[:, a, :], op0=ALU.mult, op1=ALU.add).then_inc(sem("y_used0"), 1)
                if 0 <= b < NT:
                    dve.wait_ge(sem("linear_added"), b + 1)
                    stat_b = mark(v.bn_stats(st6[:, ln3.n, :], X[:, b, :]))
                if 0 <= a < NT:
                    dve.wait_ge(sem("y_used0"), 2 * a + 2)
                    stat_a = mark(v.bn_stats(st6[:, ln2.n, :], X[:, a, :]))
                if 0 <= b < NT:
                    if b >= 2:
                        dve.wait_ge(ln3.full, b - 1)
                    dve.wait_ge(sem("dve_chain"), stat_b)
                    stat_b = mark(v.bn_aggr(mv[:, ln3.n, b % 2, :], st6[:, ln3.n, :]))
                if 0 <= a < NT:
                    if a >= 2:
                        dve.wait_ge(ln2.full, a - 1)
                    dve.wait_ge(sem("dve_chain"), stat_a)
                    stat_a = mark(v.bn_aggr(mv[:, ln2.n, a % 2, :], st6[:, ln2.n, :]))
                if 0 <= b < NT:
                    dve.wait_ge(sem("dve_chain"), stat_b)
                    var = mv[:, ln3.n, b % 2, 1:2]
                    v.tensor_scalar_add(var, var, LN_EPS).then_inc(ln3.var, 1)
                if 0 <= a < NT:
                    dve.wait_ge(sem("dve_chain"), stat_a)
                    var = mv[:, ln2.n, a % 2, 1:2]
                    v.tensor_scalar_add(var, var, LN_EPS).then_inc(ln2.var, 1)
                if 0 <= s - 3 < NT:
                    norm_lo(ln2, s - 3)
                if 0 <= s - 6 < NT:
                    norm_lo(ln3, s - 6)
                if 0 <= s - 9 < NT:
                    logits(1, s - 9)
            route(1)
            slots_of(1)
            for n, group in enumerate(last_groups):
                dve.wait_ge(sem(f"y_gathered1_{n}"), 16)
                for i in group:
                    combine(i)

        @block.tensor
        def _(pe):
            t = nc.tensor

            def mm(o, a, b, start, stop):
                return t.matmul(o, a, b, start=start, stop=stop)

            def three(o, ah, al, bh, bl, first, last):
                mm(o, ah, bh, first, False)
                mm(o, ah, bl, False, False)
                return mm(o, al, bh, False, last)

            pe.wait_ge(sem("ctx_loaded"), 16)
            pe.wait_ge(sem("wk_loaded"), 16)
            pe.wait_ge(sem("heads_ready"), 1)
            for s in range(NP + 1):
                if s < NP:
                    if s >= 2:
                        pe.wait_ge(sem("k_copied"), s - 1)
                    for dc in range(DC):
                        last = mm(bank[3 + s % 2][:, 0:NB * L], wk_s[:, dc, s * P:(s + 1) * P], ctx_s[:, dc, :],
                                  dc == 0, dc == DC - 1)
                    last.then_inc(sem("k_done"), 1)
                if s >= 1:
                    pe.wait_ge(sem("k_sq"), s)
                    if s >= 2:
                        pe.wait_ge(sem("k_ms"), s - 1)
                    mm(bank[5][:, 0:NB * L], heads2, ksq[:, s - 1, :], True, True).then_inc(sem("k_ssq"), 1)
            pe.wait_ge(sem("wv_loaded"), 16)
            for j in range(NP):
                if j >= 2:
                    pe.wait_ge(sem("vt_copied"), 2 * (j - 1))
                for dc in range(DC):
                    last = mm(bank[1 + j % 2][:, 0:NB * L], wv_s[:, dc, j * P:(j + 1) * P], ctx_s[:, dc, :],
                              dc == 0, dc == DC - 1)
                last.then_inc(sem("vt_done"), 1)
            pe.wait_ge(sem("mean_ready"), 1)
            pe.wait_ge(sem("cw2_loaded"), 16)
            pe.wait_ge(sem("k_copied"), NP)
            for b in range(NB):
                for dc in range(DC):
                    last = mm(bank[3 + b][:, 0:D], cmb[:, dc, b, :], cw2[:, dc, :], dc == 0, dc == DC - 1)
                last.then_inc(sem("mean_done"), 1)
            pe.wait_ge(sem("wo_loaded"), 16)
            pe.wait_ge(sem("vt_copied"), NH)
            pe.wait_ge(sem("consts_ready"), 1)

            def v_wo(n):
                b, c = divmod(n, KC)
                if n >= 2:
                    pe.wait_ge(sem("vw_hi"), n - 1)
                js = [j for j in range(NP) if -P < P * c - PW * j < PW]
                for j in js:
                    o = P + P * c - PW * j
                    last = mm(bank[6 + n % 2][:, 0:D], zt[:, j, b, o:o + P], wo_s[:, j, :],
                              j == js[0], j == js[-1] and c < KC - 1)
                if c == KC - 1:
                    pe.wait_ge(sem("bo_loaded"), 16)
                    last = mm(bank[6 + n % 2][:, 0:D], ident_f, bo_row, False, True)
                last.then_inc(sem("vw_done"), 1)

            def transposed(o, i):
                pe.wait_ge(o.lo, i + 1)
                if i >= 1:
                    pe.wait_ge(o.cols, i)
                for c in range(2 * DC):
                    last = t.transpose(o.ps[:, c, :], o.rows[:, i % 2, c * P:(c + 1) * P], ident_h[:, :])
                last.then_inc(o.tr, 1)

            def q_proj(i):
                pe.wait_ge(ln0.cols, i + 1)
                if i == 0:
                    pe.wait_ge(sem("chunk_lo0"), 1)
                    pe.wait_ge(sem("chunk_lo1"), 1)
                if i >= 1:
                    pe.wait_ge(sem("q_lo"), i)
                xT = ln0.xT[:, i % 2]
                for j in range(NP):
                    w = slice(j * P, (j + 1) * P)
                    for dc in range(DC):
                        last = three(q_ps[:, j, :], wq_h[:, dc, w], wq_l[:, dc, w], xT[:, dc, :], xT[:, DC + dc, :],
                                     dc == 0, dc == DC - 1)
                last.then_inc(sem("q_done"), 1)

            def scores(i):
                pe.wait_ge(sem("q_lo"), i + 1)
                if i == 0:
                    pe.wait_ge(sem("kb_ready"), 2)
                    pe.wait_ge(sem("ctx_bias_ready"), NB)
                if i >= 1:
                    pe.wait_ge(sem("scores_shifted"), i)
                if i >= 7:
                    pe.wait_ge(sem("logits_read0"), i - 6)
                b = i // (NT // NB)
                for j in range(NP):
                    kh = kbh[:, j, b].rearrange("p a k -> p (a k)")
                    kl = kbl[:, j, b].rearrange("p a k -> p (a k)")
                    last = three(bank[3 + j // 3][:, PW * (j % 3):PW * (j % 3 + 1)], qh[:, j, :], ql[:, j, :], kh, kl,
                                 True, True)
                    if j == NP - 1:
                        last.then_inc(sem("scores_done"), 1)
                    last = mm(SSQ[:, 2 * j:2 * j + 2], qsq[:, j, :], heads2[:, 0:DH + 1:DH], True, True)
                last.then_inc(sem("ssq_done"), 1)

            def weights_t(i, n):
                if n == 0:
                    pe.wait_ge(sem("weights_ready"), i + 1)
                if i == 0 and n == 0:
                    pe.wait_ge(sem("vw_ready"), NB * KC)
                if NG * i + n >= 2:
                    pe.wait_ge(sem("pt_lo"), NG * i + n - 1)
                a, b = groups[n]
                for c in range(a, b):
                    last = t.transpose(bank[6 + (NG * i + n) % 2][:, (c - a) * P:(c - a + 1) * P],
                                       pb[i % 3][:, c * P:(c + 1) * P], ident_f)
                last.then_inc(sem("weights_tr"), 1)

            def attn(i):
                pe.wait_ge(sem("pt_lo"), NG * (i + 1))
                pe.wait_ge(ln0.cols, min(NT, i + 5))
                if i >= 2:
                    pe.wait_ge(ln1.cols, i - 1)
                if i >= 1:
                    pe.wait_ge(sem("attn_added"), i)
                b = i // (NT // NB)
                for c in range(KC):
                    last = three(o_ps, pth[:, c, :], ptl[:, c, :], vw[:, b, c, 0, :], vw[:, b, c, 1, :],
                                 c == 0, c == KC - 1)
                last.then_inc(sem("attn_done"), 1)

            def logits(layer, o, i):
                pe.wait_ge(o.cols, i + 1)
                if i == 0:
                    pe.wait_ge(sem("chunk_lo0"), PRE // 2)
                    pe.wait_ge(sem("chunk_lo1"), PRE // 2)
                if i >= 1 + layer:
                    pe.wait_ge(sem(f"logits_read{layer}"), i - layer)
                if layer == 0:
                    pe.wait_ge(sem("scores_shifted"), min(NT, i + 6))
                for dc in range(DC):
                    last = three((LOG1 if layer else LOG)[i % 2], o.xT[:, i % 2, dc, :], o.xT[:, i % 2, DC + dc, :], rws[:, 0, layer, dc, :],
                                 rws[:, 1, layer, dc, :], dc == 0, dc == DC - 1)
                last.then_inc(sem(f"logits_done{layer}"), 1)

            for n in range(VW_FIRST):
                v_wo(n)
            for s in range(NT + 9):
                if 0 <= s - 5 < NT:
                    weights_t(s - 5, 0)
                    weights_t(s - 5, 1)
                if 0 <= s - 1 < NT:
                    if s - 1 >= 5:
                        pe.wait_ge(sem("attn_added"), s - 5)
                    if s - 1 >= 7:
                        pe.wait_ge(ln1.cols, s - 7)
                    transposed(ln0, s - 1)
                if 0 <= s - 7 < NT:
                    pe.wait_ge(sem("attn_added"), min(NT, s - 5))
                    if s - 1 >= NT:
                        pe.wait_ge(ln0.cols, NT)
                    transposed(ln1, s - 7)
                if 0 <= s - 2 < NT:
                    scores(s - 2)
                if 0 <= s - 5 < NT:
                    weights_t(s - 5, 2)
                if 0 <= s - 8 < NT:
                    logits(0, ln1, s - 8)
                for n in range(VW_FIRST + VW_STEP * s, min(NB * KC, VW_FIRST + VW_STEP * (s + 1))):
                    v_wo(n)
                if 0 <= s - 1 < NT:
                    q_proj(s - 1)
                if 0 <= s - 5 < NT:
                    attn(s - 5)

            def route(layer):
                r = routes[layer]
                hot = r[:, 5 * P:5 * P + NT * E]
                pe.wait_ge(sem("hot"), layer + 1)
                if layer == 0:
                    pe.wait_ge(sem("pt_lo"), NG * NT)
                mm(bank[7][:, 128:128 + NT * E], ones[:, :], hot, True, True)
                mm(bank[7][:, 256:256 + NT * E], before[:, :], hot, True, True).then_inc(sem("counts_done"), 1)
                at_q = r[:, 128:128 + NT * NQ].bitcast(F16).rearrange("p (n q) -> p n q", q=NQ)
                pe.wait_ge(sem("places"), layer + 1)
                for n in range(2 * NT):
                    if n % NT == 0:
                        pe.wait_ge(sem("rows_hot"), 2 * layer + n // NT + 1)
                    last = mm(bank[6][:, 0:NQ], onehots[layer][:, n, :], at_q[:, n, :], n == 0, n == 2 * NT - 1)
                last.then_inc(sem("tokens_done"), 1)

            weights_at = {}

            def slot_tr(layer, j):
                m = moes[layer]
                pe.wait_ge(sem(f"rows_gathered{layer}_{j % RING}"), 16 * A * (j // RING + 1))
                if j >= 2:
                    pe.wait_ge(sem(f"slot_cols{layer}"), j - 1)
                cols = slot_columns(j)
                for a in range(A):
                    for c in range(2 * DC):
                        last = t.transpose(cols[:, c, a * P:(a + 1) * P], m.rows[:, j % RING, a, c * P:(c + 1) * P],
                                           ident_h[:, :])
                last.then_inc(sem(f"slot_tr{layer}"), 1)

            def slot_up(layer, j):
                m = moes[layer]
                per = DC * m.H
                e = weights_at[j]
                pe.wait_ge(sem(f"slot_cols{layer}"), j + 1)
                xT = m.xT[:, j % 2]
                for a in range(m.PARTS):
                    u = m.PARTS * j + a
                    if u >= 2:
                        pe.wait_ge(sem(f"h_biased{layer}"), u - 1)
                    ps = hidden(m, u)
                    for hc in range(m.HH):
                        for dc in range(DC):
                            o = dc * m.H + (a * m.HH + hc) * P
                            last = three(ps[:, hc, :], m.wa[:, bass.ds(e + o, P)], m.wa[:, bass.ds(e + (per + o), P)],
                                         xT[:, dc, :], xT[:, DC + dc, :], dc == 0, dc == DC - 1)
                    last.then_inc(sem(f"slot_h{layer}"), 1)

            def slot_down(layer, j):
                m = moes[layer]
                per = DC * m.H
                e = weights_at[j]
                pe.wait_ge(sem(f"h_lo{layer}"), m.PARTS * (j + 1))
                if j >= 3 - A:
                    pe.wait_ge(sem(f"y_ready{layer}"), j - 2 + A)
                for hc in range(m.HC):
                    wh = m.wb[:, bass.ds(e + hc * D, D)]
                    wl = m.wb[:, bass.ds(e + (per + hc * D), D)]
                    for a in range(A):
                        c = slice(a * P, (a + 1) * P)
                        last = three(slot_banks(j)[:, a, :], m.hh[:, j % 2, hc, c], m.hl[:, j % 2, hc, c], wh, wl,
                                     hc == 0, hc == m.HC - 1)
                last.then_inc(sem(f"slot_y{layer}"), 1)

            def slots_of(layer):
                m = moes[layer]
                pe.wait_ge(sem("routed"), layer + 1)
                n = B_CH if layer == 0 else NCH
                pe.wait_ge(sem("chunk_lo0"), n // 2)
                pe.wait_ge(sem("chunk_lo1"), n // 2)
                for s in range(NSLOT + m.LAG + 1):
                    if s < NSLOT:
                        weights_at[s] = pe.value_load(expert[0:1, 1, s:s + 1], min_val=0, max_val=(E - 1) * 2 * DC * m.H)
                        slot_tr(layer, s)
                    if 0 <= s - 1 < NSLOT:
                        slot_up(layer, s - 1)
                    if 0 <= s - m.LAG - 1 < NSLOT:
                        slot_down(layer, s - m.LAG - 1)

            def linear(i):
                pe.wait_ge(ln2.cols, i + 1)
                if i >= 2:
                    pe.wait_ge(sem("linear_added"), i - 1)
                xT = ln2.xT[:, i % 2]
                for dc in range(DC):
                    three(c_ps[i % 2], xT[:, dc, :], xT[:, DC + dc, :], wc[:, 0, dc, :], wc[:, 1, dc, :], dc == 0, False)
                for n in range(2):
                    last = mm(c_ps[i % 2], ident_h[:, :], ctx_bias[:, i // (NT // NB), n, :], False, n == 1)
                last.then_inc(sem("linear_done"), 1)

            route(0)
            slots_of(0)
            for s in range(NT + 8):
                if 0 <= s - 3 < NT:
                    transposed(ln2, s - 3)
                if 0 <= s - 6 < NT:
                    transposed(ln3, s - 6)
                if 0 <= s - 3 < NT:
                    linear(s - 3)
                if 0 <= s - 7 < NT:
                    logits(1, ln3, s - 7)
            route(1)
            slots_of(1)


def kernel(**inputs):
    import numpy as np
    import concourse.bacc as bacc
    from concourse.bass_utils import run_bass_kernel_spmd

    a = {k: np.asarray(v) for k, v in inputs.items()}
    D = a["x"].shape[-1]
    P_ = 128
    E = a["L0_ffn_b_in"].shape[0]

    def per_part(b):
        return b.reshape(E, -1, P_).transpose(2, 0, 1).reshape(P_, -1)

    arrays = {
        "x": a["x"].reshape(-1, D),
        "ctx_t": a["ctx_1024"].reshape(-1, D).T,
        "wq": a["L0_xattn_Wq"].reshape(D, -1),
        "wk": a["L0_xattn_Wk"].reshape(D, -1),
        "wv": a["L0_xattn_Wv"].reshape(D, -1),
        "scale_q": a["L0_xattn_scale_q"],
        "scale_k": a["L0_xattn_scale_k"],
        "wo": a["L0_xattn_Wo"].reshape(-1, D),
        "bo": a["L0_xattn_bo"],
        "rw0": a["L0_ffn_router_w"],
        "w_in0": a["L0_ffn_w_in"],
        "b_in0": per_part(a["L0_ffn_b_in"]),
        "w_out0": a["L0_ffn_w_out"],
        "b_out0": a["L0_ffn_b_out"].reshape(-1),
        "cw1_t": a["L1_xattn_W"][:, :D].T,
        "cw2_t": a["L1_xattn_W"][:, D:].T,
        "cb": a["L1_xattn_b"],
        "rw1_t": a["L1_ffn_router_w"].T,
        "rb1": a["L1_ffn_router_b"],
        "w1_t": a["L1_ffn_w1"].transpose(0, 2, 1),
        "b1": per_part(a["L1_ffn_b1"]),
        "w2_t": a["L1_ffn_w2"].transpose(0, 2, 1),
        "b2": a["L1_ffn_b2"].reshape(-1),
    }
    arrays = {k: np.ascontiguousarray(v) for k, v in arrays.items()}
    nc = bacc.Bacc("TRN2", target_bir_lowering=False, num_devices=1)
    args = [nc.dram_tensor(k, v.shape, mybir.dt.from_np(v.dtype), kind="ExternalInput").ap() for k, v in arrays.items()]
    out = nc.dram_tensor("out", arrays["x"].shape, F32, kind="ExternalOutput").ap()
    build(nc, *args, out)
    r = run_bass_kernel_spmd(nc, [arrays], core_ids=[0])
    return r.results[0]["out"].reshape(a["x"].shape)
```
